# Optimizing a Trainium2 kernel written in Bass

```python
import numpy as np
import jax
import jax.numpy as jnp

def _softmax(x, axis=-1):
    return jax.nn.softmax(x, axis=axis)

def _gelu(x):
    return jax.nn.gelu(x, approximate=True)

def _silu(x):
    return jax.nn.silu(x)

def _sigmoid(x):
    return jax.nn.sigmoid(x)

def _layernorm(x, axis=-1, eps=1e-05):
    m = jnp.mean(x, axis=axis, keepdims=True)
    v = jnp.var(x, axis=axis, keepdims=True)
    return (x - m) / jnp.sqrt(v + eps)

def _scatter_add(tgt, idx, src, axis=0):
    return tgt.at[idx].add(src)

def _segment_sum(src, seg, n):
    return jax.ops.segment_sum(src, seg, n)
kernel_name = 'mk_gnn_ffn_d1_gnn_r8_a689a7'

def setup_inputs(seed: int=0):
    np.random.seed(seed)
    _w = jnp.asarray

    def _rec_inputs():
        import jax
        import jax.numpy as jnp
        _gk = jax.random.key(seed)
        x = -8.776e-05 + 1 * jax.random.normal(jax.random.fold_in(_gk, 1), (6250, 256), jnp.float32)
        src = jax.random.randint(jax.random.fold_in(_gk, 2), (100000,), 0, 6250, jnp.int32)
        dst = jnp.minimum((6250 * jax.random.uniform(jax.random.fold_in(_gk, 3), (100000,)) ** 2.0).astype(jnp.int32), 49999)
        _o = jnp.argsort(dst, stable=True)
        src = src[_o]
        dst = dst[_o]
        edge_attr_64 = 1.36993e-05 + 0.999972 * jax.random.normal(jax.random.fold_in(_gk, 11), (100000, 64), jnp.float32)
        edge_weight = jax.random.uniform(jax.random.fold_in(_gk, 13), (100000,), jnp.float32, 0.0, 0.999998)
        return (x, src, dst, edge_attr_64, edge_weight)
    x, src, dst, edge_attr_64, edge_weight = _rec_inputs()

    def _L0_gnn_setup():
        import jax, jax.numpy as jnp
        import numpy as np
        N = 2500
        E = 40000
        D = 256
        H = 8
        DH = D // H
        ED = 64
        FF = 4 * D
        EPS = 1e-05

        def _layernorm(x, g, b):
            m = jnp.mean(x, axis=-1, keepdims=True)
            v = jnp.var(x, axis=-1, keepdims=True)
            return (x - m) * jax.lax.rsqrt(v + EPS) * g + b

        def _edge_attention(xn, edge_index, ef, ew, Wq, bq, Wk, bk, Wv, bv, We, be, Wo, bo):
            n = xn.shape[0]
            scale = DH ** (-0.5)
            q = (xn @ Wq + bq).reshape(n, H, DH)
            k = (xn @ Wk + bk).reshape(n, H, DH)
            v = (xn @ Wv + bv).reshape(n, H, DH)
            src, dst = (edge_index[0], edge_index[1])
            ep = ef @ We + be
            scores = jnp.einsum('ehd,ehd->eh', q[dst], k[src] + ep[:, None, :]) * scale
            scores = scores * ew[:, None]
            m = jax.ops.segment_max(scores, dst, num_segments=n)
            m = jnp.where(jnp.isfinite(m), m, 0.0)
            ex = jnp.exp(scores - m[dst])
            s = jax.ops.segment_sum(ex, dst, num_segments=n)
            attn = ex / s[dst]
            out = jax.ops.segment_sum(attn[:, :, None] * v[src], dst, num_segments=n)
            out = out.reshape(n, D) @ Wo + bo
            return out
        key = jax.random.key(seed)
        ks = jax.random.split(key, 32)

        def lin_w(k, i, o):
            return (jax.random.normal(k, (i, o), jnp.float32) / np.sqrt(i)).astype(jnp.float32)
        return {'x': jax.random.normal(ks[0], (N, D), jnp.float32), 'edge_features': jax.random.normal(ks[1], (E, ED), jnp.float32), 'edge_weights': jax.random.uniform(ks[2], (E,), jnp.float32), 'edge_index': jax.random.randint(ks[3], (2, E), 0, N, dtype=jnp.int32), 'Wq': lin_w(ks[4], D, D), 'bq': jnp.zeros((D,), jnp.float32), 'Wk': lin_w(ks[5], D, D), 'bk': jnp.zeros((D,), jnp.float32), 'Wv': lin_w(ks[6], D, D), 'bv': jnp.zeros((D,), jnp.float32), 'We': lin_w(ks[7], ED, DH), 'be': jnp.zeros((DH,), jnp.float32), 'Wo': lin_w(ks[8], D, D), 'bo': jnp.zeros((D,), jnp.float32), 'ln1_g': jnp.ones((D,), jnp.float32), 'ln1_b': jnp.zeros((D,), jnp.float32), 'ln2_g': jnp.ones((D,), jnp.float32), 'ln2_b': jnp.zeros((D,), jnp.float32), 'W1': lin_w(ks[9], D, FF), 'b1': jnp.zeros((FF,), jnp.float32), 'W2': lin_w(ks[10], FF, D), 'b2': jnp.zeros((D,), jnp.float32), 'alpha': jnp.ones((1,), jnp.float32), 'beta': jnp.ones((1,), jnp.float32)}
    _L0_gnn_all = _L0_gnn_setup()
    _L0_gnn_in = {k: v for k, v in _L0_gnn_all.items() if k in ('Wq', 'bq', 'Wk', 'bk', 'Wv', 'bv', 'We', 'be', 'Wo', 'bo', 'ln1_g', 'ln1_b', 'ln2_g', 'ln2_b', 'W1', 'b1', 'W2', 'b2', 'alpha', 'beta')}
    del _L0_gnn_all

    def _L0_ffn_setup():
        import jax, jax.numpy as jnp
        import numpy as np
        B, S, D, E, H, K = (4, 512, 256, 8, 512, 2)
        key = jax.random.key(seed)
        ks = jax.random.split(key, 6)
        x = jax.random.normal(ks[0], (B, S, D), jnp.float32)
        Wg = jax.random.normal(ks[1], (D, E), jnp.float32) * 0.02
        bg = jnp.zeros((E,), jnp.float32)
        W1 = jax.random.normal(ks[2], (E, D, H), jnp.float32) * 0.02
        b1 = jnp.zeros((E, H), jnp.float32)
        W2 = jax.random.normal(ks[3], (E, H, D), jnp.float32) * 0.02
        b2 = jnp.zeros((E, D), jnp.float32)
        return {'x': x, 'Wg': Wg, 'bg': bg, 'W1': W1, 'b1': b1, 'W2': W2, 'b2': b2}
    _L0_ffn_all = _L0_ffn_setup()
    _L0_ffn_in = {k: v for k, v in _L0_ffn_all.items() if k in ('Wg', 'bg', 'W1', 'b1', 'W2', 'b2')}
    del _L0_ffn_all
    return {'x': x, 'src': src, 'dst': dst, 'edge_attr_64': edge_attr_64, 'edge_weight': edge_weight, 'L0_gnn_Wq': _L0_gnn_in['Wq'], 'L0_gnn_bq': _L0_gnn_in['bq'], 'L0_gnn_Wk': _L0_gnn_in['Wk'], 'L0_gnn_bk': _L0_gnn_in['bk'], 'L0_gnn_Wv': _L0_gnn_in['Wv'], 'L0_gnn_bv': _L0_gnn_in['bv'], 'L0_gnn_We': _L0_gnn_in['We'], 'L0_gnn_be': _L0_gnn_in['be'], 'L0_gnn_Wo': _L0_gnn_in['Wo'], 'L0_gnn_bo': _L0_gnn_in['bo'], 'L0_gnn_ln1_g': _L0_gnn_in['ln1_g'], 'L0_gnn_ln1_b': _L0_gnn_in['ln1_b'], 'L0_gnn_ln2_g': _L0_gnn_in['ln2_g'], 'L0_gnn_ln2_b': _L0_gnn_in['ln2_b'], 'L0_gnn_W1': _L0_gnn_in['W1'], 'L0_gnn_b1': _L0_gnn_in['b1'], 'L0_gnn_W2': _L0_gnn_in['W2'], 'L0_gnn_b2': _L0_gnn_in['b2'], 'L0_gnn_alpha': _L0_gnn_in['alpha'], 'L0_gnn_beta': _L0_gnn_in['beta'], 'L0_ffn_Wg': _L0_ffn_in['Wg'], 'L0_ffn_bg': _L0_ffn_in['bg'], 'L0_ffn_W1': _L0_ffn_in['W1'], 'L0_ffn_b1': _L0_ffn_in['b1'], 'L0_ffn_W2': _L0_ffn_in['W2'], 'L0_ffn_b2': _L0_ffn_in['b2']}

def reference(x, src, dst, edge_attr_64, edge_weight, L0_gnn_Wq, L0_gnn_bq, L0_gnn_Wk, L0_gnn_bk, L0_gnn_Wv, L0_gnn_bv, L0_gnn_We, L0_gnn_be, L0_gnn_Wo, L0_gnn_bo, L0_gnn_ln1_g, L0_gnn_ln1_b, L0_gnn_ln2_g, L0_gnn_ln2_b, L0_gnn_W1, L0_gnn_b1, L0_gnn_W2, L0_gnn_b2, L0_gnn_alpha, L0_gnn_beta, L0_ffn_Wg, L0_ffn_bg, L0_ffn_W1, L0_ffn_b1, L0_ffn_W2, L0_ffn_b2):
    import jax
    import jax.numpy as jnp

    def _L0_gnn_ref(x, edge_features, edge_weights, edge_index, Wq, bq, Wk, bk, Wv, bv, We, be, Wo, bo, ln1_g, ln1_b, ln2_g, ln2_b, W1, b1, W2, b2, alpha, beta):
        import jax, jax.numpy as jnp
        import numpy as np
        N = 2500
        E = 40000
        D = 256
        H = 8
        DH = D // H
        ED = 64
        FF = 4 * D
        EPS = 1e-05

        def _layernorm(x, g, b):
            m = jnp.mean(x, axis=-1, keepdims=True)
            v = jnp.var(x, axis=-1, keepdims=True)
            return (x - m) * jax.lax.rsqrt(v + EPS) * g + b

        def _edge_attention(xn, edge_index, ef, ew, Wq, bq, Wk, bk, Wv, bv, We, be, Wo, bo):
            n = xn.shape[0]
            scale = DH ** (-0.5)
            q = (xn @ Wq + bq).reshape(n, H, DH)
            k = (xn @ Wk + bk).reshape(n, H, DH)
            v = (xn @ Wv + bv).reshape(n, H, DH)
            src, dst = (edge_index[0], edge_index[1])
            ep = ef @ We + be
            scores = jnp.einsum('ehd,ehd->eh', q[dst], k[src] + ep[:, None, :]) * scale
            scores = scores * ew[:, None]
            m = jax.ops.segment_max(scores, dst, num_segments=n)
            m = jnp.where(jnp.isfinite(m), m, 0.0)
            ex = jnp.exp(scores - m[dst])
            s = jax.ops.segment_sum(ex, dst, num_segments=n)
            attn = ex / s[dst]
            out = jax.ops.segment_sum(attn[:, :, None] * v[src], dst, num_segments=n)
            out = out.reshape(n, D) @ Wo + bo
            return out
        xn = _layernorm(x, ln1_g, ln1_b)
        attn_out = _edge_attention(xn, edge_index, edge_features, edge_weights, Wq, bq, Wk, bk, Wv, bv, We, be, Wo, bo)
        x = x + alpha * attn_out
        xn = _layernorm(x, ln2_g, ln2_b)
        ff = jax.nn.gelu(xn @ W1 + b1, approximate=False) @ W2 + b2
        x = x + beta * ff
        return x

    def _L0_ffn_ref(x, Wg, bg, W1, b1, W2, b2):
        import jax, jax.numpy as jnp
        import numpy as np
        B, S, D, E, H, K = (4, 512, 256, 8, 512, 2)
        Bv, Sv, Dv = x.shape
        gate_scores = x @ Wg + bg
        _, idx = jax.lax.top_k(gate_scores, K)
        mask = jax.nn.one_hot(idx, E, dtype=x.dtype).sum(axis=-2)
        xf = x.reshape(-1, Dv)
        mf = mask.reshape(-1, E)
        h = jax.nn.gelu(jnp.einsum('td,edh->teh', xf, W1) + b1[None], approximate=False)
        y = jnp.einsum('teh,ehd->ted', h, W2) + b2[None]
        out = jnp.einsum('ted,te->td', y, mf)
        return out.reshape(Bv, Sv, Dv)
    edge_index = jnp.stack([src, dst])
    x = x + _L0_gnn_ref(_layernorm(x, axis=-1), edge_attr_64, edge_weight, edge_index, L0_gnn_Wq, L0_gnn_bq, L0_gnn_Wk, L0_gnn_bk, L0_gnn_Wv, L0_gnn_bv, L0_gnn_We, L0_gnn_be, L0_gnn_Wo, L0_gnn_bo, L0_gnn_ln1_g, L0_gnn_ln1_b, L0_gnn_ln2_g, L0_gnn_ln2_b, L0_gnn_W1, L0_gnn_b1, L0_gnn_W2, L0_gnn_b2, L0_gnn_alpha, L0_gnn_beta)
    x = x + _L0_ffn_ref(_layernorm(x, axis=-1)[None], L0_ffn_Wg, L0_ffn_bg, L0_ffn_W1, L0_ffn_b1, L0_ffn_W2, L0_ffn_b2)[0]
    return x

_drawn_inputs = setup_inputs


def setup_inputs(seed=0):
    import zlib

    import numpy as np

    out = dict(_drawn_inputs(seed))
    spreads = {'L0_gnn_bq': (0.0, 0.375),
     'L0_gnn_bk': (0.0, 0.8),
     'L0_gnn_bv': (0.0, 0.1),
     'L0_gnn_be': (0.0, 0.8),
     'L0_gnn_bo': (0.0, 0.1),
     'L0_gnn_ln1_g': (1.0, 0.2),
     'L0_gnn_ln1_b': (0.0, 0.1),
     'L0_gnn_ln2_g': (1.0, 0.2),
     'L0_gnn_ln2_b': (0.0, 0.1),
     'L0_gnn_b1': (0.0, 0.1),
     'L0_gnn_b2': (0.0, 0.1),
     'L0_ffn_bg': (0.0, 0.1),
     'L0_ffn_b1': (0.0, 0.485),
     'L0_ffn_b2': (0.0, 0.1)}
    factors = {}
    for name, (base, spread) in spreads.items():
        noise = np.random.default_rng([zlib.crc32(name.encode()), seed]).standard_normal(out[name].shape)
        drawn = base * np.exp(spread * noise) if base else spread * noise
        out[name] = jnp.asarray(drawn.astype(out[name].dtype))
    for name, factor in factors.items():
        out[name] = (out[name] * factor).astype(out[name].dtype)
    return out
```

```python
import concourse.bass as bass
from concourse import mybir
from contextlib import ExitStack

fp32 = mybir.dt.float32
i32 = mybir.dt.int32
u32 = mybir.dt.uint32
ALU = mybir.AluOpType
ACT = mybir.ActivationFunctionType
AX = mybir.AxisListType

P = 128
NODES, D, HEADS, DH = 6250, 256, 8, 32
EDGES, ED = 100000, 64
FF, EXPERTS, EH = 1024, 8, 512
EPS = 1e-5
KC = D // P
WINDOWS = 50
EDGE_TILES = (EDGES + P - 1) // P
GROUP = 16
STEPS = (EDGE_TILES + WINDOWS - 1 + GROUP - 1) // GROUP * GROUP
SCOLS = (STEPS + P - 1) // P
STEPS_UP = SCOLS * P
TABLE_WINDOWS = STEPS - EDGE_TILES + 1
CHUNKS = 16
CHUNK_STEPS = STEPS // CHUNKS
CHUNK = CHUNK_STEPS * P
PAIRS = STEPS // 2
ACC = D + HEADS
BIG = 1e30
TINY = 1e-30


def bcast(ap, shape):
    return ap.broadcast_to(shape)


class Tools:

    def __init__(self, nc, ctx):
        self.nc, self.ctx = nc, ctx

    def sb(self, name, shape, dt=fp32):
        return self.ctx.enter_context(self.nc.sbuf_tensor(name, shape, dt))

    def ps(self, name, shape, dt=fp32):
        return self.ctx.enter_context(self.nc.psum_tensor(name, shape, dt))

    def sem(self, name):
        return self.ctx.enter_context(self.nc.semaphore(name))


def setup_phase(nc, g, a):
    with ExitStack() as ctx:
        t = Tools(nc, ctx)
        last_i = t.sb("last_i", [P, EDGE_TILES], i32)
        exit_step = t.sb("exit_step", [P, EDGE_TILES])
        iota_tile = t.sb("iota_tile", [P, EDGE_TILES])
        below = t.sb("below", [P, EDGE_TILES])
        iota_p = t.sb("iota_p", [P, 1])
        iota_step = t.sb("iota_step", [P, SCOLS])
        tile_f = t.sb("tile_f", [P, SCOLS])
        win_f = t.sb("win_f", [P, SCOLS])
        win_base = t.sb("win_base", [P, SCOLS])
        tile_i = t.sb("tile_i", [P, SCOLS], i32)
        win_i = t.sb("win_i", [P, SCOLS], i32)
        dst_g = t.sb("dst_g", [P, SCOLS, P], i32)
        src_g = t.sb("src_g", [P, SCOLS, P], i32)
        ew_g = t.sb("ew_g", [P, SCOLS, P])
        rel_g = t.sb("rel_g", [P, SCOLS, P])
        srcf_g = t.sb("srcf_g", [P, SCOLS, P])
        key_g = t.sb("key_g", [P, SCOLS, P])
        ok_g = t.sb("ok_g", [P, SCOLS, P])
        pad = t.sb("pad", [1, 1])
        tp = t.ps("tp", [P, 3, 512])
        loaded, consts, chain = t.sem("su_loaded"), t.sem("su_consts"), t.sem("su_chain")
        gathered, rows_out, rows_in = t.sem("su_gathered"), t.sem("su_rows_out"), t.sem("su_rows_in")
        tiles_known, laid, turned, evac = t.sem("su_tiles"), t.sem("su_laid"), t.sem("su_turned"), t.sem("su_evac")
        keys_out = t.sem("su_keys_out")
        block = ctx.enter_context(nc.Block())

        @block.sync
        def _(sp):
            sp.dma_start(last_i[:], bcast(a.last_dst, [P, EDGE_TILES])).then_inc(loaded, 16)
            sp.wait_ge(tiles_known, 1)
            with nc.allow_non_contiguous_dma(reason="two rows of 896 numbers"):
                sp.dma_start(a.steps_d[0:1, :].rearrange("o (c p) -> p (o c)", p=P), tile_i[:]).then_inc(rows_out, 16)
                sp.dma_start(a.steps_d[1:2, :].rearrange("o (c p) -> p (o c)", p=P), win_i[:]).then_inc(rows_out, 16)
            sp.wait_ge(rows_out, 32)
            sp.dma_start(g.tile_row[:], a.steps_d[0:1, :]).then_inc(rows_in, 16)
            sp.dma_start(g.win_row[0:1, 2:], a.steps_d[1:2, :]).then_inc(rows_in, 16)
            sp.wait_ge(laid, 1)
            sp.dma_start(a.keys_d[0:1, 1:1 + STEPS_UP * P].rearrange("o (c p e) -> p (o c) e", p=P, e=P),
                         key_g[:]).then_inc(keys_out, 16)
            sp.dma_start(a.keys_d[0:1, 0:1], pad[:]).then_inc(keys_out, 16)
            sp.wait_ge(keys_out, 32)
            sp.wait_ge(rows_in, 32)

        @block.gpsimd
        def _(pool):
            nc.gpsimd.iota(iota_tile[:], [[1, EDGE_TILES]], base=0, channel_multiplier=0,
                           allow_small_or_imprecise_dtypes=True).then_inc(consts, 1)
            nc.gpsimd.iota(iota_step[:], [[P, SCOLS]], base=0, channel_multiplier=1,
                           allow_small_or_imprecise_dtypes=True).then_inc(consts, 1)
            nc.gpsimd.iota(iota_p[:], [[0, 1]], base=0, channel_multiplier=1,
                           allow_small_or_imprecise_dtypes=True).then_inc(consts, 1)
            nc.gpsimd.iota(g.iota_row[:], [[1, P]], base=0, channel_multiplier=0,
                           allow_small_or_imprecise_dtypes=True).then_inc(consts, 1)
            nc.gpsimd.memset(pad[:], -5.0).then_inc(consts, 1)
            nc.gpsimd.memset(g.ones[:], 1.0).then_inc(consts, 1)
            nc.gpsimd.memset(g.win_row[0:1, 0:2], 0).then_inc(consts, 1)
            pool.wait_ge(tiles_known, 1)
            for c in range(SCOLS):
                for into, rows in ((dst_g, a.dst_rows), (src_g, a.src_rows), (ew_g, a.ew_rows)):
                    nc.gpsimd.indirect_dma_start(
                        out=into[:, c, :], out_offset=None, in_=rows,
                        in_offset=bass.IndirectOffsetOnAxis(ap=tile_i[:, c:c + 1], axis=0)).then_inc(gathered, 16)

        @block.vector
        def _(dve):
            count = [0]

            def link(ins):
                count[0] += 1
                ins.then_inc(chain, 1)
                dve.wait_ge(chain, count[0])

            dve.wait_ge(consts, 7)
            link(nc.vector.tensor_scalar(g.ident[:], g.iota_row[:], iota_p[:], None, ALU.is_equal))
            dve.wait_ge(loaded, 16)
            link(nc.vector.tensor_scalar(last_i[:], last_i[:], 7, None, ALU.arith_shift_right))
            link(nc.vector.tensor_tensor(exit_step[:], last_i[:], iota_tile[:], ALU.add))
            for c in range(SCOLS):
                link(nc.vector.tensor_scalar(below[:], exit_step[:], iota_step[:, c:c + 1], None,
                                             ALU.is_lt, ALU.add, accum_out=tile_f[:, c:c + 1]))
            link(nc.vector.tensor_scalar(tile_f[:], tile_f[:], float(EDGE_TILES - 1), None, ALU.min))
            link(nc.vector.tensor_tensor(win_f[:], iota_step[:], tile_f[:], ALU.subtract))
            link(nc.vector.tensor_scalar(win_base[:], win_f[:], -float(P), None, ALU.mult))
            link(nc.vector.tensor_copy(win_i[:], win_f[:]))
            nc.vector.tensor_copy(tile_i[:], tile_f[:]).then_inc(tiles_known, 1)
            dve.wait_ge(gathered, 16 * 3 * SCOLS)
            for c in range(SCOLS):
                link(nc.vector.tensor_scalar(rel_g[:, c, :], dst_g[:, c, :], win_base[:, c:c + 1], None, ALU.add))
            link(nc.vector.tensor_scalar(ok_g[:], rel_g[:], 0.0, None, ALU.is_ge))
            link(nc.vector.scalar_tensor_tensor(ok_g[:], rel_g[:], float(P), ok_g[:], ALU.is_lt, ALU.mult))
            link(nc.vector.scalar_tensor_tensor(key_g[:], dst_g[:], 1.0, ok_g[:], ALU.add, ALU.mult))
            nc.vector.tensor_copy(srcf_g[:], src_g[:]).then_inc(laid, 1)
            for c in range(SCOLS):
                dve.wait_ge(turned, 3 * (c + 1))
                cols = slice(c * P, (c + 1) * P)
                nc.vector.tensor_copy(g.rel[:, cols], tp[:, 0, 0:P])
                nc.vector.tensor_copy(g.src[:, cols], tp[:, 1, 0:P])
                nc.vector.tensor_scalar(g.ew[:, cols], tp[:, 2, 0:P], float(DH) ** -0.5, None,
                                        ALU.mult).then_inc(evac, 1)

        @block.tensor
        def _(pe):
            pe.wait_ge(laid, 1)
            for c in range(SCOLS):
                if c:
                    pe.wait_ge(evac, c)
                for n, rows in enumerate((rel_g, srcf_g, ew_g)):
                    nc.tensor.transpose(tp[:, n, 0:P], rows[:, c, :], g.ident[:]).then_inc(turned, 1)


def variances(nc, link, st, tmp, var_ready):
    me, ve, mo, vo = st[:, :, 1], st[:, :, 2], st[:, :, 4], st[:, :, 5]
    s, d, v = tmp[:, 0, :], tmp[:, 1, :], tmp[:, 2, :]
    link(nc.vector.tensor_tensor(s, me, mo, ALU.add))
    link(nc.vector.tensor_tensor(d, me, mo, ALU.subtract))
    link(nc.vector.tensor_tensor(v, ve, vo, ALU.add))
    link(nc.vector.tensor_scalar(v, v, 1.0 / D, EPS, ALU.mult, ALU.add))
    link(nc.vector.tensor_tensor(d, d, d, ALU.mult))
    nc.vector.scalar_tensor_tensor(v, d, 0.25, v, ALU.mult, ALU.add).then_inc(var_ready, 1)


def scales(nc, link, tmp, mv, mv_ready):
    link(nc.vector.reciprocal(mv[:, 0, :], tmp[:, 2, :]))
    nc.vector.scalar_tensor_tensor(mv[:, 1, :], tmp[:, 0, :], -0.5, mv[:, 0, :],
                                   ALU.mult, ALU.mult).then_inc(mv_ready, 1)


def node_phase(nc, g, a):
    HALF = WINDOWS // 2
    with ExitStack() as ctx:
        t = Tools(nc, ctx)
        xs = t.sb("xs", [P, WINDOWS, D])
        st = t.sb("st", [P, WINDOWS, 6])
        tmp = t.sb("tmp", [P, 3, WINDOWS])
        wqkv = t.sb("wqkv", [P, KC, 3 * D])
        bqkv = t.sb("bqkv", [P, 3 * D])
        g1, b1 = t.sb("g1", [P, KC]), t.sb("b1", [P, KC])
        xn = t.sb("xn", [P, 2, D])
        xT = t.sb("xT", [P, 2, KC, P])
        kv = t.sb("kv", [P, 2, 2 * D])
        tp = [t.ps(f"tp_a{u}", [P, 512]) for u in range(2)]
        qk_ps = [t.ps(f"qk_ps{u}", [P, 512]) for u in range(2)]
        v_ps = [t.ps(f"v_ps{u}", [P, 512]) for u in range(2)]
        x_in, w_in, chain = t.sem("na_x_in"), t.sem("na_w_in"), t.sem("na_chain")
        var_ready, root_ready, mv_ready = t.sem("na_var"), t.sem("na_root"), t.sem("na_mv")
        stats, normed = t.sem("na_stats"), t.sem("na_normed")
        xn_ready, xT_ready, zeroed = t.sem("na_xn"), t.sem("na_xT"), t.sem("na_zeroed")
        xn_turned, qkv_taken = t.sem("na_turned"), t.sem("na_taken")
        qkv_ready = t.sem("na_qkv")
        kv_out = [t.sem("na_kv_out0"), t.sem("na_kv_out1")]
        block = ctx.enter_context(nc.Block())
        k_w = a.k_d.rearrange("(w p) d -> w p d", p=P)
        v_w = a.v_d.rearrange("(w p) d -> w p d", p=P)

        @block.sync
        def _(sp):
            sp.dma_start(xs[:], a.x.rearrange("(w p) d -> p w d", p=P)).then_inc(x_in, 16)
            with nc.allow_non_contiguous_dma(reason="two short vectors"):
                sp.dma_start(g1[:], a.ln1_g.rearrange("o (c p) -> p (o c)", p=P)).then_inc(w_in, 16)
                sp.dma_start(b1[:], a.ln1_b.rearrange("o (c p) -> p (o c)", p=P)).then_inc(w_in, 16)
            sp.dma_start(wqkv[:], a.wqkv.rearrange("(c p) n -> p c n", p=P)).then_inc(w_in, 16)
            sp.dma_start(bqkv[:], bcast(a.bqkv, [P, 3 * D])).then_inc(w_in, 16)
            with sp.Fori(0, HALF) as i:
                for u in range(2):
                    w = i * 2 + u
                    sp.wait_ge(qkv_taken, w + 3)
                    sp.dma_start(k_w[bass.ds(w, 1), :, :].rearrange("o p d -> (o p) d"),
                                 kv[:, u, 0:D]).then_inc(kv_out[u], 16)
                    sp.dma_start(v_w[bass.ds(w, 1), :, :].rearrange("o p d -> (o p) d"),
                                 kv[:, u, D:2 * D]).then_inc(kv_out[u], 16)
            for u in range(2):
                sp.wait_ge(kv_out[u], 32 * HALF)

        @block.gpsimd
        def _(pool):
            nc.gpsimd.memset(g.q[:, WINDOWS:, :], 0.0).then_inc(zeroed, 1)
            pool.wait_ge(zeroed, 1)

        @block.vector
        def _(dve):
            count = [0]

            def link(ins):
                count[0] += 1
                ins.then_inc(chain, 1)
                dve.wait_ge(chain, count[0])

            dve.sem_inc(qkv_taken, 2)
            dve.wait_ge(x_in, 16)
            with dve.Fori(0, HALF) as i:
                for u in range(2):
                    w = i * 2 + u
                    nc.vector.bn_stats(st[:, bass.ds(w, 1), :], xs[:, bass.ds(w, 1), :]).then_inc(stats, 1)
            dve.wait_ge(stats, WINDOWS)
            variances(nc, link, st, tmp, var_ready)
            dve.wait_ge(root_ready, 1)
            scales(nc, link, tmp, g.mv0, mv_ready)
            with dve.Fori(0, HALF) as i:
                for u in range(2):
                    w = i * 2 + u
                    dve.wait_ge(normed, w + 1)
                    nc.vector.bn_stats(st[:, bass.ds(w, 1), :], xs[:, bass.ds(w, 1), :]).then_inc(stats, 1)
            dve.wait_ge(stats, 2 * WINDOWS)
            variances(nc, link, st, tmp, var_ready)
            dve.wait_ge(root_ready, 2)
            scales(nc, link, tmp, g.mv1, mv_ready)
            dve.wait_ge(w_in, 64)
            with dve.Fori(0, HALF) as i:
                for u in range(2):
                    w = i * 2 + u
                    dve.wait_ge(xn_turned, w + 3)
                    for c in range(KC):
                        last = nc.vector.tensor_scalar(xT[:, u, c, :], tp[u][:, c * P:(c + 1) * P],
                                                       g1[:, c:c + 1], b1[:, c:c + 1], ALU.mult, ALU.add)
                    last.then_inc(xT_ready, 1)
                    dve.wait_ge(qkv_ready, w + 1)
                    nc.vector.tensor_tensor(g.q[:, bass.ds(w, 1), :].rearrange("p o d -> p (o d)"),
                                            qk_ps[u][:, 0:D], bqkv[:, 0:D], ALU.add)
                    dve.wait_ge(kv_out[u], i * 32)
                    nc.vector.tensor_tensor(kv[:, u, 0:D], qk_ps[u][:, D:2 * D], bqkv[:, D:2 * D], ALU.add)
                    nc.vector.tensor_tensor(kv[:, u, D:2 * D], v_ps[u][:, 0:D], bqkv[:, 2 * D:3 * D],
                                            ALU.add).then_inc(qkv_taken, 1)

        @block.scalar
        def _(act):
            act.wait_ge(var_ready, 1)
            nc.scalar.activation(tmp[:, 2, :], tmp[:, 2, :], ACT.Sqrt).then_inc(root_ready, 1)
            act.wait_ge(mv_ready, 1)
            with act.Fori(0, HALF) as i:
                for u in range(2):
                    w = i * 2 + u
                    nc.scalar.activation(xs[:, bass.ds(w, 1), :], xs[:, bass.ds(w, 1), :], ACT.Identity,
                                         bias=g.mv0[:, 1, bass.ds(w, 1)],
                                         scale=g.mv0[:, 0, bass.ds(w, 1)]).then_inc(normed, 1)
            act.wait_ge(var_ready, 2)
            nc.scalar.activation(tmp[:, 2, :], tmp[:, 2, :], ACT.Sqrt).then_inc(root_ready, 1)
            act.wait_ge(mv_ready, 2)
            with act.Fori(0, HALF) as i:
                for u in range(2):
                    w = i * 2 + u
                    act.wait_ge(xn_turned, w + 1)
                    nc.scalar.activation(xn[:, u:u + 1, :], xs[:, bass.ds(w, 1), :], ACT.Identity,
                                         bias=g.mv1[:, 1, bass.ds(w, 1)],
                                         scale=g.mv1[:, 0, bass.ds(w, 1)]).then_inc(xn_ready, 1)

        @block.tensor
        def _(pe):
            pe.sem_inc(xn_turned, 2)
            pe.wait_ge(w_in, 64)
            with pe.Fori(0, HALF) as i:
                for u in range(2):
                    w = i * 2 + u
                    pe.wait_ge(xn_ready, w + 1)
                    pe.wait_ge(qkv_taken, w + 1)
                    for c in range(KC):
                        last = nc.tensor.transpose(tp[u][:, c * P:(c + 1) * P], xn[:, u, c * P:(c + 1) * P], g.ident[:])
                    last.then_inc(xn_turned, 1)
                    pe.wait_ge(xT_ready, w + 1)
                    for c in range(KC):
                        nc.tensor.matmul(qk_ps[u][:], xT[:, u, c, :], wqkv[:, c, 0:2 * D], start=(c == 0), stop=(c == KC - 1))
                    for c in range(KC):
                        last = nc.tensor.matmul(v_ps[u][:, 0:D], xT[:, u, c, :], wqkv[:, c, 2 * D:3 * D],
                                                start=(c == 0), stop=(c == KC - 1))
                    last.then_inc(qkv_ready, 1)


RING = 4
BODY_PAIRS = 8
TRIPS = PAIRS // BODY_PAIRS


def gather_rows(nc, pool, g, table, rows, rows_in, rows_free, staged, stage, carried):
    with pool.Fori(0, TRIPS) as i:
        for p in range(BODY_PAIRS):
            n = i * BODY_PAIRS + p
            pool.wait_ge(rows_free, n + 1)
            if p % RING == 0:
                h = p // RING
                nc.gpsimd.tensor_copy(stage[:, h, :], g.src[:, bass.ds(n * 2, 2 * RING)]).then_inc(staged, 1)
                pool.wait_ge(staged, i * 2 + h + 1)
            pool.sem_inc(carried, 1)
            for s in range(2):
                nc.gpsimd.indirect_dma_start(
                    out=rows[:, p % RING, s, :], out_offset=None, in_=table,
                    in_offset=bass.IndirectOffsetOnAxis(ap=stage[:, p // RING, 2 * (p % RING) + s:2 * (p % RING) + s + 1],
                                                        axis=0)).then_inc(rows_in[p % RING], 16)


def arrived(i, p):
    return (i * (BODY_PAIRS // RING) + p // RING + 1) * 32


def select_pair(nc, g, onehot, slot, n, done):
    for s in range(2):
        last = nc.vector.tensor_scalar(onehot[:, slot, s, :], g.iota_row[:], g.rel[:, bass.ds(n * 2 + s, 1)],
                                       None, ALU.is_equal)
    last.then_inc(done, 1)


def score_phase(nc, g, a):
    with ExitStack() as ctx:
        t = Tools(nc, ctx)
        k = t.sb("k_rows", [P, RING, 2, D])
        stage = t.sb("k_stage", [P, 2, 2 * RING], i32)
        ef = t.sb("ef", [ED, RING, 2, P])
        we, be = t.sb("we", [ED, DH]), t.sb("be", [1, DH])
        onehot = t.sb("onehot", [P, 2, 2, P])
        onehotT = t.sb("onehotT", [P, 2, 2, P])
        turn_ps = [t.ps(f"turn_ps{u}", [P, 512]) for u in range(2)]
        ep_ps = [t.ps(f"ep_ps{u}", [P, 512]) for u in range(2)]
        q_ps = [t.ps(f"q_ps{u}", [P, 512]) for u in range(2)]
        k_in = [t.sem(f"sc_k_in{r}") for r in range(RING)]
        ef_in = [t.sem(f"sc_ef_in{r}") for r in range(RING)]
        k_free, ef_free = t.sem("sc_k_free"), t.sem("sc_ef_free")
        ep_used, q_used, turn_copied, onehotT_used = (t.sem("sc_ep_used"), t.sem("sc_q_used"),
                                                      t.sem("sc_copied"), t.sem("sc_oT_used"))
        staged, selected, turned = t.sem("sc_staged"), t.sem("sc_selected"), t.sem("sc_turned")
        w_in, carried = t.sem("sc_w_in"), t.sem("sc_carried")
        block = ctx.enter_context(nc.Block())
        ef_t = a.ef_t.rearrange("(t d) e -> t d e", d=ED)

        @block.sync
        def _(sp):
            sp.dma_start(we[:], a.We).then_inc(w_in, 16)
            sp.dma_start(be[:], a.be).then_inc(w_in, 16)
            with sp.Fori(0, TRIPS) as i:
                for p in range(BODY_PAIRS):
                    n = i * BODY_PAIRS + p
                    sp.wait_ge(ef_free, n + 1)
                    for s in range(2):
                        tile = sp.value_load(g.tile_row[0:1, bass.ds(n * 2 + s, 1)], min_val=0, max_val=EDGE_TILES - 1)
                        sp.dma_start(ef[:, p % RING, s, :],
                                     ef_t[bass.ds(tile, 1), :, :].rearrange("o d e -> (o d) e")).then_inc(ef_in[p % RING], 16)

        @block.gpsimd
        def _(pool):
            gather_rows(nc, pool, g, a.k_d, k, k_in, k_free, staged, stage, carried)

        @block.vector
        def _(dve):
            dve.sem_inc(k_free, RING)
            dve.sem_inc(ep_used, 2)
            dve.sem_inc(q_used, 2)
            select_pair(nc, g, onehot, 0, 0, selected)
            with dve.Fori(0, TRIPS) as i:
                for p in range(BODY_PAIRS):
                    n = i * BODY_PAIRS + p
                    r = p % RING
                    dve.wait_ge(turned, n)
                    select_pair(nc, g, onehot, (p + 1) % 2, n + 1, selected)
                    rows = k[:, r, :, :].rearrange("p s (h d) -> p s h d", d=DH)
                    dve.wait_ge(k_in[r], arrived(i, p))
                    dve.wait_ge(ef_free, n + 1 + RING)
                    ep = ep_ps[p % 2][:, 0:2 * DH].rearrange("p (s d) -> p s d", s=2)[:, :, None, :]
                    nc.vector.tensor_tensor(rows, rows, bcast(ep, [P, 2, HEADS, DH]), ALU.add).then_inc(ep_used, 1)
                    dve.wait_ge(ep_used, n + 3)
                    dve.wait_ge(onehotT_used, n + 3)
                    flat = k[:, r, :, :].rearrange("p s c -> p (s c)")
                    nc.vector.tensor_tensor(flat, flat, q_ps[p % 2][:], ALU.mult).then_inc(q_used, 1)
                    dve.wait_ge(q_used, n + 3)
                    nc.vector.tensor_reduce(out=g.scores[:, bass.ds(n * 2, 2), :], in_=rows, op=ALU.add,
                                            axis=AX.X).then_inc(k_free, 1)

        @block.scalar
        def _(act):
            act.sem_inc(turn_copied, 2)
            with act.Fori(0, TRIPS) as i:
                for p in range(BODY_PAIRS):
                    n = i * BODY_PAIRS + p
                    act.wait_ge(turned, n + 1)
                    act.wait_ge(onehotT_used, n + 1)
                    nc.scalar.copy(onehotT[:, p % 2, :, :].rearrange("p s m -> p (s m)"),
                                   turn_ps[p % 2][:, 0:2 * P]).then_inc(turn_copied, 1)

        @block.tensor
        def _(pe):
            pe.sem_inc(ef_free, RING)
            pe.sem_inc(onehotT_used, 2)
            pe.wait_ge(w_in, 32)
            with pe.Fori(0, TRIPS) as i:
                for p in range(BODY_PAIRS):
                    n = i * BODY_PAIRS + p
                    pe.wait_ge(selected, n + 1)
                    pe.wait_ge(turn_copied, n + 1)
                    for s in range(2):
                        last = nc.tensor.transpose(turn_ps[p % 2][:, s * P:(s + 1) * P], onehot[:, p % 2, s, :], g.ident[:])
                    last.then_inc(turned, 1)
                    pe.wait_ge(ef_in[p % RING], arrived(i, p))
                    pe.wait_ge(ep_used, n + 1)
                    for s in range(2):
                        into = ep_ps[p % 2][:, s * DH:(s + 1) * DH]
                        nc.tensor.matmul(into, ef[:, p % RING, s, :], we[:], start=True, stop=False)
                        last = nc.tensor.matmul(into, g.ones[0:1, :], be[:], start=False, stop=True)
                    last.then_inc(ef_free, 1)
                    pe.wait_ge(turn_copied, n + 3)
                    pe.wait_ge(q_used, n + 1)
                    for s in range(2):
                        win = pe.value_load(g.win_row[0:1, bass.ds(n * 2 + s + 2, 1)], min_val=0, max_val=TABLE_WINDOWS - 1)
                        last = nc.tensor.matmul(q_ps[p % 2][:, s * D:(s + 1) * D], onehotT[:, p % 2, s, :],
                                                g.q[:, bass.ds(win, 1), :].rearrange("p o d -> p (o d)"),
                                                start=True, stop=True)
                    last.then_inc(onehotT_used, 1)


def softmax_phase(nc, g, a):
    with ExitStack() as ctx:
        t = Tools(nc, ctx)
        gap = t.sb("gap", [P, CHUNK + 1])
        sT = t.sb("sT", [P, CHUNK_STEPS, P])
        fwd = g.r1[:, 0:CHUNK]
        bwd = g.r1[:, CHUNK:2 * CHUNK]
        ends = t.sb("ends", [P, 4])
        row = t.sb("row", [1, 2, P])
        enter = t.sb("enter", [1, HEADS, CHUNKS])
        swept = t.sb("swept", [1, HEADS, CHUNKS])
        shifted = t.sb("shifted", [1, P])
        carry = t.sb("carry", [P, 2])
        tps = [t.ps(f"mx_ps{u}", [P, 512]) for u in range(2)]
        row_ps = t.ps("row_ps", [P, 512])
        keys_in, gap_ready, chain = t.sem("mx_keys"), t.sem("mx_gap"), t.sem("mx_chain")
        weighted, turned, taken = t.sem("mx_weighted"), t.sem("mx_turned"), t.sem("mx_taken")
        ends_ready, row_ready, shift_ready, carry_ready = (t.sem("mx_ends"), t.sem("mx_row"),
                                                           t.sem("mx_shift"), t.sem("mx_carry"))
        max_ready, exp_ready, back, back_taken = t.sem("mx_max"), t.sem("mx_exp"), t.sem("mx_back"), t.sem("mx_back_t")
        block = ctx.enter_context(nc.Block())
        sT_flat = sT[:, :, :].rearrange("p j e -> p (j e)")
        by_chunk = g.scores[:, :, :].rearrange("p (c j) h -> p c j h", j=CHUNK_STEPS)
        in_turn = g.r1[:, 0:CHUNK].rearrange("p (j c h) -> p j c h", c=CHUNKS, h=HEADS)
        BATCHES = CHUNK_STEPS // 4

        @block.sync
        def _(sp):
            for c in range(CHUNKS):
                sp.dma_start(gap[c * HEADS:(c + 1) * HEADS, :],
                             bcast(a.keys_d[0:1, c * CHUNK:c * CHUNK + CHUNK + 1], [HEADS, CHUNK + 1])).then_inc(keys_in, 16)

        @block.vector
        def _(dve):
            count = [0]

            def link(ins):
                count[0] += 1
                ins.then_inc(chain, 1)
                dve.wait_ge(chain, count[0])

            dve.wait_ge(keys_in, 16 * CHUNKS)
            ew = g.ew[:, 0:STEPS].rearrange("p (c j) -> p c j", j=CHUNK_STEPS)[:, :, :, None]
            for c in range(CHUNKS):
                nc.vector.tensor_tensor(in_turn[:, :, c, :], by_chunk[:, c, :, :],
                                        bcast(ew[:, c, :, :], [P, CHUNK_STEPS, HEADS]), ALU.mult).then_inc(weighted, 1)
            link(nc.vector.tensor_tensor(bwd[:], gap[:, 1:], gap[:, 0:CHUNK], ALU.not_equal))
            link(nc.vector.tensor_scalar(gap[:, 0:CHUNK], bwd[:], -BIG, None, ALU.mult))
            for b in range(BATCHES):
                dve.wait_ge(turned, b + 1)
                nc.vector.tensor_copy(sT_flat[:, b * 512:(b + 1) * 512], tps[b % 2][:]).then_inc(taken, 1)
            dve.wait_ge(taken, BATCHES)

            def sweep(turn, gaps, data, out, last, step):
                def way(ap):
                    return ap[:, ::step] if step < 0 else ap
                link(nc.vector.tensor_tensor_scan(way(out), way(gaps), way(data), -BIG, ALU.add, ALU.max))
                link(nc.vector.tensor_copy(ends[:, 0:1], out[:, last:last + 1]))
                nc.vector.tensor_reduce(out=ends[:, 1:2], in_=gaps, op=ALU.min, axis=AX.X).then_inc(ends_ready, 1)
                dve.wait_ge(row_ready, turn + 1)
                ps = row_ps[0:1, 0:2 * P].rearrange("o (n c h) -> o n h c", n=2, h=HEADS)
                link(nc.vector.tensor_copy(enter[:], ps[:, 0, :, :]))
                link(nc.vector.tensor_copy(swept[:], ps[:, 1, :, :]))
                edge = 0 if step > 0 else CHUNKS - 1
                link(nc.vector.memset(swept[:, :, edge:edge + 1], -BIG))
                e, s = enter[:].rearrange("o h c -> o (h c)"), swept[:].rearrange("o h c -> o (h c)")
                link(nc.vector.tensor_tensor_scan(way(e), way(s), way(e), -BIG, ALU.add, ALU.max))
                link(nc.vector.memset(shifted[:], -BIG))
                sh = shifted[:].rearrange("o (c h) -> o h c", h=HEADS)
                if step > 0:
                    cp = nc.vector.tensor_copy(sh[:, :, 1:], enter[:, :, 0:CHUNKS - 1])
                else:
                    cp = nc.vector.tensor_copy(sh[:, :, 0:CHUNKS - 1], enter[:, :, 1:])
                cp.then_inc(shift_ready, 1)
                dve.wait_ge(carry_ready, turn + 1)
                link(nc.vector.tensor_copy(carry[:, turn:turn + 1], row_ps[:, 256:257]))
                link(nc.vector.tensor_tensor_scan(way(out), way(gaps), way(data), carry[:, turn:turn + 1],
                                                  ALU.add, ALU.max))

            link(nc.vector.memset(gap[:, CHUNK:], -BIG))
            sweep(0, gap[:, 0:CHUNK], sT_flat[:], fwd[:], CHUNK - 1, 1)
            dve.wait_ge(gap_ready, 16)
            sweep(1, gap[:, 1:CHUNK + 1], fwd[:], bwd[:], 0, -1)
            link(nc.vector.tensor_tensor(sT_flat[:], sT_flat[:], bwd[:], ALU.subtract))
            nc.vector.engine_nop().then_inc(max_ready, 1)
            for b in range(BATCHES):
                dve.wait_ge(back, b + 1)
                nc.vector.tensor_copy(by_chunk[:, :, 4 * b:4 * b + 4, :].rearrange("p c j h -> p j c h"),
                                      tps[b % 2][:].rearrange("p (j c h) -> p j c h", j=4, h=HEADS)).then_inc(back_taken, 1)
            dve.wait_ge(back_taken, BATCHES)

        @block.scalar
        def _(act):
            act.wait_ge(ends_ready, 1)
            act.dma_start(gap[0:P - HEADS, CHUNK:CHUNK + 1], gap[HEADS:P, 0:1]).then_inc(gap_ready, 16)
            for b in range(BATCHES):
                if b == 0:
                    act.wait_ge(max_ready, 1)
                nc.scalar.activation(sT_flat[:, b * 512:(b + 1) * 512], sT_flat[:, b * 512:(b + 1) * 512],
                                     ACT.Exp).then_inc(exp_ready, 1)

        @block.tensor
        def _(pe):
            pe.wait_ge(weighted, CHUNKS)
            for b in range(BATCHES):
                if b >= 2:
                    pe.wait_ge(taken, b - 1)
                for j in range(4):
                    last = nc.tensor.transpose(tps[b % 2][:, j * P:(j + 1) * P], in_turn[:, 4 * b + j, :, :].rearrange("p c h -> p (c h)"), g.ident[:])
                last.then_inc(turned, 1)
            for turn in range(2):
                pe.wait_ge(ends_ready, turn + 1)
                for n in range(2):
                    last = nc.tensor.matmul(row_ps[0:1, n * P:(n + 1) * P], ends[:, n:n + 1], g.ident[:], start=True, stop=True)
                last.then_inc(row_ready, 1)
                pe.wait_ge(shift_ready, turn + 1)
                nc.tensor.matmul(row_ps[:, 256:257], shifted[0:1, :], g.ones[0:1, 0:1], start=True, stop=True).then_inc(carry_ready, 1)
            for b in range(BATCHES):
                pe.wait_ge(exp_ready, b + 1)
                if b >= 2:
                    pe.wait_ge(back_taken, b - 1)
                for j in range(4):
                    last = nc.tensor.transpose(tps[b % 2][:, j * P:(j + 1) * P], sT[:, 4 * b + j, :], g.ident[:])
                last.then_inc(back, 1)


def gather_phase(nc, g, a):
    with ExitStack() as ctx:
        t = Tools(nc, ctx)
        v = t.sb("v_rows", [P, RING, 2, D])
        stage = t.sb("v_stage", [P, 2, 2 * RING], i32)
        onehot = t.sb("onehot_v", [P, 2, 2, P])
        sum_ps = [[t.ps(f"sum_ps{u}{s}", [P, 512]) for s in range(2)] for u in range(2)]
        v_in = [t.sem(f"ag_v_in{r}") for r in range(RING)]
        staged, selected, weighted = t.sem("ag_staged"), t.sem("ag_selected"), t.sem("ag_weighted")
        zeroed, carried = t.sem("ag_zeroed"), t.sem("ag_carried")
        summed, added, acc_chain = t.sem("ag_summed"), t.sem("ag_added"), t.sem("ag_acc")
        block = ctx.enter_context(nc.Block())

        @block.gpsimd
        def _(pool):
            gather_rows(nc, pool, g, a.v_d, v, v_in, added, staged, stage, carried)

        @block.vector
        def _(dve):
            nc.vector.memset(g.acc[:], 0.0).then_inc(zeroed, 1)
            for s in range(2):
                nc.vector.memset(sum_ps[1][s][:, 0:ACC], 0.0).then_inc(zeroed, 1)
            dve.sem_inc(added, RING - 1)
            dve.sem_inc(summed, 1)
            dve.wait_ge(zeroed, 3)
            select_pair(nc, g, onehot, 0, 0, selected)

            def add_pair(n, slot):
                for s in range(2):
                    win = dve.value_load(g.win_row[0:1, bass.ds(n * 2 + s + 2, 1)], min_val=0, max_val=TABLE_WINDOWS - 1)
                    into = g.acc[:, bass.ds(win, 1), :].rearrange("p o c -> p (o c)")
                    dve.wait_ge(acc_chain if s else added, (n + 2) if s else n + RING)
                    nc.vector.tensor_tensor(into, into, sum_ps[slot][s][:, 0:ACC],
                                            ALU.add).then_inc(added if s else acc_chain, 1)

            with dve.Fori(0, TRIPS) as i:
                for p in range(BODY_PAIRS):
                    n = i * BODY_PAIRS + p
                    r = p % RING
                    dve.wait_ge(summed, n + 1)
                    select_pair(nc, g, onehot, (p + 1) % 2, n + 1, selected)
                    rows = v[:, r, :, :].rearrange("p s (h d) -> p (s h) d", d=DH)
                    dve.wait_ge(v_in[r], arrived(i, p))
                    ex = g.scores[:, bass.ds(n * 2, 2), :].rearrange("p s h -> p (s h)")[:, :, None]
                    nc.vector.tensor_tensor(rows, rows, bcast(ex, [P, 2 * HEADS, DH]), ALU.mult).then_inc(weighted, 1)
                    add_pair(n - 1, (p + 1) % 2)
            dve.wait_ge(summed, PAIRS + 1)
            add_pair(PAIRS - 1, (PAIRS - 1) % 2)
            dve.wait_ge(added, PAIRS + RING)

        @block.tensor
        def _(pe):
            with pe.Fori(0, TRIPS) as i:
                for p in range(BODY_PAIRS):
                    n = i * BODY_PAIRS + p
                    pe.wait_ge(selected, n + 1)
                    pe.wait_ge(weighted, n + 1)
                    pe.wait_ge(added, n + RING - 1)
                    for s in range(2):
                        into = sum_ps[p % 2][s]
                        nc.tensor.matmul(into[:, 0:D], onehot[:, p % 2, s, :], v[:, p % RING, s, :], start=True, stop=True)
                        last = nc.tensor.matmul(into[:, D:ACC], onehot[:, p % 2, s, :],
                                                g.scores[:, bass.ds(n * 2 + s, 1), :].rearrange("p o h -> p (o h)"),
                                                start=True, stop=True)
                    last.then_inc(summed, 1)


def attention_out_phase(nc, g, a):
    HALF = WINDOWS // 2
    with ExitStack() as ctx:
        t = Tools(nc, ctx)
        xs = t.sb("xs_o", [P, 2, D])
        h0 = t.sb("h0", [P, 2, D])
        rs = t.sb("rs", [P, 2, HEADS])
        attn = t.sb("attn", [P, 2, D])
        attnT = t.sb("attnT", [P, 2, D])
        proj = t.sb("proj", [P, 2, D])
        wo, bo, alpha = t.sb("wo", [P, KC, D]), t.sb("bo", [P, D]), t.sb("alpha", [P, 1])
        st, tmp = t.sb("st_o", [P, WINDOWS, 6]), t.sb("tmp_o", [P, 3, WINDOWS])
        tp = [t.ps(f"tp_o{u}", [P, 512]) for u in range(2)]
        ps = [t.ps(f"ps_o{u}", [P, 512]) for u in range(2)]
        w_in, x_in = t.sem("ao_w_in"), [t.sem("ao_x_in0"), t.sem("ao_x_in1")]
        chain, rs_chain, attn_ready, turned, attnT_ready = (t.sem("ao_chain"), t.sem("ao_rs"), t.sem("ao_attn"),
                                                            t.sem("ao_turned"), t.sem("ao_attnT"))
        h0_ready, proj_ready, proj_chain, x1_ready, stats = (t.sem("ao_h0"), t.sem("ao_proj"), t.sem("ao_pch"),
                                                             t.sem("ao_x1"), t.sem("ao_stats"))
        var_ready, root_ready, mv_ready = t.sem("ao_var"), t.sem("ao_root"), t.sem("ao_mv")
        block = ctx.enter_context(nc.Block())
        x_w = a.x.rearrange("(w p) d -> w p d", p=P)

        @block.sync
        def _(sp):
            sp.dma_start(wo[:], a.Wo.rearrange("(c p) n -> p c n", p=P)).then_inc(w_in, 16)
            sp.dma_start(bo[:], bcast(a.bo, [P, D])).then_inc(w_in, 16)
            sp.dma_start(alpha[:], bcast(a.alpha, [P, 1])).then_inc(w_in, 16)
            sp.sem_inc(h0_ready, 2)
            with sp.Fori(0, HALF) as i:
                for u in range(2):
                    w = i * 2 + u
                    sp.wait_ge(h0_ready, w + 1)
                    sp.dma_start(xs[:, u, :], x_w[bass.ds(w, 1), :, :].rearrange("o p d -> (o p) d")).then_inc(x_in[u], 16)

        @block.vector
        def _(dve):
            count = [0]

            def link(ins):
                count[0] += 1
                ins.then_inc(chain, 1)
                dve.wait_ge(chain, count[0])

            dve.sem_inc(x1_ready, 2)
            dve.wait_ge(w_in, 48)
            with dve.Fori(0, HALF) as i:
                for u in range(2):
                    w = i * 2 + u
                    s_sum = g.acc[:, bass.ds(w, 1), D:ACC].rearrange("p o h -> p (o h)")
                    o = g.acc[:, bass.ds(w, 1), 0:D].rearrange("p o (h d) -> p (o h) d", d=DH)
                    nc.vector.tensor_scalar(rs[:, u, :], s_sum, TINY, None, ALU.max).then_inc(rs_chain, 1)
                    dve.wait_ge(rs_chain, w * 2 + 1)
                    nc.vector.reciprocal(rs[:, u, :], rs[:, u, :]).then_inc(rs_chain, 1)
                    dve.wait_ge(rs_chain, w * 2 + 2)
                    nc.vector.tensor_tensor(attn[:, u, :].rearrange("p (h d) -> p h d", d=DH), o,
                                            bcast(rs[:, u, :, None], [P, HEADS, DH]), ALU.mult).then_inc(attn_ready, 1)
                    dve.wait_ge(proj_ready, w + 1)
                    nc.vector.tensor_tensor(proj[:, u, :], ps[u][:, 0:D], bo[:], ALU.add).then_inc(proj_chain, 1)
                    dve.wait_ge(proj_chain, w + 1)
                    dve.wait_ge(h0_ready, w + 3)
                    x1 = g.acc[:, bass.ds(w, 1), 0:D].rearrange("p o d -> p (o d)")
                    nc.vector.scalar_tensor_tensor(x1, proj[:, u, :], alpha[:], h0[:, u, :],
                                                   ALU.mult, ALU.add).then_inc(x1_ready, 1)
                    dve.wait_ge(x1_ready, w + 3)
                    nc.vector.bn_stats(st[:, bass.ds(w, 1), :], g.acc[:, bass.ds(w, 1), 0:D]).then_inc(stats, 1)
            dve.wait_ge(stats, WINDOWS)
            variances(nc, link, st, tmp, var_ready)
            dve.wait_ge(root_ready, 1)
            scales(nc, link, tmp, g.mv1, mv_ready)
            dve.wait_ge(mv_ready, 1)

        @block.scalar
        def _(act):
            with act.Fori(0, HALF) as i:
                for u in range(2):
                    w = i * 2 + u
                    act.wait_ge(x_in[u], i * 16 + 16)
                    act.wait_ge(x1_ready, w + 1)
                    nc.scalar.activation(h0[:, u, :], xs[:, u, :], ACT.Identity, bias=g.mv0[:, 1, bass.ds(w, 1)],
                                         scale=g.mv0[:, 0, bass.ds(w, 1)]).then_inc(h0_ready, 1)
                    act.wait_ge(turned, w + 1)
                    nc.scalar.copy(attnT[:, u, :], tp[u][:, 0:D]).then_inc(attnT_ready, 1)
            act.wait_ge(var_ready, 1)
            nc.scalar.activation(tmp[:, 2, :], tmp[:, 2, :], ACT.Sqrt).then_inc(root_ready, 1)

        @block.tensor
        def _(pe):
            pe.wait_ge(w_in, 48)
            with pe.Fori(0, HALF) as i:
                for u in range(2):
                    w = i * 2 + u
                    pe.wait_ge(attn_ready, w + 1)
                    for c in range(KC):
                        last = nc.tensor.transpose(tp[u][:, c * P:(c + 1) * P], attn[:, u, c * P:(c + 1) * P], g.ident[:])
                    last.then_inc(turned, 1)
                    pe.wait_ge(attnT_ready, w + 1)
                    pe.wait_ge(x1_ready, w + 1)
                    for c in range(KC):
                        last = nc.tensor.matmul(ps[u][:, 0:D], attnT[:, u, c * P:(c + 1) * P], wo[:, c, :],
                                                start=(c == 0), stop=(c == KC - 1))
                    last.then_inc(proj_ready, 1)


def ffn_phase(nc, g, a):
    HALF = WINDOWS // 2
    FC = FF // P
    HR = 4
    with ExitStack() as ctx:
        t = Tools(nc, ctx)
        w1, w2 = t.sb("w1", [P, KC, FF]), t.sb("w2", [P, FC, D])
        b1, b2, beta = t.sb("b1_f", [P, FC]), t.sb("b2_f", [P, D]), t.sb("beta", [P, 1])
        g2, bb2 = t.sb("g2", [P, KC]), t.sb("bb2", [P, KC])
        xs = t.sb("xs_f", [P, 2, D])
        xn = t.sb("xn_f", [P, 2, D])
        xT = t.sb("xT_f", [P, KC, 2 * P])
        hT = t.sb("hT", [P, FC, 2 * P])
        part = t.sb("part", [P, 2, D])
        st, tmp = t.sb("st_f", [P, WINDOWS, 6]), t.sb("tmp_f", [P, 3, WINDOWS])
        tp = t.ps("tp_f", [P, 512])
        h_ps = [t.ps(f"h_ps{u}", [P, 512]) for u in range(HR)]
        y_ps = [t.ps(f"y_ps{u}", [P, 512]) for u in range(2)]
        w_in, x_in = t.sem("ff_w_in"), t.sem("ff_x_in")
        chain, xn_ready, turned, xT_ready = t.sem("ff_chain"), t.sem("ff_xn"), t.sem("ff_turned"), t.sem("ff_xT")
        h_ready, h_act, y_ready = t.sem("ff_h"), t.sem("ff_h_act"), t.sem("ff_y")
        part_ready, x2_ready, y_done, stats = t.sem("ff_part"), t.sem("ff_x2"), t.sem("ff_ydone"), t.sem("ff_stats")
        var_ready, root_ready, mv_ready = t.sem("ff_var"), t.sem("ff_root"), t.sem("ff_mv")
        block = ctx.enter_context(nc.Block())
        x_w = a.x.rearrange("(w p) d -> p w d", p=P)

        @block.sync
        def _(sp):
            sp.dma_start(w1[:], a.W1.rearrange("(c p) n -> p c n", p=P)).then_inc(w_in, 16)
            sp.dma_start(w2[:], a.W2.rearrange("(c p) n -> p c n", p=P)).then_inc(w_in, 16)
            with nc.allow_non_contiguous_dma(reason="short vectors"):
                sp.dma_start(b1[:], a.b1.rearrange("o (c p) -> p (o c)", p=P)).then_inc(w_in, 16)
                sp.dma_start(g2[:], a.ln2_g.rearrange("o (c p) -> p (o c)", p=P)).then_inc(w_in, 16)
                sp.dma_start(bb2[:], a.ln2_b.rearrange("o (c p) -> p (o c)", p=P)).then_inc(w_in, 16)
            sp.dma_start(b2[:], bcast(a.b2, [P, D])).then_inc(w_in, 16)
            sp.dma_start(beta[:], bcast(a.beta, [P, 1])).then_inc(w_in, 16)
            with sp.Fori(0, HALF) as i:
                sp.wait_ge(y_done, i)
                sp.dma_start(xs[:], x_w[:, bass.ds(i * 2, 2), :]).then_inc(x_in, 16)

        @block.vector
        def _(dve):
            count = [0]

            def link(ins):
                count[0] += 1
                ins.then_inc(chain, 1)
                dve.wait_ge(chain, count[0])

            dve.wait_ge(w_in, 112)
            with dve.Fori(0, HALF) as i:
                dve.wait_ge(turned, i + 1)
                for c in range(KC):
                    last = nc.vector.tensor_scalar(xT[:, c, :], tp[:, c * 2 * P:(c + 1) * 2 * P],
                                                   g2[:, c:c + 1], bb2[:, c:c + 1], ALU.mult, ALU.add)
                last.then_inc(xT_ready, 1)
                for s in range(2):
                    dve.wait_ge(y_ready, i * 2 + s + 1)
                    nc.vector.tensor_tensor(part[:, s, :], y_ps[s][:, 0:D], b2[:], ALU.add).then_inc(part_ready, 1)
                dve.wait_ge(part_ready, i * 2 + 2)
                x1 = g.acc[:, bass.ds(i * 2, 2), 0:D]
                nc.vector.scalar_tensor_tensor(x1, part[:], beta[:], x1, ALU.mult, ALU.add).then_inc(x2_ready, 1)
                dve.wait_ge(x2_ready, i + 1)
                dve.wait_ge(x_in, i * 16 + 16)
                nc.vector.tensor_tensor(x1, x1, xs[:], ALU.add).then_inc(y_done, 1)
                dve.wait_ge(y_done, i + 1)
                for s in range(2):
                    nc.vector.bn_stats(st[:, bass.ds(i * 2 + s, 1), :], g.acc[:, bass.ds(i * 2 + s, 1), 0:D]).then_inc(stats, 1)
            dve.wait_ge(stats, WINDOWS)
            variances(nc, link, st, tmp, var_ready)
            dve.wait_ge(root_ready, 1)
            scales(nc, link, tmp, g.mv2, mv_ready)
            dve.wait_ge(mv_ready, 1)

        @block.scalar
        def _(act):
            act.sem_inc(h_act, HR)

            def norm_pair(i):
                for s in range(2):
                    w = i * 2 + s
                    last = nc.scalar.activation(xn[:, s:s + 1, :], g.acc[:, bass.ds(w, 1), 0:D], ACT.Identity,
                                                bias=g.mv1[:, 1, bass.ds(w, 1)], scale=g.mv1[:, 0, bass.ds(w, 1)])
                last.then_inc(xn_ready, 1)

            act.wait_ge(w_in, 112)
            with act.Fori(0, HALF) as i:
                act.wait_ge(turned, i)
                norm_pair(i)
                for f in range(FC):
                    act.wait_ge(h_ready, i * FC + f + 1)
                    if f == 0:
                        act.wait_ge(y_ready, i * 2)
                    nc.scalar.activation(hT[:, f, :], h_ps[f % HR][:, 0:2 * P], ACT.Gelu,
                                         bias=b1[:, f:f + 1]).then_inc(h_act, 1)
            act.wait_ge(var_ready, 1)
            nc.scalar.activation(tmp[:, 2, :], tmp[:, 2, :], ACT.Sqrt).then_inc(root_ready, 1)

        @block.tensor
        def _(pe):
            pe.wait_ge(w_in, 112)
            with pe.Fori(0, HALF) as i:
                pe.wait_ge(xn_ready, i + 1)
                for c in range(KC):
                    for s in range(2):
                        last = nc.tensor.transpose(tp[:, (2 * c + s) * P:(2 * c + s + 1) * P],
                                                   xn[:, s, c * P:(c + 1) * P], g.ident[:])
                last.then_inc(turned, 1)
                pe.wait_ge(xT_ready, i + 1)
                for f in range(FC):
                    pe.wait_ge(h_act, i * FC + f + 1)
                    for c in range(KC):
                        last = nc.tensor.matmul(h_ps[f % HR][:, 0:2 * P], w1[:, c, f * P:(f + 1) * P], xT[:, c, :],
                                                start=(c == 0), stop=(c == KC - 1))
                    last.then_inc(h_ready, 1)
                pe.wait_ge(h_act, i * FC + FC + HR)
                pe.wait_ge(part_ready, i * 2)
                for s in range(2):
                    for f in range(FC):
                        last = nc.tensor.matmul(y_ps[s][:, 0:D], hT[:, f, s * P:(s + 1) * P], w2[:, f, :],
                                                start=(f == 0), stop=(f == FC - 1))
                    last.then_inc(y_ready, 1)


def mixture_phase(nc, g, a):
    HALF = WINDOWS // 2
    HC = EH // P
    HR = 4
    with ExitStack() as ctx:
        t = Tools(nc, ctx)
        w1, w2 = t.sb("w1_m", [P, EXPERTS, KC, EH]), t.sb("w2_m", [P, EXPERTS, HC, D])
        b1, b2 = t.sb("b1_m", [P, EXPERTS, HC]), t.sb("b2_m", [EXPERTS, D])
        wg, bg = t.sb("wg", [P, KC, EXPERTS]), t.sb("bg", [P, EXPERTS])
        xn = t.sb("xn_m", [P, 2, D])
        xT = t.sb("xT_m", [P, KC, 2 * P])
        hT = t.sb("hT_m", [P, 2, HC, 2 * P])
        gs, top, ind, indf = (t.sb("gs", [P, 2, EXPERTS]), t.sb("top", [P, 2, EXPERTS]),
                              t.sb("ind", [P, 2, EXPERTS], u32), t.sb("indf", [P, 2, EXPERTS]))
        first, mask, maskT = t.sb("first", [P, 2, EXPERTS]), t.sb("mask", [P, 2, EXPERTS]), t.sb("maskT", [EXPERTS, 2, P])
        res = t.sb("res", [P, 2, 2, D])
        tp = t.ps("tp_m", [P, 512])
        gate_ps = t.ps("gate_ps", [P, 512])
        h_ps = [t.ps(f"h_ps_m{u}", [P, 512]) for u in range(HR)]
        y_ps = [t.ps(f"y_ps_m{u}", [P, 512]) for u in range(2)]
        w_in, chain = t.sem("mo_w_in"), t.sem("mo_chain")
        xn_ready, turned, xT_ready = t.sem("mo_xn"), t.sem("mo_turned"), t.sem("mo_xT")
        gate_ready, gate_chain, mask_ready, maskT_ps, maskT_ready, bias_ready = (
            t.sem("mo_gate"), t.sem("mo_gch"), t.sem("mo_mask"), t.sem("mo_maskTp"), t.sem("mo_maskT"), t.sem("mo_bias"))
        h_ready, h_act, y_ready, res_ready = t.sem("mo_h"), t.sem("mo_hact"), t.sem("mo_y"), t.sem("mo_res")
        out_done = [t.sem("mo_out0"), t.sem("mo_out1")]
        block = ctx.enter_context(nc.Block())
        out_w = a.out.rearrange("(w p) d -> p w d", p=P)
        GSTEPS = 5
        carried = t.sem("mo_carried")

        @block.sync
        def _(sp):
            sp.dma_start(w1[:], a.E1.rearrange("e (c p) n -> p (e c) n", p=P).rearrange("p (e c) n -> p e c n", e=EXPERTS)).then_inc(w_in, 16)
            sp.dma_start(w2[:], a.E2.rearrange("e (c p) n -> p (e c) n", p=P).rearrange("p (e c) n -> p e c n", e=EXPERTS)).then_inc(w_in, 16)
            with nc.allow_non_contiguous_dma(reason="short vectors"):
                sp.dma_start(b1[:], a.eb1.rearrange("e (c p) -> p e c", p=P)).then_inc(w_in, 16)
            sp.dma_start(b2[:], a.eb2).then_inc(w_in, 16)
            sp.dma_start(wg[:], a.Wg.rearrange("(c p) n -> p c n", p=P)).then_inc(w_in, 16)
            sp.dma_start(bg[:], bcast(a.bg, [P, EXPERTS])).then_inc(w_in, 16)
            with sp.Fori(0, HALF) as i:
                sp.wait_ge(res_ready, (i + 1) * (EXPERTS + 1))
                sp.dma_start(out_w[:, bass.ds(i * 2, 2), :], res[:, 0, :, :]).then_inc(out_done[0], 16)
            sp.wait_ge(out_done[0], 16 * HALF)

        @block.vector
        def _(dve):
            dve.wait_ge(w_in, 96)
            with dve.Fori(0, HALF) as i:
                dve.wait_ge(gate_ready, i + 1)

                def step(n, ins):
                    ins.then_inc(gate_chain, 1)
                    dve.wait_ge(gate_chain, i * GSTEPS + n)

                step(1, nc.vector.tensor_tensor(gs[:], gate_ps[:, 0:2 * EXPERTS].rearrange("p (s e) -> p s e", s=2),
                                                bcast(bg[:, None, :], [P, 2, EXPERTS]), ALU.add))
                dve.sem_inc(carried, 1)
                for s in range(2):
                    last = nc.vector.max(top[:, s, :], gs[:, s, :])
                step(2, last)
                dve.sem_inc(carried, 1)
                for s in range(2):
                    last = nc.vector.max_index(ind[:, s, :], top[:, s, :], gs[:, s, :])
                step(3, last)
                step(4, nc.vector.tensor_copy(indf[:], ind[:]))
                for s in range(2):
                    last = nc.vector.tensor_scalar(first[:, s, :], g.iota_row[:, 0:EXPERTS], indf[:, s, 0:1], None, ALU.is_equal)
                step(5, last)
                for s in range(2):
                    last = nc.vector.scalar_tensor_tensor(mask[:, s, :], g.iota_row[:, 0:EXPERTS], indf[:, s, 1:2],
                                                          first[:, s, :], ALU.is_equal, ALU.add)
                last.then_inc(mask_ready, 1)
                dve.wait_ge(mask_ready, i + 1)
                dve.wait_ge(maskT_ps, i + 1)
                nc.vector.tensor_copy(maskT[:], gate_ps[0:EXPERTS, 2 * P:4 * P].rearrange("e (s p) -> e s p", s=2)).then_inc(maskT_ready, 1)
                dve.wait_ge(bias_ready, i + 1)
                dve.wait_ge(out_done[0], i * 16)
                y = g.acc[:, bass.ds(i * 2, 2), 0:D]
                res_now = res[:, 0, :, :]
                nc.vector.tensor_tensor(res_now, y, y_ps[1][:].rearrange("p (s d) -> p s d", s=2), ALU.add).then_inc(res_ready, 1)
                for e in range(EXPERTS):
                    dve.wait_ge(y_ready, i * EXPERTS + e + 1)
                    dve.wait_ge(res_ready, i * (EXPERTS + 1) + e + 1)
                    for s in range(2):
                        last = nc.vector.scalar_tensor_tensor(res[:, 0, s, :], y_ps[e % 2][:, s * D:(s + 1) * D], mask[:, s, e:e + 1],
                                                              res[:, 0, s, :], ALU.mult, ALU.add)
                    last.then_inc(res_ready, 1)

        @block.scalar
        def _(act):
            act.wait_ge(w_in, 96)
            act.sem_inc(h_act, HR)
            with act.Fori(0, HALF) as i:
                act.wait_ge(turned, i)
                for s in range(2):
                    w = i * 2 + s
                    last = nc.scalar.activation(xn[:, s:s + 1, :], g.acc[:, bass.ds(w, 1), 0:D], ACT.Identity,
                                                bias=g.mv2[:, 1, bass.ds(w, 1)], scale=g.mv2[:, 0, bass.ds(w, 1)])
                last.then_inc(xn_ready, 1)
                act.wait_ge(turned, i + 1)
                nc.scalar.copy(xT[:, :, :].rearrange("p c n -> p (c n)"), tp[:]).then_inc(xT_ready, 1)
                for e in range(EXPERTS):
                    if e >= 2:
                        act.wait_ge(y_ready, i * EXPERTS + e - 1)
                    for f in range(HC):
                        act.wait_ge(h_ready, i * EXPERTS * HC + e * HC + f + 1)
                        nc.scalar.activation(hT[:, e % 2, f, :], h_ps[f % HR][:, 0:2 * P], ACT.Gelu,
                                             bias=b1[:, e, f:f + 1]).then_inc(h_act, 1)

        @block.tensor
        def _(pe):
            pe.wait_ge(w_in, 96)
            with pe.Fori(0, HALF) as i:
                pe.wait_ge(xn_ready, i + 1)
                for c in range(KC):
                    for s in range(2):
                        last = nc.tensor.transpose(tp[:, (2 * c + s) * P:(2 * c + s + 1) * P],
                                                   xn[:, s, c * P:(c + 1) * P], g.ident[:])
                last.then_inc(turned, 1)
                pe.wait_ge(xT_ready, i + 1)
                for s in range(2):
                    for c in range(KC):
                        last = nc.tensor.matmul(gate_ps[:, s * EXPERTS:(s + 1) * EXPERTS], xT[:, c, s * P:(s + 1) * P],
                                                wg[:, c, :], start=(c == 0), stop=(c == KC - 1))
                last.then_inc(gate_ready, 1)

                def up(e):
                    for f in range(HC):
                        pe.wait_ge(h_act, i * EXPERTS * HC + e * HC + f + 1)
                        for c in range(KC):
                            last = nc.tensor.matmul(h_ps[f % HR][:, 0:2 * P], w1[:, e, c, f * P:(f + 1) * P], xT[:, c, :],
                                                    start=(c == 0), stop=(c == KC - 1))
                        last.then_inc(h_ready, 1)

                def down(e):
                    pe.wait_ge(h_act, i * EXPERTS * HC + (e + 1) * HC + HR)
                    pe.wait_ge(res_ready, i * (EXPERTS + 1) + e)
                    for s in range(2):
                        for f in range(HC):
                            last = nc.tensor.matmul(y_ps[e % 2][:, s * D:(s + 1) * D], hT[:, e % 2, f, s * P:(s + 1) * P],
                                                    w2[:, e, f, :], start=(f == 0), stop=(f == HC - 1))
                    last.then_inc(y_ready, 1)

                up(0)
                pe.wait_ge(mask_ready, i + 1)
                for s in range(2):
                    last = nc.tensor.transpose(gate_ps[0:EXPERTS, (2 + s) * P:(3 + s) * P], mask[:, s, :], g.ident[:])
                last.then_inc(maskT_ps, 1)
                up(1)
                pe.wait_ge(maskT_ready, i + 1)
                pe.wait_ge(res_ready, i * (EXPERTS + 1))
                for s in range(2):
                    last = nc.tensor.matmul(y_ps[1][:, s * D:(s + 1) * D], maskT[:, s, :], b2[:], start=True, stop=True)
                last.then_inc(bias_ready, 1)
                down(0)
                for e in range(2, EXPERTS):
                    up(e)
                    down(e - 1)
                down(EXPERTS - 1)


def program(nc, a):
    with ExitStack() as ctx:
        t = Tools(nc, ctx)
        g = Places()
        g.ident = t.sb("ident", [P, P])
        g.iota_row = t.sb("iota_row", [P, P])
        g.ones = t.sb("ones", [1, P])
        g.mv0, g.mv1, g.mv2 = (t.sb(f"mv{n}", [P, 2, WINDOWS]) for n in range(3))
        g.r1 = t.sb("r1", [P, TABLE_WINDOWS * ACC])
        g.acc = g.r1[:, :].rearrange("p (w c) -> p w c", c=ACC)
        g.q = g.r1[:, 0:TABLE_WINDOWS * D].rearrange("p (w d) -> p w d", d=D)
        with ExitStack() as edge_ctx:
            t = Tools(nc, edge_ctx)
            g.rel = t.sb("rel", [P, STEPS_UP])
            g.ew = t.sb("ew", [P, STEPS_UP])
            g.src = t.sb("src", [P, STEPS_UP], i32)
            g.tile_row = t.sb("tile_row", [1, STEPS_UP], i32)
            g.win_row = t.sb("win_row", [1, STEPS_UP + 2], i32)
            g.scores = t.sb("scores", [P, STEPS, HEADS])
            setup_phase(nc, g, a)
            node_phase(nc, g, a)
            score_phase(nc, g, a)
            softmax_phase(nc, g, a)
            gather_phase(nc, g, a)
        attention_out_phase(nc, g, a)
        ffn_phase(nc, g, a)
        mixture_phase(nc, g, a)


class Places:
    pass


def kernel(**inputs):
    import numpy as np
    import concourse.bacc as bacc
    from concourse.bass_utils import run_bass_kernel_spmd

    def get(name):
        return np.ascontiguousarray(inputs[name])

    def padded(rows, n, fill=0):
        out = np.full((n,) + rows.shape[1:], fill, rows.dtype)
        out[:rows.shape[0]] = rows
        return out

    n_edges = EDGE_TILES * P
    dst = padded(get("dst"), n_edges, WINDOWS * P - 1).reshape(EDGE_TILES, P)
    ef = padded(get("edge_attr_64"), n_edges).reshape(EDGE_TILES, P, ED)
    row = lambda name: get("L0_" + name).reshape(1, -1)
    arrays = {
        "x": padded(get("x"), WINDOWS * P),
        "dst_rows": dst,
        "last_dst": np.ascontiguousarray(dst[:, P - 1]).reshape(1, -1),
        "src_rows": padded(get("src"), n_edges).reshape(EDGE_TILES, P),
        "ew_rows": padded(get("edge_weight"), n_edges).reshape(EDGE_TILES, P),
        "ef_t": np.ascontiguousarray(ef.transpose(0, 2, 1)).reshape(EDGE_TILES * ED, P),
        "wqkv": np.concatenate([get("L0_gnn_W" + c) for c in "qkv"], axis=1),
        "bqkv": np.concatenate([row("gnn_b" + c) for c in "qkv"], axis=1),
        "We": get("L0_gnn_We"), "be": row("gnn_be"), "Wo": get("L0_gnn_Wo"), "bo": row("gnn_bo"),
        "ln1_g": row("gnn_ln1_g"), "ln1_b": row("gnn_ln1_b"), "ln2_g": row("gnn_ln2_g"), "ln2_b": row("gnn_ln2_b"),
        "W1": get("L0_gnn_W1"), "b1": row("gnn_b1"), "W2": get("L0_gnn_W2"), "b2": row("gnn_b2"),
        "alpha": row("gnn_alpha"), "beta": row("gnn_beta"),
        "Wg": get("L0_ffn_Wg"), "bg": row("ffn_bg"), "E1": get("L0_ffn_W1"), "eb1": get("L0_ffn_b1"),
        "E2": get("L0_ffn_W2"), "eb2": get("L0_ffn_b2"),
    }
    nc = bacc.Bacc("TRN2", target_bir_lowering=False, num_devices=1)
    a = Places()
    for name, array in arrays.items():
        a.__dict__[name] = nc.dram_tensor("in_" + name, array.shape, mybir.dt.from_np(array.dtype), kind="ExternalInput").ap()
    a.out = nc.dram_tensor("out", (WINDOWS * P, D), fp32, kind="ExternalOutput").ap()
    a.k_d = nc.dram_tensor("k_table", (WINDOWS * P, D), fp32, kind="Internal").ap()
    a.v_d = nc.dram_tensor("v_table", (WINDOWS * P, D), fp32, kind="Internal").ap()
    a.steps_d = nc.dram_tensor("steps_scratch", (2, STEPS_UP), i32, kind="Internal").ap()
    a.keys_d = nc.dram_tensor("keys_scratch", (1, 1 + STEPS_UP * P), fp32, kind="Internal").ap()
    program(nc, a)
    result = run_bass_kernel_spmd(nc, [{"in_" + name: array for name, array in arrays.items()}], core_ids=[0])
    return np.ascontiguousarray(result.results[0]["out"][:NODES])
```

```python
import concourse.bass as bass
from concourse import mybir
from contextlib import ExitStack

fp32 = mybir.dt.float32
bf16 = mybir.dt.bfloat16
i32 = mybir.dt.int32
u32 = mybir.dt.uint32
ALU = mybir.AluOpType
ACT = mybir.ActivationFunctionType
AX = mybir.AxisListType

P = 128
NODES, D, HEADS, DH = 6250, 256, 8, 32
EDGES, ED = 100000, 64
FF, EXPERTS, EH = 1024, 8, 512
EPS = 1e-5
KC = D // P
WINDOWS = 50
EDGE_TILES = (EDGES + P - 1) // P
GROUP = 16
STEPS = (EDGE_TILES + WINDOWS - 1 + GROUP - 1) // GROUP * GROUP
SCOLS = (STEPS + P - 1) // P
STEPS_UP = SCOLS * P
TABLE_WINDOWS = STEPS - EDGE_TILES + 1
CHUNKS = 16
CHUNK_STEPS = STEPS // CHUNKS
CHUNK = CHUNK_STEPS * P
ACC = D + HEADS
TOKEN_WINDOWS = (NODES + P - 1) // P
PAIRS = (2 * TOKEN_WINDOWS * P + EXPERTS * (2 * P - 1)) // (2 * P)
BIG = 1e30
TINY = 1e-30


def bcast(ap, shape):
    return ap.broadcast_to(shape)


class Tools:

    def __init__(self, nc, ctx):
        self.nc, self.ctx = nc, ctx

    def sb(self, name, shape, dt=fp32):
        return self.ctx.enter_context(self.nc.sbuf_tensor(name, shape, dt))

    def ps(self, name, shape, dt=fp32):
        return self.ctx.enter_context(self.nc.psum_tensor(name, shape, dt))

    def sem(self, name):
        return self.ctx.enter_context(self.nc.semaphore(name))


def setup_phase(nc, g, a):
    with ExitStack() as ctx:
        t = Tools(nc, ctx)
        last_i = t.sb("last_i", [P, EDGE_TILES], i32)
        exit_step = t.sb("exit_step", [P, EDGE_TILES])
        iota_tile = t.sb("iota_tile", [P, EDGE_TILES])
        below = t.sb("below", [P, EDGE_TILES])
        iota_p = t.sb("iota_p", [P, 1])
        iota_step = t.sb("iota_step", [P, SCOLS])
        tile_f = t.sb("tile_f", [P, SCOLS])
        win_f = t.sb("win_f", [P, SCOLS])
        win_base = t.sb("win_base", [P, SCOLS])
        tile_i = t.sb("tile_i", [P, SCOLS], i32)
        win_i = t.sb("win_i", [P, SCOLS], i32)
        dst_g = t.sb("dst_g", [P, SCOLS, P], i32)
        src_g = t.sb("src_g", [P, SCOLS, P], i32)
        ew_g = t.sb("ew_g", [P, SCOLS, P])
        rel_g = t.sb("rel_g", [P, SCOLS, P])
        srcf_g = t.sb("srcf_g", [P, SCOLS, P])
        key_g = t.sb("key_g", [P, SCOLS, P])
        ok_g = t.sb("ok_g", [P, SCOLS, P])
        pad = t.sb("pad", [1, 1])
        tp = t.ps("tp", [P, 3, 512])
        loaded, consts, chain = t.sem("su_loaded"), t.sem("su_consts"), t.sem("su_chain")
        gathered, rows_out, rows_in = t.sem("su_gathered"), t.sem("su_rows_out"), t.sem("su_rows_in")
        tiles_known, laid, turned, evac = t.sem("su_tiles"), t.sem("su_laid"), t.sem("su_turned"), t.sem("su_evac")
        keys_out = t.sem("su_keys_out")
        block = ctx.enter_context(nc.Block())

        @block.sync
        def _(sp):
            sp.dma_start(last_i[:], bcast(a.last_dst, [P, EDGE_TILES])).then_inc(loaded, 16)
            sp.wait_ge(tiles_known, 1)
            with nc.allow_non_contiguous_dma(reason="two rows of 896 numbers"):
                sp.dma_start(a.steps_d[0:1, :].rearrange("o (c p) -> p (o c)", p=P), tile_i[:]).then_inc(rows_out, 16)
                sp.dma_start(a.steps_d[1:2, :].rearrange("o (c p) -> p (o c)", p=P), win_i[:]).then_inc(rows_out, 16)
            sp.wait_ge(rows_out, 32)
            sp.dma_start(g.tile_row[:], a.steps_d[0:1, :]).then_inc(rows_in, 16)
            sp.dma_start(g.win_row[0:1, LEAD:], a.steps_d[1:2, :]).then_inc(rows_in, 16)
            sp.wait_ge(laid, 1)
            sp.dma_start(a.keys_d[0:1, 1:1 + STEPS_UP * P].rearrange("o (c p e) -> p (o c) e", p=P, e=P),
                         key_g[:]).then_inc(keys_out, 16)
            sp.dma_start(a.keys_d[0:1, 0:1], pad[:]).then_inc(keys_out, 16)
            sp.wait_ge(keys_out, 32)
            sp.wait_ge(rows_in, 32)

        @block.gpsimd
        def _(pool):
            nc.gpsimd.iota(iota_tile[:], [[1, EDGE_TILES]], base=0, channel_multiplier=0,
                           allow_small_or_imprecise_dtypes=True).then_inc(consts, 1)
            nc.gpsimd.iota(iota_step[:], [[P, SCOLS]], base=0, channel_multiplier=1,
                           allow_small_or_imprecise_dtypes=True).then_inc(consts, 1)
            nc.gpsimd.iota(iota_p[:], [[0, 1]], base=0, channel_multiplier=1,
                           allow_small_or_imprecise_dtypes=True).then_inc(consts, 1)
            nc.gpsimd.iota(g.iota_row[:], [[1, P]], base=0, channel_multiplier=0,
                           allow_small_or_imprecise_dtypes=True).then_inc(consts, 1)
            nc.gpsimd.memset(pad[:], -5.0).then_inc(consts, 1)
            nc.gpsimd.memset(g.ones[:], 1.0).then_inc(consts, 1)
            nc.gpsimd.memset(g.win_row[0:1, 0:LEAD], 0).then_inc(consts, 1)
            pool.wait_ge(tiles_known, 1)
            for c in range(SCOLS):
                for into, rows in ((dst_g, a.dst_rows), (src_g, a.src_rows), (ew_g, a.ew_rows)):
                    nc.gpsimd.indirect_dma_start(
                        out=into[:, c, :], out_offset=None, in_=rows,
                        in_offset=bass.IndirectOffsetOnAxis(ap=tile_i[:, c:c + 1], axis=0)).then_inc(gathered, 16)

        @block.vector
        def _(dve):
            count = [0]

            def link(ins):
                count[0] += 1
                ins.then_inc(chain, 1)
                dve.wait_ge(chain, count[0])

            dve.wait_ge(consts, 7)
            link(nc.vector.tensor_scalar(g.ident[:], g.iota_row[:], iota_p[:], None, ALU.is_equal))
            link(nc.vector.tensor_copy(g.ident_b[:], g.ident[:]))
            dve.wait_ge(loaded, 16)
            link(nc.vector.tensor_scalar(last_i[:], last_i[:], 7, None, ALU.arith_shift_right))
            link(nc.vector.tensor_tensor(exit_step[:], last_i[:], iota_tile[:], ALU.add))
            for c in range(SCOLS):
                link(nc.vector.tensor_scalar(below[:], exit_step[:], iota_step[:, c:c + 1], None,
                                             ALU.is_lt, ALU.add, accum_out=tile_f[:, c:c + 1]))
            link(nc.vector.tensor_scalar(tile_f[:], tile_f[:], float(EDGE_TILES - 1), None, ALU.min))
            link(nc.vector.tensor_tensor(win_f[:], iota_step[:], tile_f[:], ALU.subtract))
            link(nc.vector.tensor_scalar(win_base[:], win_f[:], -float(P), None, ALU.mult))
            link(nc.vector.tensor_copy(win_i[:], win_f[:]))
            nc.vector.tensor_copy(tile_i[:], tile_f[:]).then_inc(tiles_known, 1)
            dve.wait_ge(gathered, 16 * 3 * SCOLS)
            for c in range(SCOLS):
                link(nc.vector.tensor_scalar(rel_g[:, c, :], dst_g[:, c, :], win_base[:, c:c + 1], None, ALU.add))
            link(nc.vector.tensor_scalar(ok_g[:], rel_g[:], 0.0, None, ALU.is_ge))
            link(nc.vector.scalar_tensor_tensor(ok_g[:], rel_g[:], float(P), ok_g[:], ALU.is_lt, ALU.mult))
            link(nc.vector.scalar_tensor_tensor(key_g[:], dst_g[:], 1.0, ok_g[:], ALU.add, ALU.mult))
            nc.vector.tensor_copy(srcf_g[:], src_g[:]).then_inc(laid, 1)
            for c in range(SCOLS):
                dve.wait_ge(turned, 3 * (c + 1))
                cols = slice(c * P, (c + 1) * P)
                nc.vector.tensor_copy(g.rel[:, cols], tp[:, 0, 0:P])
                nc.vector.tensor_copy(g.src[:, cols], tp[:, 1, 0:P])
                nc.vector.tensor_scalar(g.ew[:, cols], tp[:, 2, 0:P], float(DH) ** -0.5, None,
                                        ALU.mult).then_inc(evac, 1)

        @block.tensor
        def _(pe):
            pe.wait_ge(laid, 1)
            for c in range(SCOLS):
                if c:
                    pe.wait_ge(evac, c)
                for n, rows in enumerate((rel_g, srcf_g, ew_g)):
                    nc.tensor.transpose(tp[:, n, 0:P], rows[:, c, :], g.ident[:]).then_inc(turned, 1)


def variances(nc, link, st, tmp, var_ready):
    me, ve, mo, vo = st[:, :, 1], st[:, :, 2], st[:, :, 4], st[:, :, 5]
    s, d, v = tmp[:, 0, :], tmp[:, 1, :], tmp[:, 2, :]
    link(nc.vector.tensor_tensor(s, me, mo, ALU.add))
    link(nc.vector.tensor_tensor(d, me, mo, ALU.subtract))
    link(nc.vector.tensor_tensor(v, ve, vo, ALU.add))
    link(nc.vector.tensor_scalar(v, v, 1.0 / D, EPS, ALU.mult, ALU.add))
    link(nc.vector.tensor_tensor(d, d, d, ALU.mult))
    nc.vector.scalar_tensor_tensor(v, d, 0.25, v, ALU.mult, ALU.add).then_inc(var_ready, 1)


def scales(nc, link, tmp, mv, mv_ready):
    link(nc.vector.reciprocal(mv[:, 0, :], tmp[:, 2, :]))
    nc.vector.scalar_tensor_tensor(mv[:, 1, :], tmp[:, 0, :], -0.5, mv[:, 0, :],
                                   ALU.mult, ALU.mult).then_inc(mv_ready, 1)


def node_phase(nc, g, a):
    HALF = WINDOWS // 2
    PIECES = 5
    PIECE = WINDOWS // PIECES
    with ExitStack() as ctx:
        t = Tools(nc, ctx)
        xs = t.sb("xs", [P, WINDOWS, D])
        st = t.sb("st", [P, WINDOWS, 6])
        tmp = t.sb("tmp", [P, 3, WINDOWS])
        wqkv = t.sb("wqkv", [P, KC, 3 * D])
        bqkv, be = t.sb("bqkv", [P, 3 * D]), t.sb("be", [P, DH])
        g1, b1 = t.sb("g1", [P, KC]), t.sb("b1", [P, KC])
        xn = t.sb("xn", [P, 2, D])
        xT = t.sb("xT", [P, 2, KC, P])
        kv = t.sb("kv", [P, 2, 2 * D])
        q32 = t.sb("q32", [P, 2, D])
        rest = t.sb("rest", [P, 2, D])
        tp = [t.ps(f"tp_a{u}", [P, 512]) for u in range(2)]
        qk_ps = [t.ps(f"qk_ps{u}", [P, 512]) for u in range(2)]
        v_ps = [t.ps(f"v_ps{u}", [P, 512]) for u in range(2)]
        x_in, w_in, chain = [t.sem(f"na_x_in{h}") for h in range(PIECES)], t.sem("na_w_in"), t.sem("na_chain")
        var_ready, root_ready, mv_ready = t.sem("na_var"), t.sem("na_root"), t.sem("na_mv")
        stats, normed, xn_ready = t.sem("na_stats"), t.sem("na_normed"), t.sem("na_xn")
        xn_turned, xT_ready, qkv_taken, q_split = t.sem("na_turned"), t.sem("na_xT"), t.sem("na_taken"), t.sem("na_split")
        qkv_ready, q32_ready, zeroed = t.sem("na_qkv"), t.sem("na_q32"), t.sem("na_zeroed")
        hi_ready, rest_ready, mid_ready = t.sem("na_hi"), t.sem("na_rest"), t.sem("na_mid")
        kv_out = [t.sem("na_kv_out0"), t.sem("na_kv_out1")]
        block = ctx.enter_context(nc.Block())
        k_w = a.k_d.rearrange("(w p) d -> w p d", p=P)
        v_w = a.v_d.rearrange("(w p) d -> w p d", p=P)

        @block.sync
        def _(sp):
            x_w = a.x.rearrange("(w p) d -> p w d", p=P)
            for h in range(PIECES):
                ws = slice(h * PIECE, (h + 1) * PIECE)
                sp.dma_start(xs[:, ws, :], x_w[:, ws, :]).then_inc(x_in[h], 16)
            with nc.allow_non_contiguous_dma(reason="two short vectors"):
                sp.dma_start(g1[:], a.ln1_g.rearrange("o (c p) -> p (o c)", p=P)).then_inc(w_in, 16)
                sp.dma_start(b1[:], a.ln1_b.rearrange("o (c p) -> p (o c)", p=P)).then_inc(w_in, 16)
            sp.dma_start(wqkv[:], a.wqkv.rearrange("(c p) n -> p c n", p=P)).then_inc(w_in, 16)
            sp.dma_start(bqkv[:], bcast(a.bqkv, [P, 3 * D])).then_inc(w_in, 16)
            sp.dma_start(be[:], bcast(a.be, [P, DH])).then_inc(w_in, 16)
            with sp.Fori(0, HALF) as i:
                for u in range(2):
                    w = i * 2 + u
                    sp.wait_ge(qkv_taken, w + 3)
                    sp.dma_start(k_w[bass.ds(w, 1), :, :].rearrange("o p d -> (o p) d"),
                                 kv[:, u, 0:D]).then_inc(kv_out[u], 16)
                    sp.dma_start(v_w[bass.ds(w, 1), :, :].rearrange("o p d -> (o p) d"),
                                 kv[:, u, D:2 * D]).then_inc(kv_out[u], 16)
            for u in range(2):
                sp.wait_ge(kv_out[u], 32 * HALF + 32)

        @block.gpsimd
        def _(pool):
            for part in g.q:
                nc.gpsimd.memset(part[:, WINDOWS:, :], 0.0).then_inc(zeroed, 1)
            pool.sem_inc(q_split, 2)
            with pool.Fori(0, HALF) as i:
                for u in range(2):
                    w = i * 2 + u
                    hi, mid, lo = (part[:, bass.ds(w, 1), :].rearrange("p o d -> p (o d)") for part in g.q)
                    pool.wait_ge(hi_ready, w + 1)
                    nc.gpsimd.tensor_tensor(rest[:, u, :], q32[:, u, :], hi, ALU.subtract).then_inc(rest_ready, 1)
                    pool.wait_ge(mid_ready, w + 1)
                    nc.gpsimd.tensor_tensor(lo, rest[:, u, :], mid, ALU.subtract).then_inc(q_split, 1)
            pool.wait_ge(zeroed, 3)

        @block.vector
        def _(dve):
            count = [0]

            def link(ins):
                count[0] += 1
                ins.then_inc(chain, 1)
                dve.wait_ge(chain, count[0])

            for h in range(PIECES):
                dve.wait_ge(x_in[h], 16)
                with dve.Fori(0, 2) as i:
                    for n in range(PIECE // 2):
                        w = i * (PIECE // 2) + h * PIECE + n
                        nc.vector.bn_stats(st[:, bass.ds(w, 1), :], xs[:, bass.ds(w, 1), :]).then_inc(stats, 1)
            dve.wait_ge(stats, WINDOWS)
            variances(nc, link, st, tmp, var_ready)
            dve.wait_ge(root_ready, 1)
            scales(nc, link, tmp, g.mv0, mv_ready)
            with dve.Fori(0, HALF) as i:
                for u in range(2):
                    w = i * 2 + u
                    dve.wait_ge(normed, w + 1)
                    nc.vector.bn_stats(st[:, bass.ds(w, 1), :], xs[:, bass.ds(w, 1), :]).then_inc(stats, 1)
            dve.wait_ge(stats, 2 * WINDOWS)
            variances(nc, link, st, tmp, var_ready)
            dve.wait_ge(root_ready, 2)
            scales(nc, link, tmp, g.mv1, mv_ready)
            dve.wait_ge(w_in, 80)
            k_bias = bqkv[:, D:2 * D].rearrange("p (h d) -> p h d", d=DH)
            link(nc.vector.tensor_tensor(k_bias, k_bias, bcast(be[:, None, :], [P, HEADS, DH]), ALU.add))
            dve.sem_inc(xT_ready, 2)
            dve.sem_inc(qkv_taken, 2)

            def gain(w, u):
                dve.wait_ge(xn_turned, w + 3)
                dve.wait_ge(qkv_ready, w)
                for c in range(KC):
                    last = nc.vector.tensor_scalar(xT[:, u % 2, c, :], tp[u % 2][:, c * P:(c + 1) * P],
                                                   g1[:, c:c + 1], b1[:, c:c + 1], ALU.mult, ALU.add)
                last.then_inc(xT_ready, 1)

            def trip(i, last_trip):
                for u in range(2):
                    w = i * 2 + u
                    if not (last_trip and u):
                        gain(w + 1, u + 1)
                    dve.wait_ge(qkv_ready, w + 2)
                    dve.wait_ge(q_split, w + 1)
                    nc.vector.tensor_tensor(q32[:, u, :], qk_ps[u][:, 0:D], bqkv[:, 0:D], ALU.add).then_inc(q32_ready, 1)
                    dve.wait_ge(kv_out[u], i * 32 + 32)
                    nc.vector.tensor_tensor(kv[:, u, 0:D], qk_ps[u][:, D:2 * D], bqkv[:, D:2 * D], ALU.add)
                    nc.vector.tensor_tensor(kv[:, u, D:2 * D], v_ps[u][:, 0:D], bqkv[:, 2 * D:3 * D],
                                            ALU.add).then_inc(qkv_taken, 1)

            for u in range(2):
                dve.sem_inc(kv_out[u], 32)
            gain(0, 0)
            with dve.Fori(0, HALF - 1) as i:
                trip(i, False)
            trip(HALF - 1, True)

        @block.scalar
        def _(act):
            act.wait_ge(var_ready, 1)
            nc.scalar.activation(tmp[:, 2, :], tmp[:, 2, :], ACT.Sqrt).then_inc(root_ready, 1)
            act.wait_ge(mv_ready, 1)
            with act.Fori(0, HALF) as i:
                for u in range(2):
                    w = i * 2 + u
                    nc.scalar.activation(xs[:, bass.ds(w, 1), :], xs[:, bass.ds(w, 1), :], ACT.Identity,
                                         bias=g.mv0[:, 1, bass.ds(w, 1)],
                                         scale=g.mv0[:, 0, bass.ds(w, 1)]).then_inc(normed, 1)
            act.wait_ge(var_ready, 2)
            nc.scalar.activation(tmp[:, 2, :], tmp[:, 2, :], ACT.Sqrt).then_inc(root_ready, 1)
            act.wait_ge(mv_ready, 2)

            def norm(w, u):
                act.wait_ge(xn_turned, w + 1)
                nc.scalar.activation(xn[:, u:u + 1, :], xs[:, bass.ds(w, 1), :], ACT.Identity,
                                     bias=g.mv1[:, 1, bass.ds(w, 1)],
                                     scale=g.mv1[:, 0, bass.ds(w, 1)]).then_inc(xn_ready, 1)

            def trip(i, last_trip):
                for u in range(2):
                    w = i * 2 + u
                    if not last_trip:
                        norm(w + 2, u)
                    act.wait_ge(q32_ready, w + 1)
                    nc.scalar.copy(g.q[0][:, bass.ds(w, 1), :], q32[:, u:u + 1, :]).then_inc(hi_ready, 1)
                    act.wait_ge(rest_ready, w + 1)
                    nc.scalar.copy(g.q[1][:, bass.ds(w, 1), :], rest[:, u:u + 1, :]).then_inc(mid_ready, 1)

            for w in range(2):
                norm(w, w)
            with act.Fori(0, HALF - 1) as i:
                trip(i, False)
            trip(HALF - 1, True)

        @block.tensor
        def _(pe):
            def turn(w, u):
                pe.wait_ge(xn_ready, w + 1)
                pe.wait_ge(xT_ready, w + 1)
                for c in range(KC):
                    last = nc.tensor.transpose(tp[u % 2][:, c * P:(c + 1) * P], xn[:, u % 2, c * P:(c + 1) * P], g.ident[:])
                last.then_inc(xn_turned, 1)

            def trip(i, last_trip):
                for u in range(2):
                    w = i * 2 + u
                    if not (last_trip and u):
                        turn(w + 1, u + 1)
                    pe.wait_ge(xT_ready, w + 3)
                    pe.wait_ge(qkv_taken, w + 1)
                    for c in range(KC):
                        nc.tensor.matmul(qk_ps[u][:], xT[:, u, c, :], wqkv[:, c, 0:2 * D], start=(c == 0), stop=(c == KC - 1))
                    for c in range(KC):
                        last = nc.tensor.matmul(v_ps[u][:, 0:D], xT[:, u, c, :], wqkv[:, c, 2 * D:3 * D],
                                                start=(c == 0), stop=(c == KC - 1))
                    last.then_inc(qkv_ready, 1)

            pe.sem_inc(xn_turned, 2)
            pe.sem_inc(qkv_ready, 1)
            pe.wait_ge(w_in, 80)
            turn(0, 0)
            with pe.Fori(0, HALF - 1) as i:
                trip(i, False)
            trip(HALF - 1, True)


UNIT = 4
UNITS = STEPS // UNIT
BODY = 4
TRIPS = UNITS // BODY
LEAD = UNIT


def gather_rows(nc, pool, table, rows, rows_in, staged, stage, carried):
    with pool.Fori(0, TRIPS) as i:
        for p in range(BODY):
            pool.wait_ge(staged, i * BODY + p + 1)
            pool.sem_inc(carried, 1)
            for s in range(UNIT):
                nc.gpsimd.indirect_dma_start(
                    out=rows[:, p, s, 0:D], out_offset=None, in_=table,
                    in_offset=bass.IndirectOffsetOnAxis(ap=stage[:, p, s:s + 1], axis=0)).then_inc(rows_in[p], 16)


def rows_landed(eng, rows_in, i, p):
    eng.wait_ge(rows_in[p], i * (16 * UNIT) + 16 * UNIT)


def values_of(nc, row, engine, first, count, most):
    _, values = nc.values_load_multi_w_load_instructions(
        row[0:1, bass.ds(first, count)], engines=[engine], min_val=0, max_val=most,
        skip_runtime_bounds_check_because="each row is worked out on the chip within these bounds, whatever the data is")
    return values


def score_phase(nc, g, a):
    with ExitStack() as ctx:
        t = Tools(nc, ctx)
        k = t.sb("k_rows", [P, BODY, UNIT, D])
        stage = t.sb("k_stage", [P, BODY, UNIT], i32)
        ef = t.sb("ef", [ED, BODY, UNIT, P])
        we = t.sb("we", [ED, DH])
        onehot = t.sb("onehot", [P, BODY, UNIT, P], bf16)
        onehotT = t.sb("onehotT", [P, 2, UNIT, P], bf16)
        turn_ps = [t.ps(f"turn_ps{u}", [P, 1024], bf16) for u in range(2)]
        ep_ps = [t.ps(f"ep_ps{u}", [P, 512]) for u in range(2)]
        q_ps = [t.ps(f"q_ps{u}", [P, 1024]) for u in range(2)]
        k_in = [t.sem(f"sc_k_in{r}") for r in range(BODY)]
        ef_in = [t.sem(f"sc_ef_in{r}") for r in range(BODY)]
        k_free, ef_free, turned = t.sem("sc_k_free"), t.sem("sc_ef_free"), t.sem("sc_turned")
        ep_used, q_used, turn_copied, onehotT_used = (t.sem("sc_ep_used"), t.sem("sc_q_used"),
                                                      t.sem("sc_copied"), t.sem("sc_oT_used"))
        staged, selected, w_in = t.sem("sc_staged"), t.sem("sc_selected"), t.sem("sc_w_in")
        block = ctx.enter_context(nc.Block())
        ef_t = a.ef_t.rearrange("(t d) e -> t d e", d=ED)

        def load_edges(eng, name, n, p, first):
            eng.wait_ge(ef_free, n + 1)
            tiles = values_of(nc, g.tile_row, name, n * UNIT + first, 2, EDGE_TILES - 1)
            for s, tile in enumerate(tiles):
                eng.dma_start(ef[:, p % BODY, first + s, :],
                              ef_t[bass.ds(tile, 1), :, :].rearrange("o d e -> (o d) e")).then_inc(ef_in[p % BODY], 16)

        @block.sync
        def _(sp):
            sp.dma_start(we[:], a.We).then_inc(w_in, 16)
            with sp.Fori(0, TRIPS) as i:
                for p in range(BODY):
                    load_edges(sp, mybir.EngineType.SP, i * BODY + p, p, 0)

        @block.gpsimd
        def _(pool):
            gather_rows(nc, pool, a.k_d, k, k_in, staged, stage, g.carried)

        @block.vector
        def _(dve):
            def select(n, slot):
                nc.vector.tensor_tensor(onehot[:, slot % BODY, :, :], bcast(g.iota_row[:, None, :], [P, UNIT, P]),
                                        bcast(g.rel[:, bass.ds(n * UNIT, UNIT)][:, :, None], [P, UNIT, P]),
                                        ALU.is_equal).then_inc(selected, 1)

            dve.sem_inc(k_free, BODY)
            dve.sem_inc(ep_used, 2)
            dve.sem_inc(q_used, 2)

            def add_edges(i, n, slot):
                rows = k[:, slot % BODY, :, :].rearrange("p s (h d) -> p s h d", d=DH)
                ep = ep_ps[slot % 2][:, 0:UNIT * DH].rearrange("p (s d) -> p s d", s=UNIT)[:, :, None, :]
                rows_landed(dve, k_in, i + slot // BODY, slot % BODY)
                dve.wait_ge(ef_free, n + 1 + BODY)
                nc.vector.tensor_tensor(rows, rows, bcast(ep, [P, UNIT, HEADS, DH]), ALU.add).then_inc(ep_used, 1)

            def times_q(n, slot):
                flat = k[:, slot % BODY, :, :].rearrange("p s c -> p (s c)")
                dve.wait_ge(ep_used, n + 3)
                dve.wait_ge(onehotT_used, n + 3)
                nc.vector.tensor_tensor(flat, flat, q_ps[slot % 2][:], ALU.mult).then_inc(q_used, 1)

            def select_ahead(n, slot):
                dve.wait_ge(turned, n + BODY)
                select(n + 3, slot + 3)

            def sum_heads(n, slot):
                dve.wait_ge(q_used, n + 3)
                nc.vector.tensor_reduce(out=g.scores[:, bass.ds(n * UNIT, UNIT), :],
                                        in_=k[:, slot % BODY, :, :].rearrange("p s (h d) -> p s h d", d=DH),
                                        op=ALU.add, axis=AX.X).then_inc(k_free, 1)

            def trip(i, last_trip):
                for p in range(BODY):
                    n = i * BODY + p
                    more = not (last_trip and p == BODY - 1)
                    if more:
                        add_edges(i, n + 1, p + 1)
                    sum_heads(n, p)
                    if more:
                        times_q(n + 1, p + 1)
                        select_ahead(n + 1, p + 1)

            for n in range(3):
                select(n, n)
            add_edges(0, 0, 0)
            times_q(0, 0)
            select_ahead(0, 0)
            with dve.Fori(0, TRIPS - 1) as i:
                trip(i, False)
            trip(TRIPS - 1, True)

        @block.scalar
        def _(act):
            def copy_turned(n, slot):
                act.wait_ge(turned, n + 1 + BODY)
                act.wait_ge(onehotT_used, n + 1)
                nc.scalar.copy(onehotT[:, slot % 2, :, :].rearrange("p s m -> p (s m)"),
                               turn_ps[slot % 2][:, 0:UNIT * P]).then_inc(turn_copied, 1)

            def stage_rows(n, slot):
                act.wait_ge(k_free, n + 1)
                nc.scalar.copy(stage[:, slot % BODY, :], g.src[:, bass.ds(n * UNIT, UNIT)]).then_inc(staged, 1)

            def trip(i, last_trip):
                for p in range(BODY):
                    n = i * BODY + p
                    copy_turned(n + 1, p + 1)
                    if not (last_trip and p >= BODY - 3):
                        stage_rows(n + 3, p + 3)
                        load_edges(act, mybir.EngineType.Activation, n + 3, p + 3, 2)

            act.sem_inc(turn_copied, 2)
            for n in range(3):
                stage_rows(n, n)
                load_edges(act, mybir.EngineType.Activation, n, n, 2)
            copy_turned(0, 0)
            with act.Fori(0, TRIPS - 1) as i:
                trip(i, False)
            trip(TRIPS - 1, True)

        @block.tensor
        def _(pe):
            def turn(n, slot):
                pe.wait_ge(selected, n + 1)
                pe.wait_ge(turn_copied, n + 1)
                for s in range(UNIT):
                    last = nc.tensor.transpose(turn_ps[slot % 2][:, s * P:(s + 1) * P], onehot[:, slot % BODY, s, :], g.ident_b[:])
                last.then_inc(turned, 1)

            def project(i, n, slot):
                pe.wait_ge(ef_in[slot % BODY], (i + slot // BODY) * (16 * UNIT) + 16 * UNIT)
                pe.wait_ge(ep_used, n + 1)
                for s in range(UNIT):
                    last = nc.tensor.matmul(ep_ps[slot % 2][:, s * DH:(s + 1) * DH], ef[:, slot % BODY, s, :], we[:],
                                            start=True, stop=True)
                last.then_inc(ef_free, 1)

            def trip(i, last_trip):
                for p in range(BODY):
                    n = i * BODY + p
                    if p % 2 == 0:
                        wins = values_of(nc, g.win_row, mybir.EngineType.PE, n * UNIT + LEAD, 2 * UNIT, TABLE_WINDOWS - 1)
                    turn(n + 1, p + 1)
                    if not (last_trip and p == BODY - 1):
                        project(i, n + 1, p + 1)
                    pe.wait_ge(turn_copied, n + 3)
                    pe.wait_ge(q_used, n + 1)
                    for s in range(UNIT):
                        win = wins[UNIT * (p % 2) + s]
                        for part in range(3):
                            last = nc.tensor.matmul(q_ps[p % 2][:, s * D:(s + 1) * D], onehotT[:, p % 2, s, :],
                                                    g.q[part][:, bass.ds(win, 1), :].rearrange("p o d -> p (o d)"),
                                                    start=(part == 0), stop=(part == 2))
                    last.then_inc(onehotT_used, 1)

            pe.sem_inc(ef_free, BODY)
            pe.sem_inc(turned, BODY)
            pe.sem_inc(onehotT_used, 2)
            pe.wait_ge(w_in, 16)
            turn(0, 0)
            project(0, 0, 0)
            with pe.Fori(0, TRIPS - 1) as i:
                trip(i, False)
            trip(TRIPS - 1, True)


def softmax_phase(nc, g, a):
    with ExitStack() as ctx:
        t = Tools(nc, ctx)
        gap = t.sb("gap", [P, CHUNK + 1])
        sT = t.sb("sT", [P, CHUNK_STEPS, P])
        fwd = g.r1[:, 0:CHUNK]
        bwd = g.r1[:, CHUNK:2 * CHUNK]
        ends = t.sb("ends", [P, 4])
        row = t.sb("row", [1, 2, P])
        enter = t.sb("enter", [1, HEADS, CHUNKS])
        swept = t.sb("swept", [1, HEADS, CHUNKS])
        shifted = t.sb("shifted", [1, P])
        carry = t.sb("carry", [P, 2])
        zeros = t.sb("zeros", [P, D])
        tps = [t.ps(f"mx_ps{u}", [P, 512]) for u in range(2)]
        row_ps = t.ps("row_ps", [P, 512])
        zeroed, slots_cleared = t.sem("mx_zeroed"), t.sem("mx_cleared")
        keys_in, gap_ready, chain = t.sem("mx_keys"), t.sem("mx_gap"), t.sem("mx_chain")
        weighted, turned, taken = t.sem("mx_weighted"), t.sem("mx_turned"), t.sem("mx_taken")
        ends_ready, row_ready, shift_ready, carry_ready = (t.sem("mx_ends"), t.sem("mx_row"),
                                                           t.sem("mx_shift"), t.sem("mx_carry"))
        max_ready, exp_ready, back, back_taken = t.sem("mx_max"), t.sem("mx_exp"), t.sem("mx_back"), t.sem("mx_back_t")
        block = ctx.enter_context(nc.Block())
        sT_flat = sT[:, :, :].rearrange("p j e -> p (j e)")
        by_chunk = g.scores[:, :, :].rearrange("p (c j) h -> p c j h", j=CHUNK_STEPS)
        in_turn = g.r1[:, 0:CHUNK].rearrange("p (j c h) -> p j c h", c=CHUNKS, h=HEADS)
        BATCHES = CHUNK_STEPS // 4

        @block.gpsimd
        def _(pool):
            nc.gpsimd.memset(zeros[:], 0.0).then_inc(zeroed, 1)

        @block.sync
        def _(sp):
            for c in range(CHUNKS):
                sp.dma_start(gap[c * HEADS:(c + 1) * HEADS, :],
                             bcast(a.keys_d[0:1, c * CHUNK:c * CHUNK + CHUNK + 1], [HEADS, CHUNK + 1])).then_inc(keys_in, 16)
            sp.wait_ge(zeroed, 1)
            sp.dma_start(a.slots_d.rearrange("(b p) d -> p b d", p=P),
                         bcast(zeros[:, None, :], [P, 2 * PAIRS, D])).then_inc(slots_cleared, 16)
            sp.wait_ge(slots_cleared, 16)

        @block.vector
        def _(dve):
            count = [0]

            def link(ins):
                count[0] += 1
                ins.then_inc(chain, 1)
                dve.wait_ge(chain, count[0])

            dve.wait_ge(keys_in, 16 * CHUNKS)
            ew = g.ew[:, 0:STEPS].rearrange("p (c j) -> p c j", j=CHUNK_STEPS)[:, :, :, None]
            for c in range(CHUNKS):
                nc.vector.tensor_tensor(in_turn[:, :, c, :], by_chunk[:, c, :, :],
                                        bcast(ew[:, c, :, :], [P, CHUNK_STEPS, HEADS]), ALU.mult).then_inc(weighted, 1)
            link(nc.vector.tensor_tensor(bwd[:], gap[:, 1:], gap[:, 0:CHUNK], ALU.not_equal))
            link(nc.vector.tensor_scalar(gap[:, 0:CHUNK], bwd[:], -BIG, None, ALU.mult))
            for b in range(BATCHES):
                dve.wait_ge(turned, b + 1)
                nc.vector.tensor_copy(sT_flat[:, b * 512:(b + 1) * 512], tps[b % 2][:]).then_inc(taken, 1)
            dve.wait_ge(taken, BATCHES)

            def sweep(turn, gaps, data, out, last, step):
                def way(ap):
                    return ap[:, ::step] if step < 0 else ap
                link(nc.vector.tensor_tensor_scan(way(out), way(gaps), way(data), -BIG, ALU.add, ALU.max))
                link(nc.vector.tensor_copy(ends[:, 0:1], out[:, last:last + 1]))
                nc.vector.tensor_reduce(out=ends[:, 1:2], in_=gaps, op=ALU.min, axis=AX.X).then_inc(ends_ready, 1)
                dve.wait_ge(row_ready, turn + 1)
                ps = row_ps[0:1, 0:2 * P].rearrange("o (n c h) -> o n h c", n=2, h=HEADS)
                link(nc.vector.tensor_copy(enter[:], ps[:, 0, :, :]))
                link(nc.vector.tensor_copy(swept[:], ps[:, 1, :, :]))
                edge = 0 if step > 0 else CHUNKS - 1
                link(nc.vector.memset(swept[:, :, edge:edge + 1], -BIG))
                e, s = enter[:].rearrange("o h c -> o (h c)"), swept[:].rearrange("o h c -> o (h c)")
                link(nc.vector.tensor_tensor_scan(way(e), way(s), way(e), -BIG, ALU.add, ALU.max))
                link(nc.vector.memset(shifted[:], -BIG))
                sh = shifted[:].rearrange("o (c h) -> o h c", h=HEADS)
                if step > 0:
                    cp = nc.vector.tensor_copy(sh[:, :, 1:], enter[:, :, 0:CHUNKS - 1])
                else:
                    cp = nc.vector.tensor_copy(sh[:, :, 0:CHUNKS - 1], enter[:, :, 1:])
                cp.then_inc(shift_ready, 1)
                dve.wait_ge(carry_ready, turn + 1)
                link(nc.vector.tensor_copy(carry[:, turn:turn + 1], row_ps[:, 256:257]))
                link(nc.vector.tensor_tensor_scan(way(out), way(gaps), way(data), carry[:, turn:turn + 1],
                                                  ALU.add, ALU.max))

            link(nc.vector.memset(gap[:, CHUNK:], -BIG))
            sweep(0, gap[:, 0:CHUNK], sT_flat[:], fwd[:], CHUNK - 1, 1)
            dve.wait_ge(gap_ready, 16)
            sweep(1, gap[:, 1:CHUNK + 1], fwd[:], bwd[:], 0, -1)
            link(nc.vector.tensor_tensor(sT_flat[:], sT_flat[:], bwd[:], ALU.subtract))
            nc.vector.engine_nop().then_inc(max_ready, 1)
            for b in range(BATCHES):
                dve.wait_ge(back, b + 1)
                nc.vector.tensor_copy(by_chunk[:, :, 4 * b:4 * b + 4, :].rearrange("p c j h -> p j c h"),
                                      tps[b % 2][:].rearrange("p (j c h) -> p j c h", j=4, h=HEADS)).then_inc(back_taken, 1)
            dve.wait_ge(back_taken, BATCHES)

        @block.scalar
        def _(act):
            act.wait_ge(ends_ready, 1)
            act.dma_start(gap[0:P - HEADS, CHUNK:CHUNK + 1], gap[HEADS:P, 0:1]).then_inc(gap_ready, 16)
            for b in range(BATCHES):
                if b == 0:
                    act.wait_ge(max_ready, 1)
                nc.scalar.activation(sT_flat[:, b * 512:(b + 1) * 512], sT_flat[:, b * 512:(b + 1) * 512],
                                     ACT.Exp).then_inc(exp_ready, 1)

        @block.tensor
        def _(pe):
            pe.wait_ge(weighted, CHUNKS)
            for b in range(BATCHES):
                if b >= 2:
                    pe.wait_ge(taken, b - 1)
                for j in range(4):
                    last = nc.tensor.transpose(tps[b % 2][:, j * P:(j + 1) * P], in_turn[:, 4 * b + j, :, :].rearrange("p c h -> p (c h)"), g.ident[:])
                last.then_inc(turned, 1)
            for turn in range(2):
                pe.wait_ge(ends_ready, turn + 1)
                for n in range(2):
                    last = nc.tensor.matmul(row_ps[0:1, n * P:(n + 1) * P], ends[:, n:n + 1], g.ident[:], start=True, stop=True)
                last.then_inc(row_ready, 1)
                pe.wait_ge(shift_ready, turn + 1)
                nc.tensor.matmul(row_ps[:, 256:257], shifted[0:1, :], g.ones[0:1, 0:1], start=True, stop=True).then_inc(carry_ready, 1)
            for b in range(BATCHES):
                pe.wait_ge(exp_ready, b + 1)
                if b >= 2:
                    pe.wait_ge(back_taken, b - 1)
                for j in range(4):
                    last = nc.tensor.transpose(tps[b % 2][:, j * P:(j + 1) * P], sT[:, 4 * b + j, :], g.ident[:])
                last.then_inc(back, 1)


def gather_phase(nc, g, a):
    with ExitStack() as ctx:
        t = Tools(nc, ctx)
        v = t.sb("v_rows", [P, BODY, UNIT, ACC])
        stage = t.sb("v_stage", [P, BODY, UNIT], i32)
        onehot = t.sb("onehot_v", [P, 2, UNIT, P])
        sum_ps = [[t.ps(f"sum_ps{u}{s}", [P, 512]) for s in range(UNIT)] for u in range(2)]
        v_in = [t.sem(f"ag_v_in{r}") for r in range(BODY)]
        staged, selected, weighted = t.sem("ag_staged"), t.sem("ag_selected"), t.sem("ag_weighted")
        zeroed, exp_in = t.sem("ag_zeroed"), t.sem("ag_exp_in")
        PARTS = UNIT - 1
        HALF_UNIT = UNIT // 2
        summed, added, part_added = t.sem("ag_summed"), t.sem("ag_added"), t.sem("ag_part")
        block = ctx.enter_context(nc.Block())

        @block.gpsimd
        def _(pool):
            gather_rows(nc, pool, a.v_d, v, v_in, staged, stage, g.carried)

        @block.scalar
        def _(act):
            with act.Fori(0, TRIPS) as i:
                for p in range(BODY):
                    n = i * BODY + p
                    act.wait_ge(summed, n + 2)
                    nc.scalar.copy(stage[:, p, :], g.src[:, bass.ds(n * UNIT, UNIT)]).then_inc(staged, 1)
                    nc.scalar.copy(v[:, p, :, D:ACC], g.scores[:, bass.ds(n * UNIT, UNIT), :]).then_inc(exp_in, 1)

        @block.vector
        def _(dve):
            def select(n, slot):
                nc.vector.tensor_tensor(onehot[:, slot % 2, :, :], bcast(g.iota_row[:, None, :], [P, UNIT, P]),
                                        bcast(g.rel[:, bass.ds(n * UNIT, UNIT)][:, :, None], [P, UNIT, P]),
                                        ALU.is_equal).then_inc(selected, 1)

            def weigh(n, p, half):
                steps = slice(half * HALF_UNIT, (half + 1) * HALF_UNIT)
                rows = v[:, p, steps, 0:D].rearrange("p s (h d) -> p s h d", d=DH)
                ex = g.scores[:, bass.ds(n * UNIT + half * HALF_UNIT, HALF_UNIT), :][:, :, :, None]
                nc.vector.tensor_tensor(rows, rows, bcast(ex, [P, HALF_UNIT, HEADS, DH]), ALU.mult).then_inc(weighted, 1)

            def add(n, slot, s, win):
                into = g.acc[:, bass.ds(win, 1), :].rearrange("p o c -> p (o c)")
                if s:
                    dve.wait_ge(part_added, n * PARTS + 4 * PARTS + s)
                else:
                    dve.wait_ge(added, n + 2)
                return nc.vector.tensor_tensor(into, into, sum_ps[slot % 2][s][:, 0:ACC],
                                               ALU.add).then_inc(added if s == PARTS else part_added, 1)

            nc.vector.memset(g.acc[:], 0.0).then_inc(zeroed, 1)
            for s in range(UNIT):
                nc.vector.memset(sum_ps[1][s][:, 0:ACC], 0.0).then_inc(zeroed, 1)
            dve.sem_inc(added, 1)
            dve.sem_inc(selected, 2)
            dve.sem_inc(part_added, 3 * PARTS)
            dve.wait_ge(zeroed, 1 + UNIT)
            select(0, 0)
            with dve.Fori(0, TRIPS) as i:
                for p in range(BODY):
                    n = i * BODY + p
                    rows_landed(dve, v_in, i, p)
                    weigh(n, p, 0)
                    if p % 2 == 0:
                        wins = values_of(nc, g.win_row, mybir.EngineType.DVE, n * UNIT, 2 * UNIT, TABLE_WINDOWS - 1)
                    win = wins[UNIT * (p % 2):UNIT * (p % 2) + UNIT]
                    dve.wait_ge(summed, n + 1 + BODY)
                    add(n - 1, p - 1, 0, win[0])
                    weigh(n, p, 1)
                    add(n - 1, p - 1, 1, win[1])
                    select(n + 1, p + 1)
                    add(n - 1, p - 1, 2, win[2])
                    add(n - 1, p - 1, 3, win[3])
            dve.wait_ge(summed, UNITS + 1 + BODY)
            for s in range(UNIT):
                win = dve.value_load(g.win_row[0:1, UNITS * UNIT + s:UNITS * UNIT + s + 1], min_val=0, max_val=TABLE_WINDOWS - 1)
                add(UNITS - 1, UNITS - 1, s, win)
            dve.wait_ge(added, UNITS + 2)

        @block.tensor
        def _(pe):
            pe.sem_inc(summed, 1 + BODY)
            with pe.Fori(0, TRIPS) as i:
                for p in range(BODY):
                    n = i * BODY + p
                    pe.wait_ge(selected, n + 3)
                    pe.wait_ge(exp_in, n + 1)
                    pe.wait_ge(added, n + 1)
                    for s in range(UNIT):
                        if s % HALF_UNIT == 0:
                            pe.wait_ge(weighted, n * 2 + s // HALF_UNIT + 1)
                        last = nc.tensor.matmul(sum_ps[p % 2][s][:, 0:ACC], onehot[:, p % 2, s, :], v[:, p, s, :],
                                                start=True, stop=True)
                    last.then_inc(summed, 1)


def attention_out_phase(nc, g, a):
    HALF = WINDOWS // 2
    with ExitStack() as ctx:
        t = Tools(nc, ctx)
        xs = t.sb("xs_o", [P, 2, D])
        h0 = t.sb("h0", [P, 2, D])
        rs = t.sb("rs", [P, WINDOWS, HEADS])
        attn = t.sb("attn", [P, 2, D])
        attnT = t.sb("attnT", [P, 2, D])
        proj = t.sb("proj", [P, 2, D])
        wo, bo, alpha = t.sb("wo", [P, KC, D]), t.sb("bo", [P, D]), t.sb("alpha", [P, 1])
        st, tmp = t.sb("st_o", [P, WINDOWS, 6]), t.sb("tmp_o", [P, 3, WINDOWS])
        tp = [t.ps(f"tp_o{u}", [P, 512]) for u in range(2)]
        ps = [t.ps(f"ps_o{u}", [P, 512]) for u in range(2)]
        w_in, x_in = t.sem("ao_w_in"), [t.sem("ao_x_in0"), t.sem("ao_x_in1")]
        chain, attn_ready, turned, attnT_ready = (t.sem("ao_chain"), t.sem("ao_attn"),
                                                            t.sem("ao_turned"), t.sem("ao_attnT"))
        h0_ready, proj_ready, proj_chain, x1_ready, stats = (t.sem("ao_h0"), t.sem("ao_proj"), t.sem("ao_pch"),
                                                             t.sem("ao_x1"), t.sem("ao_stats"))
        var_ready, root_ready, mv_ready = t.sem("ao_var"), t.sem("ao_root"), t.sem("ao_mv")
        block = ctx.enter_context(nc.Block())
        x_w = a.x.rearrange("(w p) d -> w p d", p=P)

        @block.sync
        def _(sp):
            sp.dma_start(wo[:], a.Wo.rearrange("(c p) n -> p c n", p=P)).then_inc(w_in, 16)
            sp.dma_start(bo[:], bcast(a.bo, [P, D])).then_inc(w_in, 16)
            sp.dma_start(alpha[:], bcast(a.alpha, [P, 1])).then_inc(w_in, 16)
            sp.sem_inc(h0_ready, 2)
            with sp.Fori(0, HALF) as i:
                for u in range(2):
                    w = i * 2 + u
                    sp.wait_ge(h0_ready, w + 1)
                    sp.dma_start(xs[:, u, :], x_w[bass.ds(w, 1), :, :].rearrange("o p d -> (o p) d")).then_inc(x_in[u], 16)

        @block.vector
        def _(dve):
            count = [0]

            def link(ins):
                count[0] += 1
                ins.then_inc(chain, 1)
                dve.wait_ge(chain, count[0])

            def divide(w, u):
                o = g.acc[:, bass.ds(w, 1), 0:D].rearrange("p o (h d) -> p (o h) d", d=DH)
                nc.vector.tensor_tensor(attn[:, u, :].rearrange("p (h d) -> p h d", d=DH), o,
                                        bcast(rs[:, bass.ds(w, 1), :].rearrange("p o h -> p (o h)")[:, :, None],
                                              [P, HEADS, DH]), ALU.mult).then_inc(attn_ready, 1)

            def trip(i, last_trip):
                for u in range(2):
                    w = i * 2 + u
                    if not last_trip:
                        dve.wait_ge(turned, w + 1)
                        divide(w + 2, u)
                    dve.wait_ge(proj_ready, w + 1)
                    nc.vector.tensor_tensor(proj[:, u, :], ps[u][:, 0:D], bo[:], ALU.add).then_inc(proj_chain, 1)
                    dve.wait_ge(proj_chain, w + 1)
                    dve.wait_ge(h0_ready, w + 3)
                    x1 = g.acc[:, bass.ds(w, 1), 0:D].rearrange("p o d -> p (o d)")
                    nc.vector.scalar_tensor_tensor(x1, proj[:, u, :], alpha[:], h0[:, u, :],
                                                   ALU.mult, ALU.add).then_inc(x1_ready, 1)
                    dve.wait_ge(x1_ready, w + 3)
                    nc.vector.bn_stats(st[:, bass.ds(w, 1), :], g.acc[:, bass.ds(w, 1), 0:D]).then_inc(stats, 1)

            dve.sem_inc(x1_ready, 2)
            dve.wait_ge(w_in, 48)
            link(nc.vector.tensor_scalar(rs[:], g.acc[:, 0:WINDOWS, D:ACC], TINY, None, ALU.max))
            link(nc.vector.reciprocal(rs[:], rs[:]))
            for w in range(2):
                divide(w, w)
            with dve.Fori(0, HALF - 1) as i:
                trip(i, False)
            trip(HALF - 1, True)
            dve.wait_ge(stats, WINDOWS)
            variances(nc, link, st, tmp, var_ready)
            dve.wait_ge(root_ready, 1)
            scales(nc, link, tmp, g.mv1, mv_ready)
            dve.wait_ge(mv_ready, 1)

        @block.scalar
        def _(act):
            def take_turned(w, u):
                act.wait_ge(turned, w + 1)
                nc.scalar.copy(attnT[:, u % 2, :], tp[u % 2][:, 0:D]).then_inc(attnT_ready, 1)

            def trip(i, last_trip):
                for u in range(2):
                    w = i * 2 + u
                    if not (last_trip and u):
                        take_turned(w + 1, u + 1)
                    act.wait_ge(x_in[u], i * 16 + 16)
                    act.wait_ge(x1_ready, w + 1)
                    nc.scalar.activation(h0[:, u, :], xs[:, u, :], ACT.Identity, bias=g.mv0[:, 1, bass.ds(w, 1)],
                                         scale=g.mv0[:, 0, bass.ds(w, 1)]).then_inc(h0_ready, 1)

            take_turned(0, 0)
            with act.Fori(0, HALF - 1) as i:
                trip(i, False)
            trip(HALF - 1, True)
            act.wait_ge(var_ready, 1)
            nc.scalar.activation(tmp[:, 2, :], tmp[:, 2, :], ACT.Sqrt).then_inc(root_ready, 1)

        @block.tensor
        def _(pe):
            def turn(w, u):
                pe.wait_ge(attn_ready, w + 1)
                for c in range(KC):
                    last = nc.tensor.transpose(tp[u % 2][:, c * P:(c + 1) * P], attn[:, u % 2, c * P:(c + 1) * P], g.ident[:])
                last.then_inc(turned, 1)

            def trip(i, last_trip):
                for u in range(2):
                    w = i * 2 + u
                    if not (last_trip and u):
                        turn(w + 1, u + 1)
                    pe.wait_ge(attnT_ready, w + 1)
                    pe.wait_ge(x1_ready, w + 1)
                    for c in range(KC):
                        last = nc.tensor.matmul(ps[u][:, 0:D], attnT[:, u, c * P:(c + 1) * P], wo[:, c, :],
                                                start=(c == 0), stop=(c == KC - 1))
                    last.then_inc(proj_ready, 1)

            pe.wait_ge(w_in, 48)
            turn(0, 0)
            with pe.Fori(0, HALF - 1) as i:
                trip(i, False)
            trip(HALF - 1, True)


def ffn_phase(nc, g, a):
    HALF = WINDOWS // 2
    FC = FF // P
    HR = 4
    with ExitStack() as ctx:
        t = Tools(nc, ctx)
        w1, w2 = t.sb("w1", [P, KC, FF]), t.sb("w2", [P, FC, D])
        b1, b2, beta = t.sb("b1_f", [P, FC]), t.sb("b2_f", [P, D]), t.sb("beta", [P, 1])
        g2, bb2 = t.sb("g2", [P, KC]), t.sb("bb2", [P, KC])
        xs = t.sb("xs_f", [P, 2, D])
        xn = t.sb("xn_f", [P, 2, D])
        xT = t.sb("xT_f", [P, KC, 2 * P])
        hT = t.sb("hT", [P, FC, 2 * P])
        part = t.sb("part", [P, 2, D])
        st, tmp = t.sb("st_f", [P, WINDOWS, 6]), t.sb("tmp_f", [P, 3, WINDOWS])
        tp = t.ps("tp_f", [P, 512])
        h_ps = [t.ps(f"h_ps{u}", [P, 512]) for u in range(HR)]
        y_ps = [t.ps(f"y_ps{u}", [P, 512]) for u in range(2)]
        w_in, x_in = t.sem("ff_w_in"), t.sem("ff_x_in")
        chain, xn_ready, turned, xT_ready = t.sem("ff_chain"), t.sem("ff_xn"), t.sem("ff_turned"), t.sem("ff_xT")
        h_ready, h_act, y_ready = t.sem("ff_h"), t.sem("ff_h_act"), t.sem("ff_y")
        part_ready, x2_ready, y_done, stats = t.sem("ff_part"), t.sem("ff_x2"), t.sem("ff_ydone"), t.sem("ff_stats")
        var_ready, root_ready, mv_ready = t.sem("ff_var"), t.sem("ff_root"), t.sem("ff_mv")
        block = ctx.enter_context(nc.Block())
        x_w = a.x.rearrange("(w p) d -> p w d", p=P)

        @block.sync
        def _(sp):
            sp.dma_start(w1[:], a.W1.rearrange("(c p) n -> p c n", p=P)).then_inc(w_in, 16)
            sp.dma_start(w2[:], a.W2.rearrange("(c p) n -> p c n", p=P)).then_inc(w_in, 16)
            with nc.allow_non_contiguous_dma(reason="short vectors"):
                sp.dma_start(b1[:], a.b1.rearrange("o (c p) -> p (o c)", p=P)).then_inc(w_in, 16)
                sp.dma_start(g2[:], a.ln2_g.rearrange("o (c p) -> p (o c)", p=P)).then_inc(w_in, 16)
                sp.dma_start(bb2[:], a.ln2_b.rearrange("o (c p) -> p (o c)", p=P)).then_inc(w_in, 16)
            sp.dma_start(b2[:], bcast(a.b2, [P, D])).then_inc(w_in, 16)
            sp.dma_start(beta[:], bcast(a.beta, [P, 1])).then_inc(w_in, 16)
            sp.sem_inc(y_done, 1)
            with sp.Fori(0, HALF) as i:
                sp.wait_ge(y_done, i + 1)
                sp.dma_start(xs[:], x_w[:, bass.ds(i * 2, 2), :]).then_inc(x_in, 16)

        @block.vector
        def _(dve):
            count = [0]

            def link(ins):
                count[0] += 1
                ins.then_inc(chain, 1)
                dve.wait_ge(chain, count[0])

            def norm(n):
                for s in range(2):
                    w = n * 2 + s
                    last = nc.vector.tensor_scalar(xn[:, s:s + 1, :], g.acc[:, bass.ds(w, 1), 0:D],
                                                   g.mv1[:, 0, bass.ds(w, 1)], g.mv1[:, 1, bass.ds(w, 1)], ALU.mult, ALU.add)
                last.then_inc(xn_ready, 1)

            def gain(n):
                dve.wait_ge(turned, n + 1)
                for c in range(KC):
                    last = nc.vector.tensor_scalar(xT[:, c, :], tp[:, c * 2 * P:(c + 1) * 2 * P],
                                                   g2[:, c:c + 1], bb2[:, c:c + 1], ALU.mult, ALU.add)
                last.then_inc(xT_ready, 1)

            def trip(i, last_trip):
                if not last_trip:
                    dve.wait_ge(turned, i + 1)
                    norm(i + 1)
                    gain(i + 1)
                for s in range(2):
                    dve.wait_ge(y_ready, i * 2 + s + 3)
                    nc.vector.tensor_tensor(part[:, s, :], y_ps[s][:, 0:D], b2[:], ALU.add).then_inc(part_ready, 1)
                dve.wait_ge(part_ready, i * 2 + 4)
                x1 = g.acc[:, bass.ds(i * 2, 2), 0:D]
                nc.vector.scalar_tensor_tensor(x1, part[:], beta[:], x1, ALU.mult, ALU.add).then_inc(x2_ready, 1)
                dve.wait_ge(x2_ready, i + 1)
                dve.wait_ge(x_in, i * 16 + 16)
                nc.vector.tensor_tensor(x1, x1, xs[:], ALU.add).then_inc(y_done, 1)
                dve.wait_ge(y_done, i + 2)
                for s in range(2):
                    nc.vector.bn_stats(st[:, bass.ds(i * 2 + s, 1), :], g.acc[:, bass.ds(i * 2 + s, 1), 0:D]).then_inc(stats, 1)

            dve.sem_inc(part_ready, 2)
            dve.wait_ge(w_in, 112)
            norm(0)
            gain(0)
            with dve.Fori(0, HALF - 1) as i:
                trip(i, False)
            trip(HALF - 1, True)
            dve.wait_ge(stats, WINDOWS)
            variances(nc, link, st, tmp, var_ready)
            dve.wait_ge(root_ready, 1)
            scales(nc, link, tmp, g.mv2, mv_ready)
            dve.wait_ge(mv_ready, 1)

        @block.scalar
        def _(act):
            act.sem_inc(h_act, HR)
            act.wait_ge(w_in, 112)
            with act.Fori(0, HALF) as i:
                act.wait_ge(y_ready, i * 2 + 2)
                for f in range(FC):
                    act.wait_ge(h_ready, i * FC + f + 1)
                    nc.scalar.activation(hT[:, f, :], h_ps[f % HR][:, 0:2 * P], ACT.Gelu,
                                         bias=b1[:, f:f + 1]).then_inc(h_act, 1)
            act.wait_ge(var_ready, 1)
            nc.scalar.activation(tmp[:, 2, :], tmp[:, 2, :], ACT.Sqrt).then_inc(root_ready, 1)

        @block.tensor
        def _(pe):
            def turn(n):
                pe.wait_ge(xn_ready, n + 1)
                for c in range(KC):
                    for s in range(2):
                        last = nc.tensor.transpose(tp[:, (2 * c + s) * P:(2 * c + s + 1) * P],
                                                   xn[:, s, c * P:(c + 1) * P], g.ident[:])
                last.then_inc(turned, 1)

            def trip(i, last_trip):
                pe.wait_ge(xT_ready, i + 1)
                for f in range(FC):
                    pe.wait_ge(h_act, i * FC + f + 1)
                    for c in range(KC):
                        last = nc.tensor.matmul(h_ps[f % HR][:, 0:2 * P], w1[:, c, f * P:(f + 1) * P], xT[:, c, :],
                                                start=(c == 0), stop=(c == KC - 1))
                    last.then_inc(h_ready, 1)
                if not last_trip:
                    turn(i + 1)
                pe.wait_ge(part_ready, i * 2 + 2)
                for s in range(2):
                    for f in range(FC):
                        if s == 0 and f % HR == 0:
                            pe.wait_ge(h_act, i * FC + f + 2 * HR)
                        last = nc.tensor.matmul(y_ps[s][:, 0:D], hT[:, f, s * P:(s + 1) * P], w2[:, f, :],
                                                start=(f == 0), stop=(f == FC - 1))
                    last.then_inc(y_ready, 1)

            pe.sem_inc(y_ready, 2)
            pe.wait_ge(w_in, 112)
            turn(0)
            with pe.Fori(0, HALF - 1) as i:
                trip(i, False)
            trip(HALF - 1, True)


def route_phase(nc, g, a):
    W = TOKEN_WINDOWS
    SLOTS_W = 2 * W
    HALF_E = EXPERTS // 2
    RING = 4
    with ExitStack() as ctx:
        t = Tools(nc, ctx)
        wg, bg = t.sb("wg", [P, KC, EXPERTS]), t.sb("bg", [P, EXPERTS])
        xn = t.sb("xn_r", [P, 2, 2, D])
        xT = t.sb("xT_r", [P, 2, KC, 2 * P])
        gs = t.sb("gs", [P, WINDOWS, EXPERTS])
        best, chosen = t.sb("best", [P, W]), t.sb("chosen", [P, W])
        work = t.sb("work", [P, W, EXPERTS])
        hot = t.sb("hot", [P, EXPERTS, W, 2])
        total, rank = t.sb("total", [P, EXPERTS, SLOTS_W]), t.sb("rank", [P, EXPERTS, SLOTS_W])
        ran = t.sb("ran", [P, EXPERTS, SLOTS_W])
        ones = t.sb("ones_r", [P, EXPERTS * SLOTS_W])
        before = t.sb("before", [P, P])
        iota_p = t.sb("iota_p_r", [P, 1])
        ends, starts, pairs, pair_ends = (t.sb(name, [P, EXPERTS]) for name in ("ends_r", "starts_r", "pairs_r", "pair_ends"))
        pairs_i = t.sb("pairs_i", [P, EXPERTS], i32)
        of_pair = t.sb("of_pair", [1, PAIRS])
        place = t.sb("place_f", [P, SLOTS_W])
        rows = t.sb("rows_r", [P, RING, D])
        stage = t.sb("stage_r", [P, RING, 2], i32)
        tp = [t.ps(f"tp_r{u}", [P, 512]) for u in range(2)]
        gate_ps = [t.ps(f"gate_ps{u}", [P, 512]) for u in range(2)]
        count_ps = [t.ps(f"count_ps{n}", [P, 512]) for n in range(4)]
        w_in, weights_in = t.sem("rt_w_in"), t.sem("rt_weights_in")
        xn_ready, turned, xT_ready = t.sem("rt_xn"), t.sem("rt_turned"), t.sem("rt_xT")
        gate_ready, gs_ready = t.sem("rt_gate"), t.sem("rt_gs")
        consts, chain, hot_ready, counted = t.sem("rt_consts"), t.sem("rt_chain"), t.sem("rt_hot"), t.sem("rt_counted")
        placed, row_ready, staged = t.sem("rt_placed"), t.sem("rt_row"), t.sem("rt_staged")
        sent = [t.sem(f"rt_sent{r}") for r in range(RING)]
        block = ctx.enter_context(nc.Block())

        @block.sync
        def _(sp):
            sp.dma_start(wg[:], a.Wg.rearrange("(c p) n -> p c n", p=P)).then_inc(w_in, 16)
            sp.dma_start(bg[:], bcast(a.bg, [P, EXPERTS])).then_inc(w_in, 16)
            sp.dma_start(g.w1[:].rearrange("p e (c n) -> p (e c) n", c=KC),
                         a.E1.rearrange("e (c p) n -> p (e c) n", p=P)).then_inc(weights_in, 16)
            sp.dma_start(g.w2[:].rearrange("p e c n -> p (e c) n"),
                         a.E2.rearrange("e (c p) n -> p (e c) n", p=P)).then_inc(weights_in, 16)
            sp.wait_ge(weights_in, 32)

        @block.gpsimd
        def _(pool):
            nc.gpsimd.iota(iota_p[:], [[0, 1]], base=0, channel_multiplier=1,
                           allow_small_or_imprecise_dtypes=True).then_inc(consts, 1)
            nc.gpsimd.memset(ones[:], 1.0).then_inc(consts, 1)
            pool.wait_ge(placed, 1)

            def send(w, r):
                pool.wait_ge(row_ready, w + 1)
                nc.gpsimd.tensor_copy(stage[:, r, :], g.place[:, bass.ds(w * 2, 2)]).then_inc(staged, 1)
                pool.wait_ge(staged, w + 1)
                pool.sem_inc(g.carried, 1)
                for k in range(2):
                    nc.gpsimd.indirect_dma_start(
                        out=a.slots_d, out_offset=bass.IndirectOffsetOnAxis(ap=stage[:, r, k:k + 1], axis=0),
                        in_=rows[:, r, :], in_offset=None).then_inc(sent[r], 16)

            with pool.Fori(0, W // RING) as i:
                for r in range(RING):
                    send(i * RING + r, r)
            for w in range(W // RING * RING, W):
                send(w, w % RING)
            for r in range(RING):
                pool.wait_ge(sent[r], 32 * len(range(r, W, RING)))

        @block.scalar
        def _(act):
            def norm_pair(n, u):
                act.wait_ge(turned, n + 1)
                for s in range(2):
                    w = n * 2 + s
                    last = nc.scalar.activation(xn[:, u, s:s + 1, :], g.acc[:, bass.ds(w, 1), 0:D], ACT.Identity,
                                                bias=g.mv2[:, 1, bass.ds(w, 1)], scale=g.mv2[:, 0, bass.ds(w, 1)])
                last.then_inc(xn_ready, 1)

            act.sem_inc(turned, 2)
            with act.Fori(0, WINDOWS // 4) as i:
                for u in range(2):
                    norm_pair(i * 2 + u, u)
            norm_pair(WINDOWS // 2 - 1, 0)
            act.wait_ge(placed, 1)

            def norm_row(w, r):
                nc.scalar.activation(rows[:, r:r + 1, :], g.acc[:, bass.ds(w, 1), 0:D], ACT.Identity,
                                     bias=g.mv2[:, 1, bass.ds(w, 1)], scale=g.mv2[:, 0, bass.ds(w, 1)]).then_inc(row_ready, 1)

            for r in range(RING):
                norm_row(r, r)
            with act.Fori(0, W // RING - 1) as i:
                for r in range(RING):
                    act.wait_ge(sent[r], i * 32 + 32)
                    norm_row(i * RING + r + RING, r)
            for w in range(W // RING * RING, W):
                act.wait_ge(sent[w % RING], w // RING * 32)
                norm_row(w, w % RING)

        @block.vector
        def _(dve):
            count = [0]

            def link(ins):
                count[0] += 1
                ins.then_inc(chain, 1)
                dve.wait_ge(chain, count[0])

            def take_xT(n, u):
                dve.wait_ge(turned, n + 3)
                dve.wait_ge(gate_ready, n + 1)
                nc.vector.tensor_copy(xT[:, u, :, :].rearrange("p c n -> p (c n)"), tp[u][:]).then_inc(xT_ready, 1)

            def take_gates(n, u):
                dve.wait_ge(gate_ready, n + 3)
                nc.vector.tensor_copy(gs[:, bass.ds(n * 2, 2), :],
                                      gate_ps[u][:, 0:2 * EXPERTS].rearrange("p (s e) -> p s e", s=2)).then_inc(gs_ready, 1)

            dve.sem_inc(xT_ready, 2)
            dve.sem_inc(gs_ready, 2)
            take_xT(0, 0)
            with dve.Fori(0, WINDOWS // 4) as i:
                for u in range(2):
                    take_xT(i * 2 + u + 1, 1 - u)
                    take_gates(i * 2 + u, u)
            take_gates(WINDOWS // 2 - 1, 0)
            dve.wait_ge(gs_ready, WINDOWS // 2 + 2)
            dve.wait_ge(w_in, 32)
            dve.wait_ge(consts, 2)
            link(nc.vector.tensor_scalar(before[:], g.iota_row[:], iota_p[:], None, ALU.is_gt))
            scores = gs[:, 0:W, :]
            by_expert = [P, W, EXPERTS]
            experts = bcast(g.iota_row[:, None, 0:EXPERTS], by_expert)
            link(nc.vector.tensor_tensor(scores, scores, bcast(bg[:, None, :], by_expert), ALU.add))
            for k in range(2):
                link(nc.vector.tensor_reduce(out=best[:], in_=scores, op=ALU.max, axis=AX.X))
                link(nc.vector.tensor_tensor(work[:], scores, bcast(best[:, :, None], by_expert), ALU.is_equal))
                link(nc.vector.scalar_tensor_tensor(work[:], work[:], -float(EXPERTS), experts, ALU.mult, ALU.add))
                link(nc.vector.tensor_reduce(out=chosen[:], in_=work[:], op=ALU.min, axis=AX.X))
                link(nc.vector.scalar_tensor_tensor(work[:], experts, -float(EXPERTS), bcast(chosen[:, :, None], by_expert),
                                                    ALU.add, ALU.is_equal))
                link(nc.vector.tensor_copy(hot[:, :, :, k].rearrange("p e w -> p w e"), work[:]))
                if k == 0:
                    link(nc.vector.scalar_tensor_tensor(scores, work[:], -BIG, scores, ALU.mult, ALU.add))
            nc.vector.engine_nop().then_inc(hot_ready, 1)
            for h in range(2):
                for n, into in enumerate((total, rank)):
                    dve.wait_ge(counted, 2 * h + n + 1)
                    link(nc.vector.tensor_copy(into[:, h * HALF_E:(h + 1) * HALF_E, :].rearrange("p e s -> p (e s)"),
                                               count_ps[2 * h + n][:, 0:HALF_E * SLOTS_W]))
            flat = [ap[:].rearrange("p e s -> p (e s)") for ap in (ran, total, rank)]
            link(nc.vector.tensor_tensor_scan(flat[0], ones[:], flat[1], 0.0, ALU.mult, ALU.add))
            link(nc.vector.tensor_copy(ends[:], ran[:, :, SLOTS_W - 1]))
            link(nc.vector.tensor_tensor(flat[0], flat[0], flat[1], ALU.subtract))
            link(nc.vector.tensor_tensor(flat[0], flat[0], flat[2], ALU.add))
            link(nc.vector.memset(starts[:, 0:1], 0.0))
            link(nc.vector.tensor_copy(starts[:, 1:], ends[:, 0:EXPERTS - 1]))
            link(nc.vector.tensor_tensor(pairs[:], ends[:], starts[:], ALU.subtract))
            link(nc.vector.tensor_scalar(pairs[:], pairs[:], float(2 * P - 1), None, ALU.add))
            link(nc.vector.tensor_copy(pairs_i[:], pairs[:]))
            link(nc.vector.tensor_scalar(pairs_i[:], pairs_i[:], 8, None, ALU.arith_shift_right))
            link(nc.vector.tensor_copy(pairs[:], pairs_i[:]))
            link(nc.vector.tensor_tensor_scan(pair_ends[:], ones[:, 0:EXPERTS], pairs[:], 0.0, ALU.mult, ALU.add))
            link(nc.vector.tensor_tensor(pairs[:], pair_ends[:], pairs[:], ALU.subtract))
            link(nc.vector.scalar_tensor_tensor(starts[:], pairs[:], float(2 * P), starts[:], ALU.mult, ALU.subtract))
            link(nc.vector.tensor_tensor(ran[:], ran[:], bcast(starts[:, :, None], [P, EXPERTS, SLOTS_W]), ALU.add))
            link(nc.vector.tensor_tensor(ran[:], ran[:], hot[:].rearrange("p e w k -> p e (w k)"), ALU.mult))
            link(nc.vector.tensor_reduce(out=place[:], in_=ran[:].rearrange("p e s -> p s e"), op=ALU.add, axis=AX.X))
            nc.vector.tensor_copy(g.place[:], place[:]).then_inc(placed, 1)
            link(nc.vector.memset(of_pair[:], 0.0))
            for e in range(EXPERTS):
                link(nc.vector.scalar_tensor_tensor(of_pair[:], g.iota_row[0:1, 0:PAIRS], pair_ends[0:1, e:e + 1],
                                                    of_pair[:], ALU.is_ge, ALU.add))
            link(nc.vector.tensor_scalar(of_pair[:], of_pair[:], float(EXPERTS - 1), None, ALU.min))
            link(nc.vector.tensor_copy(g.expert_row[:], of_pair[:]))

        @block.tensor
        def _(pe):
            def turn(n, u):
                pe.wait_ge(xn_ready, n + 1)
                pe.wait_ge(xT_ready, n + 1)
                for c in range(KC):
                    for s in range(2):
                        last = nc.tensor.transpose(tp[u][:, (2 * c + s) * P:(2 * c + s + 1) * P],
                                                   xn[:, u, s, c * P:(c + 1) * P], g.ident[:])
                last.then_inc(turned, 1)

            def gates(n, u):
                pe.wait_ge(xT_ready, n + 3)
                pe.wait_ge(gs_ready, n + 1)
                for s in range(2):
                    for c in range(KC):
                        last = nc.tensor.matmul(gate_ps[u][:, s * EXPERTS:(s + 1) * EXPERTS], xT[:, u, c, s * P:(s + 1) * P],
                                                wg[:, c, :], start=(c == 0), stop=(c == KC - 1))
                last.then_inc(gate_ready, 1)

            pe.sem_inc(gate_ready, 2)
            pe.wait_ge(w_in, 32)
            turn(0, 0)
            with pe.Fori(0, WINDOWS // 4) as i:
                for u in range(2):
                    turn(i * 2 + u + 1, 1 - u)
                    gates(i * 2 + u, u)
            gates(WINDOWS // 2 - 1, 0)
            pe.wait_ge(hot_ready, 1)
            for h in range(2):
                slots = hot[:, h * HALF_E:(h + 1) * HALF_E, :, :].rearrange("p e w k -> p (e w k)")
                for n, weights in enumerate((ones[:, 0:P], before[:])):
                    nc.tensor.matmul(count_ps[2 * h + n][:, 0:HALF_E * SLOTS_W], weights, slots,
                                     start=True, stop=True).then_inc(counted, 1)


def expert_phase(nc, g, a):
    HC = EH // P
    RING = 4
    LAST = PAIRS - 1
    with ExitStack() as ctx:
        t = Tools(nc, ctx)
        b1, b2 = t.sb("b1_m", [P, EXPERTS, HC]), t.sb("b2_m", [P, EXPERTS, D])
        x = t.sb("x_m", [P, RING, 2, D])
        xT = t.sb("xT_m", [P, 2, KC, 2 * P])
        w1 = t.sb("w1_now", [P, 2, KC * EH])
        hT = t.sb("hT_m", [P, 2, HC, 2 * P])
        res = t.sb("res_m", [P, 2, 2, D])
        tp = [t.ps(f"tp_m{u}", [P, 512]) for u in range(2)]
        h_ps = [t.ps(f"h_ps_m{f}", [P, 512]) for f in range(HC)]
        y_ps = [t.ps(f"y_ps_m{u}", [P, 512]) for u in range(2)]
        w_in, x_in = t.sem("mo_w_in"), [t.sem(f"mo_x_in{r}") for r in range(RING)]
        turned, fed, h_ready, h_act = t.sem("mo_turned"), t.sem("mo_fed"), t.sem("mo_h"), t.sem("mo_hact")
        y_ready, res_ready, out_done = t.sem("mo_y"), t.sem("mo_res"), [t.sem("mo_out0"), t.sem("mo_out1")]
        block = ctx.enter_context(nc.Block())
        slots = a.slots_d.rearrange("(n s p) d -> p n s d", s=2, p=P)
        results = a.results_d.rearrange("(n s p) d -> p n s d", s=2, p=P)

        def expert_of(name, n):
            return values_of(nc, g.expert_row, name, n, 1, EXPERTS - 1)[0]

        @block.sync
        def _(sp):
            def load(n, r):
                sp.wait_ge(turned, n + 1)
                sp.dma_start(x[:, r:r + 1, :, :], slots[:, bass.ds(n, 1), :, :]).then_inc(x_in[r], 16)

            def store(n, u):
                sp.wait_ge(res_ready, n + 3)
                sp.dma_start(results[:, bass.ds(n, 1), :, :], res[:, u:u + 1, :, :]).then_inc(out_done[u], 16)

            sp.sem_inc(turned, RING)
            with nc.allow_non_contiguous_dma(reason="short vectors"):
                sp.dma_start(b1[:], a.eb1.rearrange("e (c p) -> p e c", p=P)).then_inc(w_in, 16)
            for n in range(RING):
                load(n, n)
            sp.dma_start(b2[:].rearrange("p e d -> p (e d)"), bcast(a.eb2, [P, EXPERTS * D])).then_inc(w_in, 16)
            with sp.Fori(0, (PAIRS - RING) // RING) as i:
                for r in range(RING):
                    store(i * RING + r, r % 2)
                    load(i * RING + r + RING, r)
            for n in range((PAIRS - RING) // RING * RING, PAIRS):
                store(n, n % 2)
                if n + RING < PAIRS:
                    load(n + RING, n % RING)
            for u in range(2):
                sp.wait_ge(out_done[u], 16 + 16 * len(range(u, PAIRS, 2)))

        @block.vector
        def _(dve):
            def feed(n, u, expert):
                dve.wait_ge(turned, n + 1 + RING)
                dve.wait_ge(h_ready, n * HC + 1)
                nc.vector.tensor_copy(xT[:, u, :, :].rearrange("p c n -> p (c n)"), tp[u][:])
                nc.vector.tensor_copy(w1[:, u:u + 1, :], g.w1[:, bass.ds(expert, 1), :]).then_inc(fed, 1)

            def take(n, i, u, expert):
                dve.wait_ge(y_ready, n + 3)
                dve.wait_ge(out_done[u], i * 16 + 16)
                nc.vector.tensor_tensor(res[:, u, :, :], y_ps[u][:].rearrange("p (s d) -> p s d", s=2),
                                        bcast(b2[:, bass.ds(expert, 1), :], [P, 2, D]), ALU.add).then_inc(res_ready, 1)

            dve.sem_inc(fed, 2)
            dve.sem_inc(res_ready, 2)
            for u in range(2):
                dve.sem_inc(out_done[u], 16)
            dve.wait_ge(w_in, 32)
            for n in range(2):
                feed(n, n, expert_of(mybir.EngineType.DVE, n))
            with dve.Fori(0, (PAIRS - 2) // 2) as i:
                for u in range(2):
                    n = i * 2 + u
                    feed(n + 2, u, expert_of(mybir.EngineType.DVE, n + 2))
                    take(n, i, u, expert_of(mybir.EngineType.DVE, n))
            for n in range((PAIRS - 2) // 2 * 2, PAIRS):
                if n + 2 <= LAST:
                    feed(n + 2, n % 2, expert_of(mybir.EngineType.DVE, n + 2))
                take(n, n // 2, n % 2, expert_of(mybir.EngineType.DVE, n))

        @block.scalar
        def _(act):
            def hidden(n, u):
                expert = expert_of(mybir.EngineType.Activation, n)
                act.wait_ge(y_ready, n + 1)
                for f in range(HC):
                    act.wait_ge(h_ready, (n + 2) * HC + f + 1)
                    nc.scalar.activation(hT[:, u, f, :], h_ps[f][:, 0:2 * P], ACT.Gelu,
                                         bias=b1[:, bass.ds(expert, 1), f]).then_inc(h_act, 1)

            act.sem_inc(h_act, HC)
            act.wait_ge(w_in, 32)
            with act.Fori(0, PAIRS // 2) as i:
                for u in range(2):
                    hidden(i * 2 + u, u)
            for n in range(PAIRS // 2 * 2, PAIRS):
                hidden(n, n % 2)

        @block.tensor
        def _(pe):
            def turn(n, r, trip):
                pe.wait_ge(x_in[r], trip * 16 + 16)
                pe.wait_ge(fed, n + 1)
                for c in range(KC):
                    for s in range(2):
                        last = nc.tensor.transpose(tp[r % 2][:, (2 * c + s) * P:(2 * c + s + 1) * P],
                                                   x[:, r, s, c * P:(c + 1) * P], g.ident[:])
                last.then_inc(turned, 1)

            def up(n, u):
                pe.wait_ge(fed, n + 3)
                for f in range(HC):
                    pe.wait_ge(h_act, n * HC + f + 1)
                    for c in range(KC):
                        last = nc.tensor.matmul(h_ps[f][:, 0:2 * P], w1[:, u, c * EH + f * P:c * EH + (f + 1) * P], xT[:, u, c, :],
                                                start=(c == 0), stop=(c == KC - 1))
                    last.then_inc(h_ready, 1)

            def down(n, u):
                expert = expert_of(mybir.EngineType.PE, n)
                pe.wait_ge(h_act, n * HC + 2 * HC)
                pe.wait_ge(res_ready, n + 1)
                for s in range(2):
                    for f in range(HC):
                        last = nc.tensor.matmul(y_ps[u][:, s * D:(s + 1) * D], hT[:, u, f, s * P:(s + 1) * P],
                                                g.w2[:, bass.ds(expert, 1), f, :].rearrange("p o d -> p (o d)"),
                                                start=(f == 0), stop=(f == HC - 1))
                last.then_inc(y_ready, 1)

            pe.sem_inc(y_ready, 2)
            pe.sem_inc(h_ready, 2 * HC)
            turn(0, 0, 0)
            up(0, 0)
            turn(1, 1, 0)
            with pe.Fori(0, (PAIRS - 2) // RING) as i:
                for r in range(RING):
                    n = i * RING + r
                    up(n + 1, (r + 1) % 2)
                    turn(n + 2, (r + 2) % RING, i + (r + 2) // RING)
                    down(n, r % 2)
            for n in range((PAIRS - 2) // RING * RING, PAIRS):
                if n + 1 <= LAST:
                    up(n + 1, (n + 1) % 2)
                if n + 2 <= LAST:
                    turn(n + 2, (n + 2) % RING, (n + 2) // RING)
                down(n, n % 2)


def combine_phase(nc, g, a):
    W = TOKEN_WINDOWS
    RING = 4
    with ExitStack() as ctx:
        t = Tools(nc, ctx)
        rows = t.sb("rows_c", [P, RING, 2, D])
        stage = t.sb("stage_c", [P, RING, 2], i32)
        both = t.sb("both", [P, RING, D])
        out = t.sb("out_c", [P, RING, D])
        rows_in, out_done = [t.sem(f"cb_in{r}") for r in range(RING)], [t.sem(f"cb_out{r}") for r in range(RING)]
        staged, added, out_ready = t.sem("cb_staged"), t.sem("cb_added"), t.sem("cb_ready")
        block = ctx.enter_context(nc.Block())
        out_w = a.out.rearrange("(w p) d -> p w d", p=P)

        def windows(eng, step):
            with eng.Fori(0, W // RING) as i:
                for r in range(RING):
                    step(i * RING + r, r, i)
            for w in range(W // RING * RING, W):
                step(w, w % RING, w // RING)

        @block.gpsimd
        def _(pool):
            def fetch(w, r, i):
                pool.wait_ge(added, w + 1)
                nc.gpsimd.tensor_copy(stage[:, r, :], g.place[:, bass.ds(w * 2, 2)]).then_inc(staged, 1)
                pool.wait_ge(staged, w + 1)
                pool.sem_inc(g.carried, 1)
                for k in range(2):
                    nc.gpsimd.indirect_dma_start(
                        out=rows[:, r, k, :], out_offset=None, in_=a.results_d,
                        in_offset=bass.IndirectOffsetOnAxis(ap=stage[:, r, k:k + 1], axis=0)).then_inc(rows_in[r], 16)

            windows(pool, fetch)

        @block.vector
        def _(dve):
            def add(w, r, i):
                dve.wait_ge(rows_in[r], i * 32 + 32)
                nc.vector.tensor_tensor(both[:, r, :], rows[:, r, 0, :], rows[:, r, 1, :], ALU.add).then_inc(added, 1)
                dve.wait_ge(added, w + 1 + RING)
                dve.wait_ge(out_done[r], i * 16 + 16)
                nc.vector.tensor_tensor(out[:, r:r + 1, :], both[:, r:r + 1, :], g.acc[:, bass.ds(w, 1), 0:D],
                                        ALU.add).then_inc(out_ready, 1)

            dve.sem_inc(added, RING)
            for r in range(RING):
                dve.sem_inc(out_done[r], 16)
            windows(dve, add)

        @block.sync
        def _(sp):
            def store(w, r, i):
                sp.wait_ge(out_ready, w + 1)
                sp.dma_start(out_w[:, bass.ds(w, 1), :], out[:, r:r + 1, :]).then_inc(out_done[r], 16)

            windows(sp, store)
            for r in range(RING):
                sp.wait_ge(out_done[r], 16 + 16 * len(range(r, W, RING)))


def program(nc, a):
    with ExitStack() as ctx:
        t = Tools(nc, ctx)
        g = Places()
        g.carried = t.sem("carried")
        g.ident = t.sb("ident", [P, P])
        g.iota_row = t.sb("iota_row", [P, P])
        g.ones = t.sb("ones", [1, P])
        g.mv0, g.mv1, g.mv2 = (t.sb(f"mv{n}", [P, 2, WINDOWS]) for n in range(3))
        g.r1 = t.sb("r1", [P, TABLE_WINDOWS * ACC])
        g.acc = g.r1[:, :].rearrange("p (w c) -> p w c", c=ACC)
        halves = g.r1[:, :].bitcast(bf16)
        q_size = TABLE_WINDOWS * D
        with ExitStack() as edge_ctx:
            t = Tools(nc, edge_ctx)
            g.rel = t.sb("rel", [P, STEPS_UP])
            g.ew = t.sb("ew", [P, STEPS_UP])
            g.src = t.sb("src", [P, STEPS_UP], i32)
            g.ident_b = t.sb("ident_b", [P, P], bf16)
            g.tile_row = t.sb("tile_row", [1, STEPS_UP], i32)
            g.win_row = t.sb("win_row", [1, STEPS_UP + LEAD], i32)
            setup_phase(nc, g, a)
            g.scores = t.sb("scores", [P, STEPS, HEADS])
            with ExitStack() as q_ctx:
                q_lo = Tools(nc, q_ctx).sb("q_lo", [P, TABLE_WINDOWS, D], bf16)
                g.q = [halves[:, n * q_size:(n + 1) * q_size].rearrange("p (w d) -> p w d", d=D) for n in range(2)]
                g.q.append(q_lo)
                node_phase(nc, g, a)
                score_phase(nc, g, a)
            softmax_phase(nc, g, a)
            gather_phase(nc, g, a)
        t = Tools(nc, ctx)
        attention_out_phase(nc, g, a)
        ffn_phase(nc, g, a)
        g.place = t.sb("place", [P, 2 * TOKEN_WINDOWS], i32)
        g.expert_row = t.sb("expert_row", [1, PAIRS], i32)
        g.w1 = t.sb("expert_w1", [P, EXPERTS, KC * EH])
        g.w2 = t.sb("expert_w2", [P, EXPERTS, EH // P, D])
        route_phase(nc, g, a)
        expert_phase(nc, g, a)
        combine_phase(nc, g, a)


class Places:
    pass


def kernel(**inputs):
    import numpy as np
    import concourse.bacc as bacc
    from concourse.bass_utils import run_bass_kernel_spmd

    def get(name):
        return np.ascontiguousarray(inputs[name])

    def padded(rows, n, fill=0):
        out = np.full((n,) + rows.shape[1:], fill, rows.dtype)
        out[:rows.shape[0]] = rows
        return out

    n_edges = EDGE_TILES * P
    dst = padded(get("dst"), n_edges, WINDOWS * P - 1).reshape(EDGE_TILES, P)
    ef = padded(get("edge_attr_64"), n_edges).reshape(EDGE_TILES, P, ED)
    row = lambda name: get("L0_" + name).reshape(1, -1)
    arrays = {
        "x": padded(get("x"), WINDOWS * P),
        "dst_rows": dst,
        "last_dst": np.ascontiguousarray(dst[:, P - 1]).reshape(1, -1),
        "src_rows": padded(get("src"), n_edges).reshape(EDGE_TILES, P),
        "ew_rows": padded(get("edge_weight"), n_edges).reshape(EDGE_TILES, P),
        "ef_t": np.ascontiguousarray(ef.transpose(0, 2, 1)).reshape(EDGE_TILES * ED, P),
        "wqkv": np.concatenate([get("L0_gnn_W" + c) for c in "qkv"], axis=1),
        "bqkv": np.concatenate([row("gnn_b" + c) for c in "qkv"], axis=1),
        "We": get("L0_gnn_We"), "be": row("gnn_be"), "Wo": get("L0_gnn_Wo"), "bo": row("gnn_bo"),
        "ln1_g": row("gnn_ln1_g"), "ln1_b": row("gnn_ln1_b"), "ln2_g": row("gnn_ln2_g"), "ln2_b": row("gnn_ln2_b"),
        "W1": get("L0_gnn_W1"), "b1": row("gnn_b1"), "W2": get("L0_gnn_W2"), "b2": row("gnn_b2"),
        "alpha": row("gnn_alpha"), "beta": row("gnn_beta"),
        "Wg": get("L0_ffn_Wg"), "bg": row("ffn_bg"), "E1": get("L0_ffn_W1"), "eb1": get("L0_ffn_b1"),
        "E2": get("L0_ffn_W2"), "eb2": row("ffn_b2"),
    }
    nc = bacc.Bacc("TRN2", target_bir_lowering=False, num_devices=1)
    a = Places()
    for name, array in arrays.items():
        a.__dict__[name] = nc.dram_tensor("in_" + name, array.shape, mybir.dt.from_np(array.dtype), kind="ExternalInput").ap()
    a.out = nc.dram_tensor("out", (TOKEN_WINDOWS * P, D), fp32, kind="ExternalOutput").ap()
    a.k_d = nc.dram_tensor("k_table", (WINDOWS * P, D), fp32, kind="Internal").ap()
    a.v_d = nc.dram_tensor("v_table", (WINDOWS * P, D), fp32, kind="Internal").ap()
    a.slots_d = nc.dram_tensor("slots_table", (PAIRS * 2 * P, D), fp32, kind="Internal").ap()
    a.results_d = nc.dram_tensor("results_table", (PAIRS * 2 * P, D), fp32, kind="Internal").ap()
    a.steps_d = nc.dram_tensor("steps_scratch", (2, STEPS_UP), i32, kind="Internal").ap()
    a.keys_d = nc.dram_tensor("keys_scratch", (1, 1 + STEPS_UP * P), fp32, kind="Internal").ap()
    program(nc, a)
    result = run_bass_kernel_spmd(nc, [{"in_" + name: array for name, array in arrays.items()}], core_ids=[0])
    return np.ascontiguousarray(result.results[0]["out"][:NODES])
```

```python
import concourse.bass as bass
from concourse import mybir
from contextlib import ExitStack

fp32 = mybir.dt.float32
bf16 = mybir.dt.bfloat16
i32 = mybir.dt.int32
u32 = mybir.dt.uint32
ALU = mybir.AluOpType
ACT = mybir.ActivationFunctionType
AX = mybir.AxisListType

P = 128
NODES, D, HEADS, DH = 6250, 256, 8, 32
EDGES, ED = 100000, 64
FF, EXPERTS, EH = 1024, 8, 512
EPS = 1e-5
STATS_UNROLL = 10
KC = D // P
WINDOWS = 50
EDGE_TILES = (EDGES + P - 1) // P
GROUP = 16
STEPS = (EDGE_TILES + WINDOWS - 1 + GROUP - 1) // GROUP * GROUP
SCOLS = (STEPS + P - 1) // P
STEPS_UP = SCOLS * P
TABLE_WINDOWS = STEPS - EDGE_TILES + 1
CHUNKS = 16
CHUNK_STEPS = STEPS // CHUNKS
CHUNK = CHUNK_STEPS * P
ACC = D + HEADS
TOKEN_WINDOWS = (NODES + P - 1) // P
OUT_WINDOWS = TOKEN_WINDOWS + 2
PAIRS = (2 * TOKEN_WINDOWS * P + EXPERTS * (2 * P - 1)) // (2 * P)
BIG = 2.0 ** 100
TINY = 1e-30


def bcast(ap, shape):
    return ap.broadcast_to(shape)


class Tools:

    def __init__(self, nc, ctx):
        self.nc, self.ctx = nc, ctx

    def sb(self, name, shape, dt=fp32):
        return self.ctx.enter_context(self.nc.sbuf_tensor(name, shape, dt))

    def ps(self, name, shape, dt=fp32):
        return self.ctx.enter_context(self.nc.psum_tensor(name, shape, dt))

    def sem(self, name):
        return self.ctx.enter_context(self.nc.semaphore(name))


def setup_phase(nc, g, a):
    with ExitStack() as ctx:
        t = Tools(nc, ctx)
        last_i = t.sb("last_i", [P, EDGE_TILES], i32)
        exit_step = t.sb("exit_step", [P, EDGE_TILES])
        iota_tile = t.sb("iota_tile", [P, EDGE_TILES])
        below = t.sb("below", [P, EDGE_TILES])
        iota_p = t.sb("iota_p", [P, 1])
        iota_step = t.sb("iota_step", [P, SCOLS])
        tile_f = t.sb("tile_f", [P, SCOLS])
        win_f = t.sb("win_f", [P, SCOLS])
        win_base = t.sb("win_base", [P, SCOLS])
        tile_i = t.sb("tile_i", [P, SCOLS], i32)
        win_i = t.sb("win_i", [P, SCOLS], i32)
        ends_g = t.sb("ends_g", [P, SCOLS, 2 * P], i32)
        dst_g, src_g = ends_g[:, :, 0:P], ends_g[:, :, P:2 * P]
        ew_g = t.sb("ew_g", [P, SCOLS, P])
        rel_g = t.sb("rel_g", [P, SCOLS, P])
        srcf_g = t.sb("srcf_g", [P, SCOLS, P])
        key_g = t.sb("key_g", [P, SCOLS, P])
        ok_g = t.sb("ok_g", [P, SCOLS, P])
        pad = t.sb("pad", [1, 1])
        tp = [t.ps(f"tp_s{u}", [P, 512]) for u in range(2)]
        loaded, consts, chain = t.sem("su_loaded"), t.sem("su_consts"), t.sem("su_chain")
        gathered, rows_out, rows_in = t.sem("su_gathered"), t.sem("su_rows_out"), t.sem("su_rows_in")
        tiles_known, laid, turned, evac = t.sem("su_tiles"), t.sem("su_laid"), t.sem("su_turned"), t.sem("su_evac")
        keys_out, x_in, stats = t.sem("su_keys_out"), t.sem("su_x_in"), t.sem("su_stats")
        block = ctx.enter_context(nc.Block())

        @block.sync
        def _(sp):
            sp.dma_start(last_i[:], bcast(a.last_dst, [P, EDGE_TILES])).then_inc(loaded, 16)
            sp.dma_start(g.xs, a.x.rearrange("(w p) d -> p w d", p=P)).then_inc(x_in, 16)
            sp.wait_ge(tiles_known, 1)
            with nc.allow_non_contiguous_dma(reason="two rows of 896 numbers"):
                sp.dma_start(a.steps_d[0:1, :].rearrange("o (c p) -> p (o c)", p=P), tile_i[:]).then_inc(rows_out, 16)
                sp.dma_start(a.steps_d[1:2, :].rearrange("o (c p) -> p (o c)", p=P), win_i[:]).then_inc(rows_out, 16)
            sp.wait_ge(rows_out, 32)
            sp.dma_start(g.tile_row[:], a.steps_d[0:1, :]).then_inc(rows_in, 16)
            sp.dma_start(g.win_row[0:1, LEAD:], a.steps_d[1:2, :]).then_inc(rows_in, 16)
            sp.wait_ge(laid, 1)
            sp.dma_start(a.keys_d[0:1, 1:1 + STEPS_UP * P].rearrange("o (c p e) -> p (o c) e", p=P, e=P),
                         key_g[:]).then_inc(keys_out, 16)
            sp.dma_start(a.keys_d[0:1, 0:1], pad[:]).then_inc(keys_out, 16)
            sp.wait_ge(keys_out, 32)
            sp.wait_ge(rows_in, 32)

        @block.gpsimd
        def _(pool):
            nc.gpsimd.iota(iota_tile[:], [[1, EDGE_TILES]], base=0, channel_multiplier=0,
                           allow_small_or_imprecise_dtypes=True).then_inc(consts, 1)
            nc.gpsimd.iota(iota_step[:], [[P, SCOLS]], base=0, channel_multiplier=1,
                           allow_small_or_imprecise_dtypes=True).then_inc(consts, 1)
            nc.gpsimd.iota(iota_p[:], [[0, 1]], base=0, channel_multiplier=1,
                           allow_small_or_imprecise_dtypes=True).then_inc(consts, 1)
            nc.gpsimd.iota(g.iota_row[:], [[1, P]], base=0, channel_multiplier=0,
                           allow_small_or_imprecise_dtypes=True).then_inc(consts, 1)
            nc.gpsimd.memset(pad[:], -5.0).then_inc(consts, 1)
            nc.gpsimd.memset(g.ones[:], 1.0).then_inc(consts, 1)
            nc.gpsimd.memset(g.win_row[0:1, 0:LEAD], 0).then_inc(consts, 1)
            pool.wait_ge(tiles_known, 1)
            for c in range(SCOLS):
                for into, rows in ((ends_g, a.ends_rows), (ew_g, a.ew_rows)):
                    nc.gpsimd.indirect_dma_start(
                        out=into[:, c, :], out_offset=None, in_=rows,
                        in_offset=bass.IndirectOffsetOnAxis(ap=tile_i[:, c:c + 1], axis=0)).then_inc(gathered, 16)

        @block.vector
        def _(dve):
            count = [0]

            def link(ins):
                count[0] += 1
                ins.then_inc(chain, 1)
                dve.wait_ge(chain, count[0])

            dve.wait_ge(consts, 7)
            link(nc.vector.tensor_scalar(g.ident[:], g.iota_row[:], iota_p[:], None, ALU.is_equal))
            link(nc.vector.tensor_copy(g.ident_b[:], g.ident[:]))
            dve.wait_ge(loaded, 16)
            link(nc.vector.tensor_scalar(last_i[:], last_i[:], 7, None, ALU.arith_shift_right))
            link(nc.vector.tensor_tensor(exit_step[:], last_i[:], iota_tile[:], ALU.add))
            for c in range(SCOLS):
                link(nc.vector.tensor_scalar(below[:], exit_step[:], iota_step[:, c:c + 1], None,
                                             ALU.is_lt, ALU.add, accum_out=tile_f[:, c:c + 1]))
            link(nc.vector.tensor_scalar(tile_f[:], tile_f[:], float(EDGE_TILES - 1), None, ALU.min))
            link(nc.vector.tensor_tensor(win_f[:], iota_step[:], tile_f[:], ALU.subtract))
            link(nc.vector.tensor_scalar(win_base[:], win_f[:], -float(P), None, ALU.mult))
            link(nc.vector.tensor_copy(win_i[:], win_f[:]))
            nc.vector.tensor_copy(tile_i[:], tile_f[:]).then_inc(tiles_known, 1)
            dve.wait_ge(x_in, 16)
            with dve.Fori(0, WINDOWS // STATS_UNROLL) as i:
                for n in range(STATS_UNROLL):
                    w = i * STATS_UNROLL + n
                    nc.vector.bn_stats(g.st[:, bass.ds(w, 1), :], g.xs[:, bass.ds(w, 1), :]).then_inc(stats, 1)
            dve.wait_ge(stats, WINDOWS)
            dve.wait_ge(gathered, 16 * 2 * SCOLS)
            for c in range(SCOLS):
                link(nc.vector.tensor_scalar(rel_g[:, c, :], dst_g[:, c, :], win_base[:, c:c + 1], None, ALU.add))
            link(nc.vector.tensor_scalar(ok_g[:], rel_g[:], 0.0, None, ALU.is_ge))
            link(nc.vector.scalar_tensor_tensor(ok_g[:], rel_g[:], float(P), ok_g[:], ALU.is_lt, ALU.mult))
            link(nc.vector.scalar_tensor_tensor(key_g[:], dst_g, 1.0, ok_g[:], ALU.add, ALU.mult))
            nc.vector.tensor_copy(srcf_g[:], src_g).then_inc(laid, 1)
            for c in range(SCOLS):
                dve.wait_ge(turned, 3 * (c + 1))
                cols = slice(c * P, (c + 1) * P)
                nc.vector.tensor_copy(g.rel[:, cols], tp[c % 2][:, 0:P])
                nc.vector.tensor_copy(g.src[:, cols], tp[c % 2][:, P:2 * P])
                nc.vector.tensor_scalar(g.ew[:, cols], tp[c % 2][:, 2 * P:3 * P], float(DH) ** -0.5, None,
                                        ALU.mult).then_inc(evac, 1)

        @block.tensor
        def _(pe):
            pe.wait_ge(laid, 1)
            for c in range(SCOLS):
                if c >= 2:
                    pe.wait_ge(evac, c - 1)
                for n, rows in enumerate((rel_g, srcf_g, ew_g)):
                    nc.tensor.transpose(tp[c % 2][:, n * P:(n + 1) * P], rows[:, c, :], g.ident[:]).then_inc(turned, 1)


def variances(nc, link, st, tmp, var_ready):
    me, ve, mo, vo = st[:, :, 1], st[:, :, 2], st[:, :, 4], st[:, :, 5]
    s, d, v = tmp[:, 0, :], tmp[:, 1, :], tmp[:, 2, :]
    link(nc.vector.tensor_tensor(s, me, mo, ALU.add))
    link(nc.vector.tensor_tensor(d, me, mo, ALU.subtract))
    link(nc.vector.tensor_tensor(v, ve, vo, ALU.add))
    link(nc.vector.tensor_scalar(v, v, 1.0 / D, EPS, ALU.mult, ALU.add))
    link(nc.vector.tensor_tensor(d, d, d, ALU.mult))
    nc.vector.scalar_tensor_tensor(v, d, 0.25, v, ALU.mult, ALU.add).then_inc(var_ready, 1)


def scales(nc, link, tmp, mv, mv_ready):
    link(nc.vector.reciprocal(mv[:, 0, :], tmp[:, 2, :]))
    nc.vector.scalar_tensor_tensor(mv[:, 1, :], tmp[:, 0, :], -0.5, mv[:, 0, :],
                                   ALU.mult, ALU.mult).then_inc(mv_ready, 1)


def node_phase(nc, g, a):
    HALF = WINDOWS // 2
    with ExitStack() as ctx:
        t = Tools(nc, ctx)
        xs, st = g.xs, g.st
        tmp = t.sb("tmp", [P, 3, WINDOWS])
        wqkv = t.sb("wqkv", [P, KC, 3 * D])
        bqkv, be = t.sb("bqkv", [P, 3 * D]), t.sb("be", [P, DH])
        g1, b1 = t.sb("g1", [P, KC]), t.sb("b1", [P, KC])
        xn = t.sb("xn", [P, 2, D])
        xT = t.sb("xT", [P, 2, KC, P])
        kv = t.sb("kv", [P, 2, 2 * D])
        q32 = t.sb("q32", [P, 2, D])
        rest = t.sb("rest", [P, 2, D])
        tp = [t.ps(f"tp_a{u}", [P, 512]) for u in range(2)]
        qk_ps = [t.ps(f"qk_ps{u}", [P, 512]) for u in range(2)]
        v_ps = [t.ps(f"v_ps{u}", [P, 512]) for u in range(2)]
        w_in, chain = t.sem("na_w_in"), t.sem("na_chain")
        var_ready, root_ready, mv_ready = t.sem("na_var"), t.sem("na_root"), t.sem("na_mv")
        stats, normed, xn_ready = t.sem("na_stats"), t.sem("na_normed"), t.sem("na_xn")
        xn_turned, xT_ready, qkv_taken, q_split = t.sem("na_turned"), t.sem("na_xT"), t.sem("na_taken"), t.sem("na_split")
        qkv_ready, q32_ready, zeroed = t.sem("na_qkv"), t.sem("na_q32"), t.sem("na_zeroed")
        hi_ready, rest_ready, mid_ready = t.sem("na_hi"), t.sem("na_rest"), t.sem("na_mid")
        kv_out = [t.sem("na_kv_out0"), t.sem("na_kv_out1")]
        block = ctx.enter_context(nc.Block())
        k_w = a.k_d.rearrange("(w p) d -> w p d", p=P)
        v_w = a.v_d.rearrange("(w p) d -> w p d", p=P)

        @block.sync
        def _(sp):
            with nc.allow_non_contiguous_dma(reason="two short vectors"):
                sp.dma_start(g1[:], a.ln1_g.rearrange("o (c p) -> p (o c)", p=P)).then_inc(w_in, 16)
                sp.dma_start(b1[:], a.ln1_b.rearrange("o (c p) -> p (o c)", p=P)).then_inc(w_in, 16)
            sp.dma_start(wqkv[:], a.wqkv.rearrange("(c p) n -> p c n", p=P)).then_inc(w_in, 16)
            sp.dma_start(bqkv[:], bcast(a.bqkv, [P, 3 * D])).then_inc(w_in, 16)
            sp.dma_start(be[:], bcast(a.be, [P, DH])).then_inc(w_in, 16)
            with sp.Fori(0, HALF) as i:
                for u in range(2):
                    w = i * 2 + u
                    sp.wait_ge(qkv_taken, w + 3)
                    sp.dma_start(k_w[bass.ds(w, 1), :, :].rearrange("o p d -> (o p) d"),
                                 kv[:, u, 0:D]).then_inc(kv_out[u], 16)
                    sp.dma_start(v_w[bass.ds(w, 1), :, :].rearrange("o p d -> (o p) d"),
                                 kv[:, u, D:2 * D]).then_inc(kv_out[u], 16)
            for u in range(2):
                sp.wait_ge(kv_out[u], 32 * HALF + 32)

        @block.gpsimd
        def _(pool):
            for part in g.q:
                nc.gpsimd.memset(part[:, WINDOWS:, :], 0.0).then_inc(zeroed, 1)
            pool.sem_inc(q_split, 2)
            with pool.Fori(0, HALF) as i:
                for u in range(2):
                    w = i * 2 + u
                    hi, mid, lo = (part[:, bass.ds(w, 1), :].rearrange("p o d -> p (o d)") for part in g.q)
                    pool.wait_ge(hi_ready, w + 1)
                    nc.gpsimd.tensor_tensor(rest[:, u, :], q32[:, u, :], hi, ALU.subtract).then_inc(rest_ready, 1)
                    pool.wait_ge(mid_ready, w + 1)
                    nc.gpsimd.tensor_tensor(lo, rest[:, u, :], mid, ALU.subtract).then_inc(q_split, 1)
            pool.wait_ge(zeroed, 3)

        @block.vector
        def _(dve):
            count = [0]

            def link(ins):
                count[0] += 1
                ins.then_inc(chain, 1)
                dve.wait_ge(chain, count[0])

            variances(nc, link, st, tmp, var_ready)
            dve.wait_ge(root_ready, 1)
            scales(nc, link, tmp, g.mv0, mv_ready)
            with dve.Fori(0, HALF) as i:
                for u in range(2):
                    w = i * 2 + u
                    dve.wait_ge(normed, w + 1)
                    nc.vector.bn_stats(st[:, bass.ds(w, 1), :], xs[:, bass.ds(w, 1), :]).then_inc(stats, 1)
            dve.wait_ge(stats, WINDOWS)
            variances(nc, link, st, tmp, var_ready)
            dve.wait_ge(root_ready, 2)
            scales(nc, link, tmp, g.mv1, mv_ready)
            dve.wait_ge(w_in, 80)
            k_bias = bqkv[:, D:2 * D].rearrange("p (h d) -> p h d", d=DH)
            link(nc.vector.tensor_tensor(k_bias, k_bias, bcast(be[:, None, :], [P, HEADS, DH]), ALU.add))
            dve.sem_inc(xT_ready, 2)
            dve.sem_inc(qkv_taken, 2)

            def gain(w, u):
                dve.wait_ge(xn_turned, w + 3)
                dve.wait_ge(qkv_ready, w + 1)
                for c in range(KC):
                    last = nc.vector.tensor_scalar(xT[:, u % 2, c, :], tp[u % 2][:, c * P:(c + 1) * P],
                                                   g1[:, c:c + 1], b1[:, c:c + 1], ALU.mult, ALU.add)
                last.then_inc(xT_ready, 1)

            def trip(i, last_trip):
                for u in range(2):
                    w = i * 2 + u
                    if not (last_trip and u):
                        gain(w + 1, u + 1)
                    dve.wait_ge(qkv_ready, w + 3)
                    dve.wait_ge(q_split, w + 1)
                    nc.vector.tensor_tensor(q32[:, u, :], qk_ps[u][:, 0:D], bqkv[:, 0:D], ALU.add).then_inc(q32_ready, 1)
                    dve.wait_ge(kv_out[u], i * 32 + 32)
                    nc.vector.tensor_tensor(kv[:, u, 0:D], qk_ps[u][:, D:2 * D], bqkv[:, D:2 * D], ALU.add)
                    nc.vector.tensor_tensor(kv[:, u, D:2 * D], v_ps[u][:, 0:D], bqkv[:, 2 * D:3 * D],
                                            ALU.add).then_inc(qkv_taken, 1)

            for u in range(2):
                dve.sem_inc(kv_out[u], 32)
            gain(0, 0)
            with dve.Fori(0, HALF - 1) as i:
                trip(i, False)
            trip(HALF - 1, True)

        @block.scalar
        def _(act):
            act.wait_ge(var_ready, 1)
            nc.scalar.activation(tmp[:, 2, :], tmp[:, 2, :], ACT.Sqrt).then_inc(root_ready, 1)
            act.wait_ge(mv_ready, 1)
            with act.Fori(0, HALF) as i:
                for u in range(2):
                    w = i * 2 + u
                    nc.scalar.activation(xs[:, bass.ds(w, 1), :], xs[:, bass.ds(w, 1), :], ACT.Identity,
                                         bias=g.mv0[:, 1, bass.ds(w, 1)],
                                         scale=g.mv0[:, 0, bass.ds(w, 1)]).then_inc(normed, 1)
            act.wait_ge(var_ready, 2)
            nc.scalar.activation(tmp[:, 2, :], tmp[:, 2, :], ACT.Sqrt).then_inc(root_ready, 1)
            act.wait_ge(mv_ready, 2)

            def norm(w, u):
                act.wait_ge(xn_turned, w + 1)
                nc.scalar.activation(xn[:, u:u + 1, :], xs[:, bass.ds(w, 1), :], ACT.Identity,
                                     bias=g.mv1[:, 1, bass.ds(w, 1)],
                                     scale=g.mv1[:, 0, bass.ds(w, 1)]).then_inc(xn_ready, 1)

            def trip(i, last_trip):
                for u in range(2):
                    w = i * 2 + u
                    if not last_trip:
                        norm(w + 2, u)
                    act.wait_ge(q32_ready, w + 1)
                    nc.scalar.copy(g.q[0][:, bass.ds(w, 1), :], q32[:, u:u + 1, :]).then_inc(hi_ready, 1)
                    act.wait_ge(rest_ready, w + 1)
                    nc.scalar.copy(g.q[1][:, bass.ds(w, 1), :], rest[:, u:u + 1, :]).then_inc(mid_ready, 1)

            for w in range(2):
                norm(w, w)
            with act.Fori(0, HALF - 1) as i:
                trip(i, False)
            trip(HALF - 1, True)

        @block.tensor
        def _(pe):
            def turn(w, u):
                pe.wait_ge(xn_ready, w + 1)
                pe.wait_ge(xT_ready, w + 1)
                for c in range(KC):
                    last = nc.tensor.transpose(tp[u % 2][:, c * P:(c + 1) * P], xn[:, u % 2, c * P:(c + 1) * P], g.ident[:])
                last.then_inc(xn_turned, 1)

            def trip(i, last_trip):
                for u in range(2):
                    w = i * 2 + u
                    if not (last_trip and u):
                        turn(w + 1, u + 1)
                    pe.wait_ge(xT_ready, w + 3)
                    pe.wait_ge(qkv_taken, w + 1)
                    for c in range(KC):
                        nc.tensor.matmul(qk_ps[u][:], xT[:, u, c, :], wqkv[:, c, 0:2 * D], start=(c == 0), stop=(c == KC - 1))
                    for c in range(KC):
                        last = nc.tensor.matmul(v_ps[u][:, 0:D], xT[:, u, c, :], wqkv[:, c, 2 * D:3 * D],
                                                start=(c == 0), stop=(c == KC - 1))
                    last.then_inc(qkv_ready, 1)

            pe.sem_inc(xn_turned, 2)
            pe.sem_inc(qkv_ready, 2)
            pe.wait_ge(w_in, 80)
            turn(0, 0)
            with pe.Fori(0, HALF - 1) as i:
                trip(i, False)
            trip(HALF - 1, True)


UNIT = 4
UNITS = STEPS // UNIT
BODY = 4
TRIPS = UNITS // BODY
LEAD = UNIT


def gather_rows(nc, pool, table, rows, rows_in, staged, stage, carried):
    with pool.Fori(0, TRIPS) as i:
        for p in range(BODY):
            pool.wait_ge(staged, i * BODY + p + 1)
            pool.sem_inc(carried, 1)
            for s in range(UNIT):
                nc.gpsimd.indirect_dma_start(
                    out=rows[:, p, s, 0:D], out_offset=None, in_=table,
                    in_offset=bass.IndirectOffsetOnAxis(ap=stage[:, p, s:s + 1], axis=0)).then_inc(rows_in[p], 16)


def rows_landed(eng, rows_in, i, p):
    eng.wait_ge(rows_in[p], i * (16 * UNIT) + 16 * UNIT)


def values_of(nc, row, engine, first, count, most):
    _, values = nc.values_load_multi_w_load_instructions(
        row[0:1, bass.ds(first, count)], engines=[engine], min_val=0, max_val=most,
        skip_runtime_bounds_check_because="each row is worked out on the chip within these bounds, whatever the data is")
    return values


def score_phase(nc, g, a):
    with ExitStack() as ctx:
        t = Tools(nc, ctx)
        k = t.sb("k_rows", [P, BODY, UNIT, D])
        stage = t.sb("k_stage", [P, BODY, UNIT], i32)
        ef = t.sb("ef", [ED, BODY, UNIT, P])
        we = t.sb("we", [ED, DH])
        onehot = t.sb("onehot", [P, BODY, UNIT, P], bf16)
        onehotT = t.sb("onehotT", [P, 2, UNIT, P], bf16)
        turn_ps = [t.ps(f"turn_ps{u}", [P, 1024], bf16) for u in range(2)]
        ep_ps = [t.ps(f"ep_ps{u}", [P, 512]) for u in range(2)]
        q_ps = [t.ps(f"q_ps{u}", [P, 1024]) for u in range(2)]
        k_in = [t.sem(f"sc_k_in{r}") for r in range(BODY)]
        ef_in = [t.sem(f"sc_ef_in{r}") for r in range(BODY)]
        k_free, ef_free, turned = t.sem("sc_k_free"), t.sem("sc_ef_free"), t.sem("sc_turned")
        ep_used, q_used, turn_copied, onehotT_used = (t.sem("sc_ep_used"), t.sem("sc_q_used"),
                                                      t.sem("sc_copied"), t.sem("sc_oT_used"))
        keys_in = t.sem("sc_keys_in")
        staged, selected, w_in = t.sem("sc_staged"), t.sem("sc_selected"), t.sem("sc_w_in")
        block = ctx.enter_context(nc.Block())
        ef_t = a.ef_t.rearrange("(t d) e -> t d e", d=ED)

        def load_edges(eng, name, n, p, first):
            eng.wait_ge(ef_free, n + 1)
            tiles = values_of(nc, g.tile_row, name, n * UNIT + first, 2, EDGE_TILES - 1)
            for s, tile in enumerate(tiles):
                eng.dma_start(ef[:, p % BODY, first + s, :],
                              ef_t[bass.ds(tile, 1), :, :].rearrange("o d e -> (o d) e")).then_inc(ef_in[p % BODY], 16)

        @block.sync
        def _(sp):
            sp.dma_start(we[:], a.We).then_inc(w_in, 16)
            with sp.Fori(0, TRIPS) as i:
                for p in range(BODY):
                    load_edges(sp, mybir.EngineType.SP, i * BODY + p, p, 0)
            for c in range(CHUNKS):
                sp.dma_start(g.gap[c * HEADS:(c + 1) * HEADS, :],
                             bcast(a.keys_d[0:1, c * CHUNK:c * CHUNK + CHUNK + 1], [HEADS, CHUNK + 1])).then_inc(keys_in, 16)
            sp.wait_ge(keys_in, 16 * CHUNKS)

        @block.gpsimd
        def _(pool):
            gather_rows(nc, pool, a.k_d, k, k_in, staged, stage, g.carried)

        @block.vector
        def _(dve):
            def select(n, slot):
                nc.vector.tensor_tensor(onehot[:, slot % BODY, :, :], bcast(g.iota_row[:, None, :], [P, UNIT, P]),
                                        bcast(g.rel[:, bass.ds(n * UNIT, UNIT)][:, :, None], [P, UNIT, P]),
                                        ALU.is_equal).then_inc(selected, 1)

            dve.sem_inc(k_free, BODY)
            dve.sem_inc(ep_used, 2)
            dve.sem_inc(q_used, 2)

            def add_edges(i, n, slot):
                rows = k[:, slot % BODY, :, :].rearrange("p s (h d) -> p s h d", d=DH)
                ep = ep_ps[slot % 2][:, 0:UNIT * DH].rearrange("p (s d) -> p s d", s=UNIT)[:, :, None, :]
                rows_landed(dve, k_in, i + slot // BODY, slot % BODY)
                dve.wait_ge(ef_free, n + 1 + BODY)
                nc.vector.tensor_tensor(rows, rows, bcast(ep, [P, UNIT, HEADS, DH]), ALU.add).then_inc(ep_used, 1)

            def times_q(n, slot):
                flat = k[:, slot % BODY, :, :].rearrange("p s c -> p (s c)")
                dve.wait_ge(ep_used, n + 3)
                dve.wait_ge(onehotT_used, n + 3)
                nc.vector.tensor_tensor(flat, flat, q_ps[slot % 2][:], ALU.mult).then_inc(q_used, 1)

            def select_ahead(n, slot):
                dve.wait_ge(turned, n + BODY)
                select(n + 3, slot + 3)

            def sum_heads(n, slot):
                dve.wait_ge(q_used, n + 3)
                nc.vector.tensor_reduce(out=g.scores[:, bass.ds(n * UNIT, UNIT), :],
                                        in_=k[:, slot % BODY, :, :].rearrange("p s (h d) -> p s h d", d=DH),
                                        op=ALU.add, axis=AX.X).then_inc(k_free, 1)

            def trip(i, last_trip):
                for p in range(BODY):
                    n = i * BODY + p
                    more = not (last_trip and p == BODY - 1)
                    if more:
                        add_edges(i, n + 1, p + 1)
                    sum_heads(n, p)
                    if more:
                        times_q(n + 1, p + 1)
                        select_ahead(n + 1, p + 1)

            for n in range(3):
                select(n, n)
            add_edges(0, 0, 0)
            times_q(0, 0)
            select_ahead(0, 0)
            with dve.Fori(0, TRIPS - 1) as i:
                trip(i, False)
            trip(TRIPS - 1, True)

        @block.scalar
        def _(act):
            def copy_turned(n, slot):
                act.wait_ge(turned, n + 1 + BODY)
                act.wait_ge(onehotT_used, n + 1)
                nc.scalar.copy(onehotT[:, slot % 2, :, :].rearrange("p s m -> p (s m)"),
                               turn_ps[slot % 2][:, 0:UNIT * P]).then_inc(turn_copied, 1)

            def stage_rows(n, slot):
                act.wait_ge(k_free, n + 1)
                nc.scalar.copy(stage[:, slot % BODY, :], g.src[:, bass.ds(n * UNIT, UNIT)]).then_inc(staged, 1)

            def trip(i, last_trip):
                for p in range(BODY):
                    n = i * BODY + p
                    copy_turned(n + 1, p + 1)
                    if not (last_trip and p >= BODY - 3):
                        stage_rows(n + 3, p + 3)
                        load_edges(act, mybir.EngineType.Activation, n + 3, p + 3, 2)

            act.sem_inc(turn_copied, 2)
            for n in range(3):
                stage_rows(n, n)
                load_edges(act, mybir.EngineType.Activation, n, n, 2)
            copy_turned(0, 0)
            with act.Fori(0, TRIPS - 1) as i:
                trip(i, False)
            trip(TRIPS - 1, True)

        @block.tensor
        def _(pe):
            def turn(n, slot):
                pe.wait_ge(selected, n + 1)
                pe.wait_ge(turn_copied, n + 1)
                for s in range(UNIT):
                    last = nc.tensor.transpose(turn_ps[slot % 2][:, s * P:(s + 1) * P], onehot[:, slot % BODY, s, :], g.ident_b[:])
                last.then_inc(turned, 1)

            def project(i, n, slot):
                pe.wait_ge(ef_in[slot % BODY], (i + slot // BODY) * (16 * UNIT) + 16 * UNIT)
                pe.wait_ge(ep_used, n + 1)
                for s in range(UNIT):
                    last = nc.tensor.matmul(ep_ps[slot % 2][:, s * DH:(s + 1) * DH], ef[:, slot % BODY, s, :], we[:],
                                            start=True, stop=True)
                last.then_inc(ef_free, 1)

            def trip(i, last_trip):
                for p in range(BODY):
                    n = i * BODY + p
                    if p % 2 == 0:
                        wins = values_of(nc, g.win_row, mybir.EngineType.PE, n * UNIT + LEAD, 2 * UNIT, TABLE_WINDOWS - 1)
                    turn(n + 1, p + 1)
                    if not (last_trip and p == BODY - 1):
                        project(i, n + 1, p + 1)
                    pe.wait_ge(turn_copied, n + 3)
                    pe.wait_ge(q_used, n + 1)
                    for s in range(UNIT):
                        win = wins[UNIT * (p % 2) + s]
                        for part in range(3):
                            last = nc.tensor.matmul(q_ps[p % 2][:, s * D:(s + 1) * D], onehotT[:, p % 2, s, :],
                                                    g.q[part][:, bass.ds(win, 1), :].rearrange("p o d -> p (o d)"),
                                                    start=(part == 0), stop=(part == 2))
                    last.then_inc(onehotT_used, 1)

            pe.sem_inc(ef_free, BODY)
            pe.sem_inc(turned, BODY)
            pe.sem_inc(onehotT_used, 2)
            pe.wait_ge(w_in, 16)
            turn(0, 0)
            project(0, 0, 0)
            with pe.Fori(0, TRIPS - 1) as i:
                trip(i, False)
            trip(TRIPS - 1, True)


def softmax_phase(nc, g, a):
    with ExitStack() as ctx:
        t = Tools(nc, ctx)
        sT = t.sb("sT", [P, CHUNK_STEPS, P])
        fwd = g.r1[:, 0:CHUNK]
        bwd = g.r1[:, CHUNK:2 * CHUNK]
        ends = t.sb("ends", [P, 2])
        row = t.sb("row", [1, 2, P])
        enter = t.sb("enter", [1, HEADS, CHUNKS])
        swept = t.sb("swept", [1, HEADS, CHUNKS])
        shifted = t.sb("shifted", [1, P])
        carry = t.sb("carry", [P, 2])
        zeros = t.sb("zeros", [P, 2, D + 1])
        tps = [t.ps(f"mx_ps{u}", [P, 512]) for u in range(2)]
        row_ps = t.ps("row_ps", [P, 512])
        zeroed, slots_cleared = t.sem("mx_zeroed"), t.sem("mx_cleared")
        gap_ready, chain = t.sem("mx_gap"), t.sem("mx_chain")
        weighted, turned, taken = t.sem("mx_weighted"), t.sem("mx_turned"), t.sem("mx_taken")
        ends_ready, row_ready, shift_ready, carry_ready = (t.sem("mx_ends"), t.sem("mx_row"),
                                                           t.sem("mx_shift"), t.sem("mx_carry"))
        max_ready, exp_ready, back, back_taken = t.sem("mx_max"), t.sem("mx_exp"), t.sem("mx_back"), t.sem("mx_back_t")
        block = ctx.enter_context(nc.Block())
        sT_flat = sT[:, :, :].rearrange("p j e -> p (j e)")
        gap = g.gap
        by_chunk = g.scores[:, :, :].rearrange("p (c j) h -> p c j h", j=CHUNK_STEPS)
        in_turn = g.r1[:, 0:CHUNK].rearrange("p (j c h) -> p j c h", c=CHUNKS, h=HEADS)
        BATCHES = CHUNK_STEPS // 4

        @block.gpsimd
        def _(pool):
            nc.gpsimd.memset(zeros[:, :, 0:D], 0.0).then_inc(zeroed, 1)
            for s in range(2):
                nc.gpsimd.iota(zeros[:, s, D:D + 1].bitcast(i32), [[0, 1]], base=(TOKEN_WINDOWS + s) * P,
                               channel_multiplier=1).then_inc(zeroed, 1)

        @block.sync
        def _(sp):
            sp.wait_ge(zeroed, 3)
            for s in range(2):
                sp.dma_start(a.slots_d.rearrange("(n s p) d -> p n s d", s=2, p=P)[:, :, s, :],
                             bcast(zeros[:, s:s + 1, :], [P, PAIRS, D + 1])).then_inc(slots_cleared, 16)
            sp.wait_ge(slots_cleared, 32)

        @block.vector
        def _(dve):
            count = [0]

            def link(ins):
                count[0] += 1
                ins.then_inc(chain, 1)
                dve.wait_ge(chain, count[0])

            ew = g.ew[:, 0:STEPS].rearrange("p (c j) -> p c j", j=CHUNK_STEPS)[:, :, :, None]
            for c in range(CHUNKS):
                nc.vector.tensor_tensor(in_turn[:, :, c, :], by_chunk[:, c, :, :],
                                        bcast(ew[:, c, :, :], [P, CHUNK_STEPS, HEADS]), ALU.mult).then_inc(weighted, 1)
            link(nc.vector.tensor_tensor(bwd[:], gap[:, 1:], gap[:, 0:CHUNK], ALU.not_equal))
            link(nc.vector.tensor_scalar(gap[:, 0:CHUNK], bwd[:], -BIG, None, ALU.mult, ALU.add, accum_out=ends[:, 1:2]))
            for b in range(BATCHES):
                dve.wait_ge(turned, b + 1)
                nc.vector.tensor_copy(sT_flat[:, b * 512:(b + 1) * 512], tps[b % 2][:]).then_inc(taken, 1)
            dve.wait_ge(taken, BATCHES)

            def sweep(turn, gaps, data, out, last, step):
                def way(ap):
                    return ap[:, ::step] if step < 0 else ap
                link(nc.vector.tensor_tensor_scan(way(out), way(gaps), way(data), -BIG, ALU.add, ALU.max))
                nc.vector.tensor_copy(ends[:, 0:1], out[:, last:last + 1]).then_inc(ends_ready, 1)
                dve.wait_ge(row_ready, turn + 1)
                ps = row_ps[0:1, 0:2 * P].rearrange("o (n c h) -> o n h c", n=2, h=HEADS)
                link(nc.vector.tensor_copy(enter[:], ps[:, 0, :, :]))
                link(nc.vector.tensor_copy(swept[:], ps[:, 1, :, :]))
                edge = 0 if step > 0 else CHUNKS - 1
                link(nc.vector.memset(swept[:, :, edge:edge + 1], -BIG))
                e, s = enter[:].rearrange("o h c -> o (h c)"), swept[:].rearrange("o h c -> o (h c)")
                link(nc.vector.tensor_tensor_scan(way(e), way(s), way(e), -BIG, ALU.add, ALU.max))
                link(nc.vector.memset(shifted[:], -BIG))
                sh = shifted[:].rearrange("o (c h) -> o h c", h=HEADS)
                if step > 0:
                    cp = nc.vector.tensor_copy(sh[:, :, 1:], enter[:, :, 0:CHUNKS - 1])
                else:
                    cp = nc.vector.tensor_copy(sh[:, :, 0:CHUNKS - 1], enter[:, :, 1:])
                cp.then_inc(shift_ready, 1)
                dve.wait_ge(carry_ready, turn + 1)
                link(nc.vector.tensor_copy(carry[:, turn:turn + 1], row_ps[:, 256:257]))
                link(nc.vector.tensor_tensor_scan(way(out), way(gaps), way(data), carry[:, turn:turn + 1],
                                                  ALU.add, ALU.max))

            link(nc.vector.memset(gap[:, CHUNK:], -BIG))
            sweep(0, gap[:, 0:CHUNK], sT_flat[:], fwd[:], CHUNK - 1, 1)
            dve.wait_ge(gap_ready, 16)
            link(nc.vector.tensor_tensor(ends[:, 1:2], ends[:, 1:2], gap[:, 0:1], ALU.subtract))
            link(nc.vector.tensor_tensor(ends[:, 1:2], ends[:, 1:2], gap[:, CHUNK:CHUNK + 1], ALU.add))
            sweep(1, gap[:, 1:CHUNK + 1], fwd[:], bwd[:], 0, -1)
            link(nc.vector.tensor_tensor(sT_flat[:], sT_flat[:], bwd[:], ALU.subtract))
            nc.vector.engine_nop().then_inc(max_ready, 1)
            for b in range(BATCHES):
                dve.wait_ge(back, b + 1)
                nc.vector.tensor_copy(by_chunk[:, :, 4 * b:4 * b + 4, :].rearrange("p c j h -> p j c h"),
                                      tps[b % 2][:].rearrange("p (j c h) -> p j c h", j=4, h=HEADS)).then_inc(back_taken, 1)
            dve.wait_ge(back_taken, BATCHES)

        @block.scalar
        def _(act):
            act.wait_ge(ends_ready, 1)
            act.dma_start(gap[0:P - HEADS, CHUNK:CHUNK + 1], gap[HEADS:P, 0:1]).then_inc(gap_ready, 16)
            for b in range(BATCHES):
                if b == 0:
                    act.wait_ge(max_ready, 1)
                nc.scalar.activation(sT_flat[:, b * 512:(b + 1) * 512], sT_flat[:, b * 512:(b + 1) * 512],
                                     ACT.Exp).then_inc(exp_ready, 1)

        @block.tensor
        def _(pe):
            pe.wait_ge(weighted, CHUNKS)
            for b in range(BATCHES):
                if b >= 2:
                    pe.wait_ge(taken, b - 1)
                for j in range(4):
                    last = nc.tensor.transpose(tps[b % 2][:, j * P:(j + 1) * P], in_turn[:, 4 * b + j, :, :].rearrange("p c h -> p (c h)"), g.ident[:])
                last.then_inc(turned, 1)
            for turn in range(2):
                pe.wait_ge(ends_ready, turn + 1)
                for n in range(2):
                    last = nc.tensor.matmul(row_ps[0:1, n * P:(n + 1) * P], ends[:, n:n + 1], g.ident[:], start=True, stop=True)
                last.then_inc(row_ready, 1)
                pe.wait_ge(shift_ready, turn + 1)
                nc.tensor.matmul(row_ps[:, 256:257], shifted[0:1, :], g.ones[0:1, 0:1], start=True, stop=True).then_inc(carry_ready, 1)
            for b in range(BATCHES):
                pe.wait_ge(exp_ready, b + 1)
                if b >= 2:
                    pe.wait_ge(back_taken, b - 1)
                for j in range(4):
                    last = nc.tensor.transpose(tps[b % 2][:, j * P:(j + 1) * P], sT[:, 4 * b + j, :], g.ident[:])
                last.then_inc(back, 1)


def gather_phase(nc, g, a):
    with ExitStack() as ctx:
        t = Tools(nc, ctx)
        v = t.sb("v_rows", [P, BODY, UNIT, ACC])
        stage = t.sb("v_stage", [P, BODY, UNIT], i32)
        onehot = t.sb("onehot_v", [P, 2, UNIT, P])
        sum_ps = [[t.ps(f"sum_ps{u}{s}", [P, 512]) for s in range(UNIT)] for u in range(2)]
        v_in = [t.sem(f"ag_v_in{r}") for r in range(BODY)]
        staged, selected, weighted = t.sem("ag_staged"), t.sem("ag_selected"), t.sem("ag_weighted")
        zeroed, exp_in = t.sem("ag_zeroed"), t.sem("ag_exp_in")
        PARTS = UNIT - 1
        HALF_UNIT = UNIT // 2
        summed, added, part_added = t.sem("ag_summed"), t.sem("ag_added"), t.sem("ag_part")
        block = ctx.enter_context(nc.Block())

        @block.gpsimd
        def _(pool):
            gather_rows(nc, pool, a.v_d, v, v_in, staged, stage, g.carried)

        @block.scalar
        def _(act):
            with act.Fori(0, TRIPS) as i:
                for p in range(BODY):
                    n = i * BODY + p
                    act.wait_ge(summed, n + 2)
                    nc.scalar.copy(stage[:, p, :], g.src[:, bass.ds(n * UNIT, UNIT)]).then_inc(staged, 1)
                    nc.scalar.copy(v[:, p, :, D:ACC], g.scores[:, bass.ds(n * UNIT, UNIT), :]).then_inc(exp_in, 1)

        @block.vector
        def _(dve):
            def select(n, slot):
                nc.vector.tensor_tensor(onehot[:, slot % 2, :, :], bcast(g.iota_row[:, None, :], [P, UNIT, P]),
                                        bcast(g.rel[:, bass.ds(n * UNIT, UNIT)][:, :, None], [P, UNIT, P]),
                                        ALU.is_equal).then_inc(selected, 1)

            def weigh(n, p, half):
                steps = slice(half * HALF_UNIT, (half + 1) * HALF_UNIT)
                rows = v[:, p, steps, 0:D].rearrange("p s (h d) -> p s h d", d=DH)
                ex = g.scores[:, bass.ds(n * UNIT + half * HALF_UNIT, HALF_UNIT), :][:, :, :, None]
                nc.vector.tensor_tensor(rows, rows, bcast(ex, [P, HALF_UNIT, HEADS, DH]), ALU.mult).then_inc(weighted, 1)

            def add(n, slot, s, win):
                into = g.acc[:, bass.ds(win, 1), :].rearrange("p o c -> p (o c)")
                if s:
                    dve.wait_ge(part_added, n * PARTS + 4 * PARTS + s)
                else:
                    dve.wait_ge(added, n + 2)
                return nc.vector.tensor_tensor(into, into, sum_ps[slot % 2][s][:, 0:ACC],
                                               ALU.add).then_inc(added if s == PARTS else part_added, 1)

            nc.vector.memset(g.acc[:], 0.0).then_inc(zeroed, 1)
            for s in range(UNIT):
                nc.vector.memset(sum_ps[1][s][:, 0:ACC], 0.0).then_inc(zeroed, 1)
            dve.sem_inc(added, 1)
            dve.sem_inc(selected, 2)
            dve.sem_inc(part_added, 3 * PARTS)
            dve.wait_ge(zeroed, 1 + UNIT)
            select(0, 0)
            with dve.Fori(0, TRIPS) as i:
                for p in range(BODY):
                    n = i * BODY + p
                    rows_landed(dve, v_in, i, p)
                    weigh(n, p, 0)
                    if p % 2 == 0:
                        wins = values_of(nc, g.win_row, mybir.EngineType.DVE, n * UNIT, 2 * UNIT, TABLE_WINDOWS - 1)
                    win = wins[UNIT * (p % 2):UNIT * (p % 2) + UNIT]
                    dve.wait_ge(summed, n + 1 + BODY)
                    add(n - 1, p - 1, 0, win[0])
                    weigh(n, p, 1)
                    add(n - 1, p - 1, 1, win[1])
                    select(n + 1, p + 1)
                    add(n - 1, p - 1, 2, win[2])
                    add(n - 1, p - 1, 3, win[3])
            dve.wait_ge(summed, UNITS + 1 + BODY)
            for s in range(UNIT):
                win = dve.value_load(g.win_row[0:1, UNITS * UNIT + s:UNITS * UNIT + s + 1], min_val=0, max_val=TABLE_WINDOWS - 1)
                add(UNITS - 1, UNITS - 1, s, win)
            dve.wait_ge(added, UNITS + 2)

        @block.tensor
        def _(pe):
            pe.sem_inc(summed, 1 + BODY)
            with pe.Fori(0, TRIPS) as i:
                for p in range(BODY):
                    n = i * BODY + p
                    pe.wait_ge(selected, n + 3)
                    pe.wait_ge(exp_in, n + 1)
                    pe.wait_ge(added, n + 1)
                    for s in range(UNIT):
                        if s % HALF_UNIT == 0:
                            pe.wait_ge(weighted, n * 2 + s // HALF_UNIT + 1)
                        last = nc.tensor.matmul(sum_ps[p % 2][s][:, 0:ACC], onehot[:, p % 2, s, :], v[:, p, s, :],
                                                start=True, stop=True)
                    last.then_inc(summed, 1)


def attention_out_phase(nc, g, a):
    PAIRS_W = WINDOWS // 2
    with ExitStack() as ctx:
        t = Tools(nc, ctx)
        xs = t.sb("xs_o", [P, 2, 2, D])
        h0 = t.sb("h0", [P, 2, 2, D])
        rs = t.sb("rs", [P, WINDOWS, HEADS])
        attn = t.sb("attn", [P, 2, 2, D])
        attnT = t.sb("attnT", [P, 2, 2, D])
        wo, bo, alpha = t.sb("wo", [P, KC, D]), t.sb("bo", [1, 1, D]), t.sb("alpha", [P, 1])
        st, tmp = t.sb("st_o", [P, WINDOWS, 6]), t.sb("tmp_o", [P, 3, WINDOWS])
        tp = [t.ps(f"tp_o{u}", [P, 512]) for u in range(2)]
        ps = [t.ps(f"ps_o{u}", [P, 512]) for u in range(2)]
        w_in, x_in = t.sem("ao_w_in"), [t.sem("ao_x_in0"), t.sem("ao_x_in1")]
        chain, attn_ready, turned, attnT_ready = t.sem("ao_chain"), t.sem("ao_attn"), t.sem("ao_turned"), t.sem("ao_attnT")
        h0_ready, proj_ready, x1_ready, stats = t.sem("ao_h0"), t.sem("ao_proj"), t.sem("ao_x1"), t.sem("ao_stats")
        ffn_in = t.sem("ao_ffn_in")
        var_ready, root_ready, mv_ready = t.sem("ao_var"), t.sem("ao_root"), t.sem("ao_mv")
        block = ctx.enter_context(nc.Block())
        x_w = a.x.rearrange("(w p) d -> p w d", p=P)

        def pairs(eng, step, tail):
            trips = (PAIRS_W - tail) // 2
            with eng.Fori(0, trips) as i:
                for u in range(2):
                    step(i * 2 + u, u, i, True)
            for n in range(trips * 2, PAIRS_W):
                step(n, n % 2, n // 2, n + tail < PAIRS_W)

        @block.sync
        def _(sp):
            def load(n, u, i, more):
                sp.wait_ge(h0_ready, n + 1)
                sp.dma_start(xs[:, u, :, :], x_w[:, bass.ds(n * 2, 2), :]).then_inc(x_in[u], 16)

            sp.dma_start(wo[:], a.Wo.rearrange("(c p) n -> p c n", p=P)).then_inc(w_in, 16)
            sp.dma_start(bo[:, 0, :], a.bo).then_inc(w_in, 16)
            sp.dma_start(alpha[:], bcast(a.alpha, [P, 1])).then_inc(w_in, 16)
            sp.sem_inc(h0_ready, 2)
            w1, w2, b1, b2, beta, gain, bias = g.ffn_weights
            sp.dma_start(w1[:], a.W1.rearrange("(c p) n -> p c n", p=P)).then_inc(ffn_in, 16)
            sp.dma_start(w2[:], a.W2.rearrange("(c p) n -> p c n", p=P)).then_inc(ffn_in, 16)
            with nc.allow_non_contiguous_dma(reason="short vectors"):
                for into, vector in ((b1, a.b1), (gain, a.ln2_g), (bias, a.ln2_b)):
                    sp.dma_start(into[:], vector.rearrange("o (c p) -> p (o c)", p=P)).then_inc(ffn_in, 16)
            sp.dma_start(b2[:], bcast(a.b2, [P, D])).then_inc(ffn_in, 16)
            sp.dma_start(beta[:], bcast(a.beta, [P, 1])).then_inc(ffn_in, 16)
            pairs(sp, load, 0)
            sp.wait_ge(ffn_in, 112)

        @block.vector
        def _(dve):
            count = [0]

            def link(ins):
                count[0] += 1
                ins.then_inc(chain, 1)
                dve.wait_ge(chain, count[0])

            def divide(n, u):
                heads = [P, 2, HEADS, DH]
                o = g.acc[:, bass.ds(n * 2, 2), 0:D].rearrange("p s (h d) -> p s h d", d=DH)
                nc.vector.tensor_tensor(attn[:, u, :, :].rearrange("p s (h d) -> p s h d", d=DH), o,
                                        bcast(rs[:, bass.ds(n * 2, 2), :][:, :, :, None], heads),
                                        ALU.mult).then_inc(attn_ready, 1)

            def finish(n, u, i, more):
                if more:
                    dve.wait_ge(turned, n + 1)
                    divide(n + 2, u)
                dve.wait_ge(proj_ready, n + 1)
                dve.wait_ge(h0_ready, n + 3)
                nc.vector.scalar_tensor_tensor(g.acc[:, bass.ds(n * 2, 2), 0:D], ps[u][:].rearrange("p (s d) -> p s d", s=2),
                                               alpha[:], h0[:, u, :, :], ALU.mult, ALU.add).then_inc(x1_ready, 1)
                dve.wait_ge(x1_ready, n + 3)
                for s in range(2):
                    nc.vector.bn_stats(st[:, bass.ds(n * 2 + s, 1), :], g.acc[:, bass.ds(n * 2 + s, 1), 0:D]).then_inc(stats, 1)

            dve.sem_inc(x1_ready, 2)
            dve.wait_ge(w_in, 48)
            link(nc.vector.tensor_scalar(rs[:], g.acc[:, 0:WINDOWS, D:ACC], TINY, None, ALU.max))
            link(nc.vector.reciprocal(rs[:], rs[:]))
            for n in range(2):
                divide(n, n)
            pairs(dve, finish, 2)
            dve.wait_ge(stats, WINDOWS)
            variances(nc, link, st, tmp, var_ready)
            dve.wait_ge(root_ready, 1)
            scales(nc, link, tmp, g.mv1, mv_ready)
            dve.wait_ge(mv_ready, 1)

        @block.scalar
        def _(act):
            def take_turned(n, u):
                act.wait_ge(turned, n + 1)
                nc.scalar.copy(attnT[:, u, :, :].rearrange("p s d -> p (s d)"), tp[u][:]).then_inc(attnT_ready, 1)

            def normed_x(n, u, i, more):
                if more:
                    take_turned(n + 1, 1 - u)
                act.wait_ge(x_in[u], i * 16 + 16)
                act.wait_ge(x1_ready, n + 1)
                for s in range(2):
                    w = n * 2 + s
                    last = nc.scalar.activation(h0[:, u, s, :], xs[:, u, s, :], ACT.Identity, bias=g.mv0[:, 1, bass.ds(w, 1)],
                                                scale=g.mv0[:, 0, bass.ds(w, 1)])
                last.then_inc(h0_ready, 1)

            take_turned(0, 0)
            pairs(act, normed_x, 1)
            act.wait_ge(var_ready, 1)
            nc.scalar.activation(tmp[:, 2, :], tmp[:, 2, :], ACT.Sqrt).then_inc(root_ready, 1)

        @block.tensor
        def _(pe):
            def turn(n, u):
                pe.wait_ge(attn_ready, n + 1)
                for s in range(2):
                    for c in range(KC):
                        cols = slice(c * P, (c + 1) * P)
                        last = nc.tensor.transpose(tp[u][:, s * D + c * P:s * D + (c + 1) * P], attn[:, u, s, cols], g.ident[:])
                last.then_inc(turned, 1)

            def project(n, u, i, more):
                if more:
                    turn(n + 1, 1 - u)
                pe.wait_ge(attnT_ready, n + 1)
                pe.wait_ge(x1_ready, n + 1)
                for s in range(2):
                    nc.tensor.matmul(ps[u][:, s * D:(s + 1) * D], g.ones[:], bo[:, 0, :], start=True, stop=False)
                    for c in range(KC):
                        last = nc.tensor.matmul(ps[u][:, s * D:(s + 1) * D], attnT[:, u, s, c * P:(c + 1) * P], wo[:, c, :],
                                                start=False, stop=(c == KC - 1))
                last.then_inc(proj_ready, 1)

            pe.wait_ge(w_in, 48)
            turn(0, 0)
            pairs(pe, project, 1)


def ffn_weights(t):
    FC = FF // P
    return (t.sb("w1_f", [P, KC, FF]), t.sb("w2_f", [P, FC, D]), t.sb("b1_f", [P, FC]), t.sb("b2_f", [P, D]),
            t.sb("beta", [P, 1]), t.sb("gain_f", [P, KC]), t.sb("bias_f", [P, KC]))


def ffn_phase(nc, g, a):
    HALF = WINDOWS // 2
    FC = FF // P
    HR = 4
    with ExitStack() as ctx:
        t = Tools(nc, ctx)
        w1, w2, b1, b2, beta, g2, bb2 = g.ffn_weights
        xs = t.sb("xs_f", [P, 2, D])
        xn = t.sb("xn_f", [P, 2, D])
        xT = t.sb("xT_f", [P, KC, 2 * P])
        hT = t.sb("hT", [P, FC, 2 * P])
        part = t.sb("part", [P, 2, D])
        st, tmp = t.sb("st_f", [P, WINDOWS, 6]), t.sb("tmp_f", [P, 3, WINDOWS])
        tp = t.ps("tp_f", [P, 512])
        h_ps = [t.ps(f"h_ps{u}", [P, 512]) for u in range(HR)]
        y_ps = [t.ps(f"y_ps{u}", [P, 512]) for u in range(2)]
        x_in = t.sem("ff_x_in")
        chain, xn_ready, turned, xT_ready = t.sem("ff_chain"), t.sem("ff_xn"), t.sem("ff_turned"), t.sem("ff_xT")
        h_ready, h_act, y_ready = t.sem("ff_h"), t.sem("ff_h_act"), t.sem("ff_y")
        part_ready, x2_ready, y_done, stats = t.sem("ff_part"), t.sem("ff_x2"), t.sem("ff_ydone"), t.sem("ff_stats")
        var_ready, root_ready, mv_ready = t.sem("ff_var"), t.sem("ff_root"), t.sem("ff_mv")
        block = ctx.enter_context(nc.Block())
        x_w = a.x.rearrange("(w p) d -> p w d", p=P)

        @block.sync
        def _(sp):
            sp.sem_inc(y_done, 1)
            with sp.Fori(0, HALF) as i:
                sp.wait_ge(y_done, i + 1)
                sp.dma_start(xs[:], x_w[:, bass.ds(i * 2, 2), :]).then_inc(x_in, 16)

        @block.vector
        def _(dve):
            count = [0]

            def link(ins):
                count[0] += 1
                ins.then_inc(chain, 1)
                dve.wait_ge(chain, count[0])

            def norm(n):
                for s in range(2):
                    w = n * 2 + s
                    last = nc.vector.tensor_scalar(xn[:, s:s + 1, :], g.acc[:, bass.ds(w, 1), 0:D],
                                                   g.mv1[:, 0, bass.ds(w, 1)], g.mv1[:, 1, bass.ds(w, 1)], ALU.mult, ALU.add)
                last.then_inc(xn_ready, 1)

            def gain(n):
                dve.wait_ge(turned, n + 1)
                for c in range(KC):
                    last = nc.vector.tensor_scalar(xT[:, c, :], tp[:, c * 2 * P:(c + 1) * 2 * P],
                                                   g2[:, c:c + 1], bb2[:, c:c + 1], ALU.mult, ALU.add)
                last.then_inc(xT_ready, 1)

            def trip(i, last_trip):
                if not last_trip:
                    dve.wait_ge(turned, i + 1)
                    norm(i + 1)
                    gain(i + 1)
                for s in range(2):
                    dve.wait_ge(y_ready, i * 2 + s + 3)
                    nc.vector.tensor_tensor(part[:, s, :], y_ps[s][:, 0:D], b2[:], ALU.add).then_inc(part_ready, 1)
                dve.wait_ge(part_ready, i * 2 + 4)
                x1 = g.acc[:, bass.ds(i * 2, 2), 0:D]
                nc.vector.scalar_tensor_tensor(x1, part[:], beta[:], x1, ALU.mult, ALU.add).then_inc(x2_ready, 1)
                dve.wait_ge(x2_ready, i + 1)
                dve.wait_ge(x_in, i * 16 + 16)
                nc.vector.tensor_tensor(x1, x1, xs[:], ALU.add).then_inc(y_done, 1)
                dve.wait_ge(y_done, i + 2)
                for s in range(2):
                    nc.vector.bn_stats(st[:, bass.ds(i * 2 + s, 1), :], g.acc[:, bass.ds(i * 2 + s, 1), 0:D]).then_inc(stats, 1)

            dve.sem_inc(part_ready, 2)
            norm(0)
            gain(0)
            with dve.Fori(0, HALF - 1) as i:
                trip(i, False)
            trip(HALF - 1, True)
            dve.wait_ge(stats, WINDOWS)
            variances(nc, link, st, tmp, var_ready)
            dve.wait_ge(root_ready, 1)
            scales(nc, link, tmp, g.mv2, mv_ready)
            dve.wait_ge(mv_ready, 1)

        @block.scalar
        def _(act):
            act.sem_inc(h_act, HR)
            with act.Fori(0, HALF) as i:
                act.wait_ge(y_ready, i * 2 + 2)
                for f in range(FC):
                    act.wait_ge(h_ready, i * FC + f + 1)
                    nc.scalar.activation(hT[:, f, :], h_ps[f % HR][:, 0:2 * P], ACT.Gelu,
                                         bias=b1[:, f:f + 1]).then_inc(h_act, 1)
            act.wait_ge(var_ready, 1)
            nc.scalar.activation(tmp[:, 2, :], tmp[:, 2, :], ACT.Sqrt).then_inc(root_ready, 1)

        @block.tensor
        def _(pe):
            def turn(n):
                pe.wait_ge(xn_ready, n + 1)
                for c in range(KC):
                    for s in range(2):
                        last = nc.tensor.transpose(tp[:, (2 * c + s) * P:(2 * c + s + 1) * P],
                                                   xn[:, s, c * P:(c + 1) * P], g.ident[:])
                last.then_inc(turned, 1)

            def trip(i, last_trip):
                pe.wait_ge(xT_ready, i + 1)
                for f in range(FC):
                    pe.wait_ge(h_act, i * FC + f + 1)
                    for c in range(KC):
                        last = nc.tensor.matmul(h_ps[f % HR][:, 0:2 * P], w1[:, c, f * P:(f + 1) * P], xT[:, c, :],
                                                start=(c == 0), stop=(c == KC - 1))
                    last.then_inc(h_ready, 1)
                if not last_trip:
                    turn(i + 1)
                pe.wait_ge(part_ready, i * 2 + 2)
                for s in range(2):
                    for f in range(FC):
                        if s == 0 and f % HR == 0:
                            pe.wait_ge(h_act, i * FC + f + 2 * HR)
                        last = nc.tensor.matmul(y_ps[s][:, 0:D], hT[:, f, s * P:(s + 1) * P], w2[:, f, :],
                                                start=(f == 0), stop=(f == FC - 1))
                    last.then_inc(y_ready, 1)

            pe.sem_inc(y_ready, 2)
            turn(0)
            with pe.Fori(0, HALF - 1) as i:
                trip(i, False)
            trip(HALF - 1, True)


def route_phase(nc, g, a):
    W = TOKEN_WINDOWS
    SLOTS_W = 2 * W
    HALF_E = EXPERTS // 2
    RING = 4
    with ExitStack() as ctx:
        t = Tools(nc, ctx)
        wg, bg = t.sb("wg", [P, KC, EXPERTS]), t.sb("bg", [P, EXPERTS])
        xn = t.sb("xn_r", [P, 2, 2, D])
        xT = t.sb("xT_r", [P, 2, KC, 2 * P])
        gs = t.sb("gs", [P, WINDOWS, EXPERTS])
        best, chosen = t.sb("best", [P, W]), t.sb("chosen", [P, W])
        work = t.sb("work", [P, W, EXPERTS])
        hot = t.sb("hot", [P, EXPERTS, W, 2])
        total, rank = t.sb("total", [P, EXPERTS, SLOTS_W]), t.sb("rank", [P, EXPERTS, SLOTS_W])
        ran = t.sb("ran", [P, EXPERTS, SLOTS_W])
        ones = t.sb("ones_r", [P, EXPERTS * SLOTS_W])
        before = t.sb("before", [P, P])
        iota_p = t.sb("iota_p_r", [P, 1])
        ends, starts, pairs, pair_ends = (t.sb(name, [P, EXPERTS]) for name in ("ends_r", "starts_r", "pairs_r", "pair_ends"))
        pairs_i = t.sb("pairs_i", [P, EXPERTS], i32)
        of_pair = t.sb("of_pair", [1, PAIRS])
        place = t.sb("place_f", [P, SLOTS_W])
        rows = t.sb("rows_r", [P, RING, D + 1])
        tokens = t.sb("tokens", [P, W], i32)
        stage = t.sb("stage_r", [P, RING, 2], i32)
        tp = [t.ps(f"tp_r{u}", [P, 512]) for u in range(2)]
        gate_ps = [t.ps(f"gate_ps{u}", [P, 512]) for u in range(2)]
        count_ps = [t.ps(f"count_ps{n}", [P, 512]) for n in range(4)]
        w_in, weights_in, y_out = t.sem("rt_w_in"), t.sem("rt_weights_in"), t.sem("rt_y_out")
        xn_ready, turned, xT_ready = t.sem("rt_xn"), t.sem("rt_turned"), t.sem("rt_xT")
        gate_ready, gs_ready = t.sem("rt_gate"), t.sem("rt_gs")
        consts, chain, hot_ready, counted = t.sem("rt_consts"), t.sem("rt_chain"), t.sem("rt_hot"), t.sem("rt_counted")
        placed, row_ready = t.sem("rt_placed"), t.sem("rt_row")
        sent = [t.sem(f"rt_sent{r}") for r in range(RING)]
        block = ctx.enter_context(nc.Block())

        @block.sync
        def _(sp):
            sp.dma_start(wg[:], a.Wg.rearrange("(c p) n -> p c n", p=P)).then_inc(w_in, 16)
            sp.dma_start(bg[:], bcast(a.bg, [P, EXPERTS])).then_inc(w_in, 16)
            sp.dma_start(g.w1[:].rearrange("p e (c n) -> p (e c) n", c=KC),
                         a.E1.rearrange("e (c p) n -> p (e c) n", p=P)).then_inc(weights_in, 16)
            sp.dma_start(g.w2[:].rearrange("p e c n -> p (e c) n"),
                         a.E2.rearrange("e (c p) n -> p (e c) n", p=P)).then_inc(weights_in, 16)
            with nc.allow_non_contiguous_dma(reason="short vectors"):
                sp.dma_start(g.b1[:], a.eb1.rearrange("e (c p) -> p e c", p=P)).then_inc(weights_in, 16)
            sp.dma_start(g.b2[:].rearrange("p e d -> p (e d)"), bcast(a.eb2, [P, EXPERTS * D])).then_inc(weights_in, 16)
            sp.dma_start(a.out.rearrange("(w p) d -> p w d", p=P), g.acc[:, 0:OUT_WINDOWS, 0:D]).then_inc(y_out, 16)
            sp.wait_ge(weights_in, 64)
            sp.wait_ge(y_out, 16)

        @block.gpsimd
        def _(pool):
            nc.gpsimd.iota(iota_p[:], [[0, 1]], base=0, channel_multiplier=1,
                           allow_small_or_imprecise_dtypes=True).then_inc(consts, 1)
            nc.gpsimd.memset(ones[:], 1.0).then_inc(consts, 1)
            nc.gpsimd.iota(tokens[:], [[P, W]], base=0, channel_multiplier=1).then_inc(consts, 1)
            pool.wait_ge(placed, 1)

            def send(w, r):
                pool.wait_ge(row_ready, w + 1)
                pool.sem_inc(g.carried, 1)
                for k in range(2):
                    nc.gpsimd.indirect_dma_start(
                        out=a.slots_d, out_offset=bass.IndirectOffsetOnAxis(ap=stage[:, r, k:k + 1], axis=0),
                        in_=rows[:, r, :], in_offset=None).then_inc(sent[r], 16)

            with pool.Fori(0, W // RING) as i:
                for r in range(RING):
                    send(i * RING + r, r)
            for w in range(W // RING * RING, W):
                send(w, w % RING)
            for r in range(RING):
                pool.wait_ge(sent[r], 32 * len(range(r, W, RING)))

        @block.scalar
        def _(act):
            def norm_pair(n, u):
                act.wait_ge(turned, n + 1)
                for s in range(2):
                    w = n * 2 + s
                    last = nc.scalar.activation(xn[:, u, s:s + 1, :], g.acc[:, bass.ds(w, 1), 0:D], ACT.Identity,
                                                bias=g.mv2[:, 1, bass.ds(w, 1)], scale=g.mv2[:, 0, bass.ds(w, 1)])
                last.then_inc(xn_ready, 1)

            act.sem_inc(turned, 2)
            with act.Fori(0, WINDOWS // 4) as i:
                for u in range(2):
                    norm_pair(i * 2 + u, u)
            norm_pair(WINDOWS // 2 - 1, 0)
            act.wait_ge(placed, 1)

            def norm_row(w, r):
                nc.scalar.activation(rows[:, r:r + 1, 0:D], g.acc[:, bass.ds(w, 1), 0:D], ACT.Identity,
                                     bias=g.mv2[:, 1, bass.ds(w, 1)], scale=g.mv2[:, 0, bass.ds(w, 1)])
                nc.scalar.copy(rows[:, r, D:D + 1].bitcast(i32), tokens[:, bass.ds(w, 1)])
                nc.scalar.copy(stage[:, r, :], g.place[:, bass.ds(w * 2, 2)]).then_inc(row_ready, 1)

            for r in range(RING):
                norm_row(r, r)
            with act.Fori(0, W // RING - 1) as i:
                for r in range(RING):
                    act.wait_ge(sent[r], i * 32 + 32)
                    norm_row(i * RING + r + RING, r)
            for w in range(W // RING * RING, W):
                act.wait_ge(sent[w % RING], w // RING * 32)
                norm_row(w, w % RING)

        @block.vector
        def _(dve):
            count = [0]

            def link(ins):
                count[0] += 1
                ins.then_inc(chain, 1)
                dve.wait_ge(chain, count[0])

            def take_xT(n, u):
                dve.wait_ge(turned, n + 3)
                dve.wait_ge(gate_ready, n + 1)
                nc.vector.tensor_copy(xT[:, u, :, :].rearrange("p c n -> p (c n)"), tp[u][:]).then_inc(xT_ready, 1)

            def take_gates(n, u):
                dve.wait_ge(gate_ready, n + 3)
                nc.vector.tensor_copy(gs[:, bass.ds(n * 2, 2), :],
                                      gate_ps[u][:, 0:2 * EXPERTS].rearrange("p (s e) -> p s e", s=2)).then_inc(gs_ready, 1)

            dve.sem_inc(xT_ready, 2)
            dve.sem_inc(gs_ready, 2)
            take_xT(0, 0)
            with dve.Fori(0, WINDOWS // 4) as i:
                for u in range(2):
                    take_xT(i * 2 + u + 1, 1 - u)
                    take_gates(i * 2 + u, u)
            take_gates(WINDOWS // 2 - 1, 0)
            dve.wait_ge(gs_ready, WINDOWS // 2 + 2)
            dve.wait_ge(w_in, 32)
            dve.wait_ge(consts, 3)
            link(nc.vector.tensor_scalar(before[:], g.iota_row[:], iota_p[:], None, ALU.is_gt))
            scores = gs[:, 0:W, :]
            by_expert = [P, W, EXPERTS]
            experts = bcast(g.iota_row[:, None, 0:EXPERTS], by_expert)
            link(nc.vector.tensor_tensor(scores, scores, bcast(bg[:, None, :], by_expert), ALU.add))
            for k in range(2):
                link(nc.vector.tensor_reduce(out=best[:], in_=scores, op=ALU.max, axis=AX.X))
                link(nc.vector.tensor_tensor(work[:], scores, bcast(best[:, :, None], by_expert), ALU.is_equal))
                link(nc.vector.scalar_tensor_tensor(work[:], work[:], -float(EXPERTS), experts, ALU.mult, ALU.add))
                link(nc.vector.tensor_reduce(out=chosen[:], in_=work[:], op=ALU.min, axis=AX.X))
                link(nc.vector.scalar_tensor_tensor(work[:], experts, -float(EXPERTS), bcast(chosen[:, :, None], by_expert),
                                                    ALU.add, ALU.is_equal))
                link(nc.vector.tensor_copy(hot[:, :, :, k].rearrange("p e w -> p w e"), work[:]))
                if k == 0:
                    link(nc.vector.scalar_tensor_tensor(scores, work[:], -BIG, scores, ALU.mult, ALU.add))
            nc.vector.engine_nop().then_inc(hot_ready, 1)
            for h in range(2):
                for n, into in enumerate((total, rank)):
                    dve.wait_ge(counted, 2 * h + n + 1)
                    link(nc.vector.tensor_copy(into[:, h * HALF_E:(h + 1) * HALF_E, :].rearrange("p e s -> p (e s)"),
                                               count_ps[2 * h + n][:, 0:HALF_E * SLOTS_W]))
            flat = [ap[:].rearrange("p e s -> p (e s)") for ap in (ran, total, rank)]
            link(nc.vector.tensor_tensor_scan(flat[0], ones[:], flat[1], 0.0, ALU.mult, ALU.add))
            link(nc.vector.tensor_copy(ends[:], ran[:, :, SLOTS_W - 1]))
            link(nc.vector.tensor_tensor(flat[0], flat[0], flat[1], ALU.subtract))
            link(nc.vector.tensor_tensor(flat[0], flat[0], flat[2], ALU.add))
            link(nc.vector.memset(starts[:, 0:1], 0.0))
            link(nc.vector.tensor_copy(starts[:, 1:], ends[:, 0:EXPERTS - 1]))
            link(nc.vector.tensor_tensor(pairs[:], ends[:], starts[:], ALU.subtract))
            link(nc.vector.tensor_scalar(pairs[:], pairs[:], float(2 * P - 1), None, ALU.add))
            link(nc.vector.tensor_copy(pairs_i[:], pairs[:]))
            link(nc.vector.tensor_scalar(pairs_i[:], pairs_i[:], 8, None, ALU.arith_shift_right))
            link(nc.vector.tensor_copy(pairs[:], pairs_i[:]))
            link(nc.vector.tensor_tensor_scan(pair_ends[:], ones[:, 0:EXPERTS], pairs[:], 0.0, ALU.mult, ALU.add))
            link(nc.vector.tensor_tensor(pairs[:], pair_ends[:], pairs[:], ALU.subtract))
            link(nc.vector.scalar_tensor_tensor(starts[:], pairs[:], float(2 * P), starts[:], ALU.mult, ALU.subtract))
            link(nc.vector.tensor_tensor(ran[:], ran[:], bcast(starts[:, :, None], [P, EXPERTS, SLOTS_W]), ALU.add))
            link(nc.vector.tensor_tensor(ran[:], ran[:], hot[:].rearrange("p e w k -> p e (w k)"), ALU.mult))
            link(nc.vector.tensor_reduce(out=place[:], in_=ran[:].rearrange("p e s -> p s e"), op=ALU.add, axis=AX.X))
            nc.vector.tensor_copy(g.place[:], place[:]).then_inc(placed, 1)
            link(nc.vector.memset(of_pair[:], 0.0))
            for e in range(EXPERTS):
                link(nc.vector.scalar_tensor_tensor(of_pair[:], g.iota_row[0:1, 0:PAIRS], pair_ends[0:1, e:e + 1],
                                                    of_pair[:], ALU.is_ge, ALU.add))
            link(nc.vector.tensor_scalar(of_pair[:], of_pair[:], float(EXPERTS - 1), None, ALU.min))
            link(nc.vector.tensor_copy(g.expert_row[:], of_pair[:]))

        @block.tensor
        def _(pe):
            def turn(n, u):
                pe.wait_ge(xn_ready, n + 1)
                pe.wait_ge(xT_ready, n + 1)
                for c in range(KC):
                    for s in range(2):
                        last = nc.tensor.transpose(tp[u][:, (2 * c + s) * P:(2 * c + s + 1) * P],
                                                   xn[:, u, s, c * P:(c + 1) * P], g.ident[:])
                last.then_inc(turned, 1)

            def gates(n, u):
                pe.wait_ge(xT_ready, n + 3)
                pe.wait_ge(gs_ready, n + 1)
                for s in range(2):
                    for c in range(KC):
                        last = nc.tensor.matmul(gate_ps[u][:, s * EXPERTS:(s + 1) * EXPERTS], xT[:, u, c, s * P:(s + 1) * P],
                                                wg[:, c, :], start=(c == 0), stop=(c == KC - 1))
                last.then_inc(gate_ready, 1)

            pe.sem_inc(gate_ready, 2)
            pe.wait_ge(w_in, 32)
            turn(0, 0)
            with pe.Fori(0, WINDOWS // 4) as i:
                for u in range(2):
                    turn(i * 2 + u + 1, 1 - u)
                    gates(i * 2 + u, u)
            gates(WINDOWS // 2 - 1, 0)
            pe.wait_ge(hot_ready, 1)
            for h in range(2):
                slots = hot[:, h * HALF_E:(h + 1) * HALF_E, :, :].rearrange("p e w k -> p (e w k)")
                for n, weights in enumerate((ones[:, 0:P], before[:])):
                    nc.tensor.matmul(count_ps[2 * h + n][:, 0:HALF_E * SLOTS_W], weights, slots,
                                     start=True, stop=True).then_inc(counted, 1)


def expert_phase(nc, g, a):
    HC = EH // P
    RING = 4
    LAST = PAIRS - 1
    with ExitStack() as ctx:
        t = Tools(nc, ctx)
        x = t.sb("x_m", [P, RING, 2, D + 1])
        xT = t.sb("xT_m", [P, 2, KC, 2 * P])
        w1 = t.sb("w1_now", [P, 2, KC * EH])
        hT = t.sb("hT_m", [P, 2, HC, 2 * P])
        res = t.sb("res_m", [P, 2, 2, D])
        tp = [t.ps(f"tp_m{u}", [P, 512]) for u in range(2)]
        h_ps = [t.ps(f"h_ps_m{f}", [P, 512]) for f in range(HC)]
        y_ps = [t.ps(f"y_ps_m{u}", [P, 512]) for u in range(2)]
        x_in = [t.sem(f"mo_x_in{r}") for r in range(RING)]
        turned, fed, h_ready, h_act = t.sem("mo_turned"), t.sem("mo_fed"), t.sem("mo_h"), t.sem("mo_hact")
        y_ready, res_ready, added, left = t.sem("mo_y"), t.sem("mo_res"), t.sem("mo_added"), t.sem("mo_left")
        block = ctx.enter_context(nc.Block())
        slots = a.slots_d.rearrange("(n s p) d -> p n s d", s=2, p=P)

        def expert_of(name, n):
            return values_of(nc, g.expert_row, name, n, 1, EXPERTS - 1)[0]

        @block.sync
        def _(sp):
            def load(n, r):
                sp.wait_ge(left, n + 1)
                sp.dma_start(x[:, r:r + 1, :, :], slots[:, bass.ds(n, 1), :, :]).then_inc(x_in[r], 16)

            sp.sem_inc(left, RING)
            for n in range(RING):
                load(n, n)
            with sp.Fori(0, (PAIRS - RING) // RING) as i:
                for r in range(RING):
                    load(i * RING + r + RING, r)
            for n in range(PAIRS // RING * RING, PAIRS):
                load(n, n % RING)

        @block.gpsimd
        def _(pool):
            def add(n, r):
                pool.wait_ge(res_ready, n + 3)
                pool.sem_inc(g.carried, 1)
                for s in range(2):
                    nc.gpsimd.indirect_dma_start(
                        out=a.out, out_offset=bass.IndirectOffsetOnAxis(ap=x[:, r, s, D:D + 1].bitcast(i32), axis=0),
                        in_=res[:, r % 2, s, :], in_offset=None, compute_op=ALU.add).then_inc(added, 16)
                pool.wait_ge(added, n * 32 + 32)
                pool.sem_inc(left, 1)

            with pool.Fori(0, PAIRS // RING) as i:
                for r in range(RING):
                    add(i * RING + r, r)
            for n in range(PAIRS // RING * RING, PAIRS):
                add(n, n % RING)

        @block.vector
        def _(dve):
            def feed(n, u, expert):
                dve.wait_ge(turned, n + 1)
                dve.wait_ge(h_ready, n * HC + 1)
                nc.vector.tensor_copy(xT[:, u, :, :].rearrange("p c n -> p (c n)"), tp[u][:])
                nc.vector.tensor_copy(w1[:, u:u + 1, :], g.w1[:, bass.ds(expert, 1), :]).then_inc(fed, 1)

            def take(n, u, expert):
                dve.wait_ge(y_ready, n + 3)
                dve.wait_ge(left, n + RING - 1)
                nc.vector.tensor_tensor(res[:, u, :, :], y_ps[u][:].rearrange("p (s d) -> p s d", s=2),
                                        bcast(g.b2[:, bass.ds(expert, 1), :], [P, 2, D]), ALU.add).then_inc(res_ready, 1)

            dve.sem_inc(fed, 2)
            dve.sem_inc(res_ready, 2)
            for n in range(2):
                feed(n, n, expert_of(mybir.EngineType.DVE, n))
            with dve.Fori(0, (PAIRS - 2) // 2) as i:
                for u in range(2):
                    n = i * 2 + u
                    feed(n + 2, u, expert_of(mybir.EngineType.DVE, n + 2))
                    take(n, u, expert_of(mybir.EngineType.DVE, n))
            for n in range((PAIRS - 2) // 2 * 2, PAIRS):
                if n + 2 <= LAST:
                    feed(n + 2, n % 2, expert_of(mybir.EngineType.DVE, n + 2))
                take(n, n % 2, expert_of(mybir.EngineType.DVE, n))

        @block.scalar
        def _(act):
            def hidden(n, u):
                expert = expert_of(mybir.EngineType.Activation, n)
                act.wait_ge(y_ready, n + 1)
                for f in range(HC):
                    act.wait_ge(h_ready, (n + 2) * HC + f + 1)
                    nc.scalar.activation(hT[:, u, f, :], h_ps[f][:, 0:2 * P], ACT.Gelu,
                                         bias=g.b1[:, bass.ds(expert, 1), f]).then_inc(h_act, 1)

            act.sem_inc(h_act, HC)
            with act.Fori(0, PAIRS // 2) as i:
                for u in range(2):
                    hidden(i * 2 + u, u)
            for n in range(PAIRS // 2 * 2, PAIRS):
                hidden(n, n % 2)

        @block.tensor
        def _(pe):
            def turn(n, r, trip):
                pe.wait_ge(x_in[r], trip * 16 + 16)
                pe.wait_ge(fed, n + 1)
                for c in range(KC):
                    for s in range(2):
                        last = nc.tensor.transpose(tp[r % 2][:, (2 * c + s) * P:(2 * c + s + 1) * P],
                                                   x[:, r, s, c * P:(c + 1) * P], g.ident[:])
                last.then_inc(turned, 1)

            def up(n, u):
                pe.wait_ge(fed, n + 3)
                for f in range(HC):
                    pe.wait_ge(h_act, n * HC + f + 1)
                    for c in range(KC):
                        last = nc.tensor.matmul(h_ps[f][:, 0:2 * P], w1[:, u, c * EH + f * P:c * EH + (f + 1) * P], xT[:, u, c, :],
                                                start=(c == 0), stop=(c == KC - 1))
                    last.then_inc(h_ready, 1)

            def down(n, u):
                expert = expert_of(mybir.EngineType.PE, n)
                pe.wait_ge(h_act, n * HC + 2 * HC)
                pe.wait_ge(res_ready, n + 1)
                for s in range(2):
                    for f in range(HC):
                        last = nc.tensor.matmul(y_ps[u][:, s * D:(s + 1) * D], hT[:, u, f, s * P:(s + 1) * P],
                                                g.w2[:, bass.ds(expert, 1), f, :].rearrange("p o d -> p (o d)"),
                                                start=(f == 0), stop=(f == HC - 1))
                last.then_inc(y_ready, 1)

            pe.sem_inc(y_ready, 2)
            pe.sem_inc(h_ready, 2 * HC)
            turn(0, 0, 0)
            up(0, 0)
            turn(1, 1, 0)
            with pe.Fori(0, (PAIRS - 2) // RING) as i:
                for r in range(RING):
                    n = i * RING + r
                    up(n + 1, (r + 1) % 2)
                    turn(n + 2, (r + 2) % RING, i + (r + 2) // RING)
                    down(n, r % 2)
            for n in range((PAIRS - 2) // RING * RING, PAIRS):
                if n + 1 <= LAST:
                    up(n + 1, (n + 1) % 2)
                if n + 2 <= LAST:
                    turn(n + 2, (n + 2) % RING, (n + 2) // RING)
                down(n, n % 2)


def program(nc, a):
    with ExitStack() as ctx:
        t = Tools(nc, ctx)
        g = Places()
        g.carried = t.sem("carried")
        g.ident = t.sb("ident", [P, P])
        g.iota_row = t.sb("iota_row", [P, P])
        g.ones = t.sb("ones", [1, P])
        g.mv0, g.mv1, g.mv2 = (t.sb(f"mv{n}", [P, 2, WINDOWS]) for n in range(3))
        g.r1 = t.sb("r1", [P, TABLE_WINDOWS * ACC])
        g.acc = g.r1[:, :].rearrange("p (w c) -> p w c", c=ACC)
        halves = g.r1[:, :].bitcast(bf16)
        q_size = TABLE_WINDOWS * D
        with ExitStack() as edge_ctx:
            t = Tools(nc, edge_ctx)
            g.rel = t.sb("rel", [P, STEPS_UP])
            g.ew = t.sb("ew", [P, STEPS_UP])
            g.src = t.sb("src", [P, STEPS_UP], i32)
            g.ident_b = t.sb("ident_b", [P, P], bf16)
            g.tile_row = t.sb("tile_row", [1, STEPS_UP], i32)
            g.win_row = t.sb("win_row", [1, STEPS_UP + LEAD], i32)
            g.scores = t.sb("scores", [P, STEPS, HEADS])
            x_or_keys = t.sb("x_or_keys", [P, WINDOWS * D])
            g.xs = x_or_keys[:, :].rearrange("p (w d) -> p w d", d=D)
            g.gap = x_or_keys[:, 0:CHUNK + 1]
            g.st = t.sb("x_stats", [P, WINDOWS, 6])
            setup_phase(nc, g, a)
            with ExitStack() as q_ctx:
                q_lo = Tools(nc, q_ctx).sb("q_lo", [P, TABLE_WINDOWS, D], bf16)
                g.q = [halves[:, n * q_size:(n + 1) * q_size].rearrange("p (w d) -> p w d", d=D) for n in range(2)]
                g.q.append(q_lo)
                node_phase(nc, g, a)
                score_phase(nc, g, a)
            softmax_phase(nc, g, a)
            gather_phase(nc, g, a)
        t = Tools(nc, ctx)
        with ExitStack() as ffn_ctx:
            g.ffn_weights = ffn_weights(Tools(nc, ffn_ctx))
            attention_out_phase(nc, g, a)
            ffn_phase(nc, g, a)
        g.place = t.sb("place", [P, 2 * TOKEN_WINDOWS], i32)
        g.expert_row = t.sb("expert_row", [1, PAIRS], i32)
        g.w1 = t.sb("expert_w1", [P, EXPERTS, KC * EH])
        g.w2 = t.sb("expert_w2", [P, EXPERTS, EH // P, D])
        g.b1, g.b2 = t.sb("expert_b1", [P, EXPERTS, EH // P]), t.sb("expert_b2", [P, EXPERTS, D])
        route_phase(nc, g, a)
        expert_phase(nc, g, a)


class Places:
    pass


def kernel(**inputs):
    import numpy as np
    import concourse.bacc as bacc
    from concourse.bass_utils import run_bass_kernel_spmd

    def get(name):
        return np.ascontiguousarray(inputs[name])

    def padded(rows, n, fill=0):
        out = np.full((n,) + rows.shape[1:], fill, rows.dtype)
        out[:rows.shape[0]] = rows
        return out

    n_edges = EDGE_TILES * P
    dst = padded(get("dst"), n_edges, WINDOWS * P - 1).reshape(EDGE_TILES, P)
    ef = padded(get("edge_attr_64"), n_edges).reshape(EDGE_TILES, P, ED)
    row = lambda name: get("L0_" + name).reshape(1, -1)
    arrays = {
        "x": padded(get("x"), WINDOWS * P),
        "ends_rows": np.concatenate([dst, padded(get("src"), n_edges).reshape(EDGE_TILES, P)], axis=1),
        "last_dst": np.ascontiguousarray(dst[:, P - 1]).reshape(1, -1),
        "ew_rows": padded(get("edge_weight"), n_edges).reshape(EDGE_TILES, P),
        "ef_t": np.ascontiguousarray(ef.transpose(0, 2, 1)).reshape(EDGE_TILES * ED, P),
        "wqkv": np.concatenate([get("L0_gnn_W" + c) for c in "qkv"], axis=1),
        "bqkv": np.concatenate([row("gnn_b" + c) for c in "qkv"], axis=1),
        "We": get("L0_gnn_We"), "be": row("gnn_be"), "Wo": get("L0_gnn_Wo"), "bo": row("gnn_bo"),
        "ln1_g": row("gnn_ln1_g"), "ln1_b": row("gnn_ln1_b"), "ln2_g": row("gnn_ln2_g"), "ln2_b": row("gnn_ln2_b"),
        "W1": get("L0_gnn_W1"), "b1": row("gnn_b1"), "W2": get("L0_gnn_W2"), "b2": row("gnn_b2"),
        "alpha": row("gnn_alpha"), "beta": row("gnn_beta"),
        "Wg": get("L0_ffn_Wg"), "bg": row("ffn_bg"), "E1": get("L0_ffn_W1"), "eb1": get("L0_ffn_b1"),
        "E2": get("L0_ffn_W2"), "eb2": row("ffn_b2"),
    }
    nc = bacc.Bacc("TRN2", target_bir_lowering=False, num_devices=1)
    a = Places()
    for name, array in arrays.items():
        a.__dict__[name] = nc.dram_tensor("in_" + name, array.shape, mybir.dt.from_np(array.dtype), kind="ExternalInput").ap()
    a.out = nc.dram_tensor("out", (OUT_WINDOWS * P, D), fp32, kind="ExternalOutput").ap()
    a.k_d = nc.dram_tensor("k_table", (WINDOWS * P, D), fp32, kind="Internal").ap()
    a.v_d = nc.dram_tensor("v_table", (WINDOWS * P, D), fp32, kind="Internal").ap()
    a.slots_d = nc.dram_tensor("slots_table", (PAIRS * 2 * P, D + 1), fp32, kind="Internal").ap()
    a.steps_d = nc.dram_tensor("steps_scratch", (2, STEPS_UP), i32, kind="Internal").ap()
    a.keys_d = nc.dram_tensor("keys_scratch", (1, 1 + STEPS_UP * P), fp32, kind="Internal").ap()
    program(nc, a)
    result = run_bass_kernel_spmd(nc, [{"in_" + name: array for name, array in arrays.items()}], core_ids=[0])
    return np.ascontiguousarray(result.results[0]["out"][:NODES])
```
